# Optimizing a Trainium2 kernel written in Bass

```python
import numpy as np
import jax
import jax.numpy as jnp

def _softmax(x, axis=-1):
    return jax.nn.softmax(x, axis=axis)

def _gelu(x):
    return jax.nn.gelu(x, approximate=True)

def _silu(x):
    return jax.nn.silu(x)

def _sigmoid(x):
    return jax.nn.sigmoid(x)

def _layernorm(x, axis=-1, eps=1e-05):
    m = jnp.mean(x, axis=axis, keepdims=True)
    v = jnp.var(x, axis=axis, keepdims=True)
    return (x - m) / jnp.sqrt(v + eps)

def _scatter_add(tgt, idx, src, axis=0):
    return tgt.at[idx].add(src)

def _segment_sum(src, seg, n):
    return jax.ops.segment_sum(src, seg, n)
kernel_name = 'mk_conv_attn_hybrid_d2_conv_nchw768_r4_f5f95c'

def setup_inputs(seed: int=0):
    np.random.seed(seed)
    _w = jnp.asarray

    def _rec_inputs():
        import jax
        import jax.numpy as jnp
        _gk = jax.random.key(seed)
        x = -0.0002221 + 1 * jax.random.normal(jax.random.fold_in(_gk, 1), (8, 192, 16, 16), jnp.float32)
        return x
    x = _rec_inputs()

    def _L0_conv_setup():
        import jax, jax.numpy as jnp
        import numpy as np
        K = 7
        PAD = K // 2
        EPS = 1e-12

        def _offsets():
            offs = []
            offs += [(i, i) for i in range(K)]
            offs += [(i, K // 2) for i in range(K)]
            offs += [(i, K - 1 - i) for i in range(K)]
            offs += [(K // 2, i) for i in range(K)]
            return offs
        key = jax.random.key(seed)
        k1, k2, k3 = jax.random.split(key, 3)
        B, C, H, W = (8, 192, 16, 16)
        OUT_C = 192
        feature = jax.random.normal(k1, (B, C, H, W), dtype=jnp.float32)
        conv_w = jax.random.normal(k2, (OUT_C, C + 4 * K), dtype=jnp.float32) * 0.02
        conv_b = jax.random.normal(k3, (OUT_C,), dtype=jnp.float32) * 0.02
        return {'feature': feature, 'conv_w': conv_w, 'conv_b': conv_b}
    _L0_conv_all = _L0_conv_setup()
    _L0_conv_in = {k: v for k, v in _L0_conv_all.items() if k in ('conv_w', 'conv_b')}
    del _L0_conv_all

    def _L1_attn_setup():
        import jax, jax.numpy as jnp
        import numpy as np
        B, S, D = (8, 512, 192)
        key = jax.random.key(seed)
        k1, k2, k3, k4 = jax.random.split(key, 4)
        x = jax.random.normal(k1, (B, S, D), dtype=jnp.float32)
        scale = 1.0 / np.sqrt(D)
        wq = jax.random.normal(k2, (D, D), dtype=jnp.float32) * scale
        wk = jax.random.normal(k3, (D, D), dtype=jnp.float32) * scale
        wv = jax.random.normal(k4, (D, D), dtype=jnp.float32) * scale
        return {'x': x, 'wq': wq, 'wk': wk, 'wv': wv}
    _L1_attn_all = _L1_attn_setup()
    _L1_attn_in = {k: v for k, v in _L1_attn_all.items() if k in ('wq', 'wk', 'wv')}
    del _L1_attn_all

    def _L1_ffn_setup():
        import jax, jax.numpy as jnp
        import numpy as np
        NUM_EXPERT = 8
        TOP_K = 1
        key = jax.random.key(seed)
        ks = jax.random.split(key, 6)
        B, S, D, E, F = (8, 512, 192, 8, 469)
        scale = 0.02
        return {'x': jax.random.normal(ks[0], (B, S, D), dtype=jnp.float32), 'Wg': jax.random.normal(ks[1], (E, D), dtype=jnp.float32) * scale, 'bg': jnp.zeros((E,), dtype=jnp.float32), 'W1': jax.random.normal(ks[2], (E, F, D), dtype=jnp.float32) * scale, 'W2': jax.random.normal(ks[3], (E, F, D), dtype=jnp.float32) * scale, 'W3': jax.random.normal(ks[4], (E, D, F), dtype=jnp.float32) * scale}
    _L1_ffn_all = _L1_ffn_setup()
    _L1_ffn_in = {k: v for k, v in _L1_ffn_all.items() if k in ('Wg', 'bg', 'W1', 'W2', 'W3')}
    del _L1_ffn_all
    return {'x': x, 'L0_conv_conv_w': _L0_conv_in['conv_w'], 'L0_conv_conv_b': _L0_conv_in['conv_b'], 'L1_attn_wq': _L1_attn_in['wq'], 'L1_attn_wk': _L1_attn_in['wk'], 'L1_attn_wv': _L1_attn_in['wv'], 'L1_ffn_Wg': _L1_ffn_in['Wg'], 'L1_ffn_bg': _L1_ffn_in['bg'], 'L1_ffn_W1': _L1_ffn_in['W1'], 'L1_ffn_W2': _L1_ffn_in['W2'], 'L1_ffn_W3': _L1_ffn_in['W3']}

def reference(x, L0_conv_conv_w, L0_conv_conv_b, L1_attn_wq, L1_attn_wk, L1_attn_wv, L1_ffn_Wg, L1_ffn_bg, L1_ffn_W1, L1_ffn_W2, L1_ffn_W3):
    import jax
    import jax.numpy as jnp

    def _L0_conv_ref(feature, conv_w, conv_b):
        import jax, jax.numpy as jnp
        import numpy as np
        K = 7
        PAD = K // 2
        EPS = 1e-12

        def _offsets():
            offs = []
            offs += [(i, i) for i in range(K)]
            offs += [(i, K // 2) for i in range(K)]
            offs += [(i, K - 1 - i) for i in range(K)]
            offs += [(K // 2, i) for i in range(K)]
            return offs
        b, c, h, w = feature.shape
        norm = jnp.sqrt(jnp.sum(feature * feature, axis=1, keepdims=True))
        feat_n = feature / jnp.maximum(norm, EPS)
        feat_pad = jnp.pad(feat_n, ((0, 0), (0, 0), (PAD, PAD), (PAD, PAD)))
        corr = jnp.stack([jnp.sum(feat_pad[:, :, r:h + r, cc:w + cc] * feat_n, axis=1) for r, cc in _offsets()], axis=1)
        x = jnp.concatenate([feature, corr], axis=1)
        out = jnp.einsum('bchw,oc->bohw', x, conv_w) + conv_b[None, :, None, None]
        return out

    def _L1_attn_ref(x, wq, wk, wv):
        import jax, jax.numpy as jnp
        import numpy as np
        B, S, D = (8, 512, 192)
        d_out = wq.shape[1]
        q = jnp.einsum('bsd,de->bse', x, wq)
        k = jnp.einsum('bsd,de->bse', x, wk)
        v = jnp.einsum('bsd,de->bse', x, wv)
        scores = jnp.einsum('bqe,bke->bqk', q, k) / jnp.sqrt(jnp.float32(d_out))
        S_len = x.shape[1]
        causal = jnp.tril(jnp.ones((S_len, S_len), dtype=bool))
        scores = jnp.where(causal[None, :, :], scores, -jnp.inf)
        attn = jax.nn.softmax(scores, axis=-1)
        out = jnp.einsum('bqk,bke->bqe', attn, v)
        return out

    def _L1_ffn_ref(x, Wg, bg, W1, W2, W3):
        import jax, jax.numpy as jnp
        import numpy as np
        NUM_EXPERT = 8
        TOP_K = 1
        B, S, D = x.shape
        E = Wg.shape[0]
        xf = x.reshape(B * S, D)
        gate = xf @ Wg.T + bg
        vals, idx = jax.lax.top_k(gate, TOP_K)
        probs = jax.nn.softmax(vals, axis=-1)
        dispatch = jnp.sum(jax.nn.one_hot(idx, E, dtype=x.dtype) * probs[..., None], axis=1)
        h = jax.nn.silu(jnp.einsum('td,efd->tef', xf, W1)) * jnp.einsum('td,efd->tef', xf, W2)
        out = jnp.einsum('tef,edf,te->td', h, W3, dispatch)
        return out.reshape(B, S, D)

    def _gn(v, G=32, eps=1e-05):
        B_, C_, H_, W_ = v.shape
        g = v.reshape(B_, G, C_ // G, H_, W_)
        m = jnp.mean(g, axis=(2, 3, 4), keepdims=True)
        s = jnp.var(g, axis=(2, 3, 4), keepdims=True)
        return ((g - m) / jnp.sqrt(s + eps)).reshape(v.shape)

    def _ln_c(v, eps=1e-06):
        m = jnp.mean(v, axis=1, keepdims=True)
        s = jnp.var(v, axis=1, keepdims=True)
        return (v - m) / jnp.sqrt(s + eps)

    def _ln_t(v, eps=1e-05):
        m = jnp.mean(v, axis=-1, keepdims=True)
        s = jnp.var(v, axis=-1, keepdims=True)
        return (v - m) / jnp.sqrt(s + eps)

    def _to_tokens(v):
        B_, C_, H_, W_ = v.shape
        return v.reshape(B_, C_, H_ * W_).transpose(0, 2, 1)

    def _from_tokens(t, like):
        B_, C_, H_, W_ = like.shape
        return t.transpose(0, 2, 1).reshape(B_, C_, H_, W_)
    x = x + _L0_conv_ref(_gn(x), L0_conv_conv_w, L0_conv_conv_b)
    t = _to_tokens(x)
    t = t + _L1_attn_ref(_ln_t(t), L1_attn_wq, L1_attn_wk, L1_attn_wv)
    t = t + _L1_ffn_ref(_ln_t(t), L1_ffn_Wg, L1_ffn_bg, L1_ffn_W1, L1_ffn_W2, L1_ffn_W3)
    x = _from_tokens(t, x)
    return x

_drawn_inputs = setup_inputs


def setup_inputs(seed=0):
    import zlib

    import numpy as np

    out = dict(_drawn_inputs(seed))
    spreads = {'L1_ffn_bg': (0.0, 0.71)}
    factors = {'L1_ffn_Wg': 3.782, 'L1_ffn_W1': 3.573, 'L1_ffn_W2': 3.551, 'L1_ffn_W3': 3.545}
    for name, (base, spread) in spreads.items():
        noise = np.random.default_rng([zlib.crc32(name.encode()), seed]).standard_normal(out[name].shape)
        drawn = base * np.exp(spread * noise) if base else spread * noise
        out[name] = jnp.asarray(drawn.astype(out[name].dtype))
    for name, factor in factors.items():
        out[name] = (out[name] * factor).astype(out[name].dtype)
    return out
```

```python
from contextlib import ExitStack

import concourse.bass as bass
from concourse import mybir

F32 = mybir.dt.float32
F32R = mybir.dt.float32r
BF16 = mybir.dt.bfloat16
I32 = mybir.dt.int32
U32 = mybir.dt.uint32
ALU = mybir.AluOpType
ACT = mybir.ActivationFunctionType
AX_X = mybir.AxisListType.X

P = 128
IMAGES = 8
SIDE = 16
PIX = SIDE * SIDE
C = 192
CA, CB = P, C - P
HALVES = PIX // P
TILES = IMAGES * HALVES
GROUPS = 32
KERNEL = 7
REACH = KERNEL // 2
PAD_PIX = REACH * SIDE
WIDE = PIX + 2 * PAD_PIX
PAIR = 2 * SIDE
PAIRS = PIX // PAIR
WINDOWS = IMAGES * PAIRS
CHUNK = 8
CHUNKS = PAIR // CHUNK
BAND_CHUNK = CHUNK * C

EXPERTS = 8
F = 469
FE = F + 1
FT = 4
W12 = 2 * FE
W3C = FT * C
STAGE = 2 * W12 + W3C
WALL = 3 * W12 + 2 * W3C
SLOTS = TILES + EXPERTS - 1
PAD = P
REGION = TILES * P + PAD
EMPTY = EXPERTS * REGION
NO_TOKEN = 1 << 20
ROW = C + 4

EPS_NORM = 1e-12
EPS = 1e-5
NEG = -1e30
SM_SCALE = float(C) ** -0.5
AHEAD = 2

S1 = {}
S2 = {}
_at = 0
for _n, _w in (("cf", 2 * C), ("gm", 4 * CA), ("rows", 4 * C), ("wq", 4 * CA), ("wk", 4 * CA), ("wv", 2 * C), ("shift", 480)):
    S1[_n] = (_at, _at + _w)
    _at += _w
S1N = _at
_at = 0
for _n, _w in (("id", P), ("mask", 3 * P), ("wg", 2 * EXPERTS), ("bg", 2 * EXPERTS), ("desc", 2 * EXPERTS), ("base", EXPERTS), ("slot", SLOTS + 1), ("tri", 2 * P)):
    S2[_n] = (_at, _at + _w)
    _at += _w
S2N = _at
SHIFT0 = 176


def build(nc, x_cm, x_tm, small1, small2, band, w_all, out):
    xs = nc.dram_tensor("token_rows", (EMPTY + P, ROW), F32).ap()
    corr = nc.dram_tensor("corr_rows", (TILES * P, C), F32).ap()

    top = ExitStack()
    with top:
        def sb(name, shape, dt=F32, ctx=top):
            return ctx.enter_context(nc.sbuf_tensor(name, shape, dt))

        def sem(name):
            return top.enter_context(nc.semaphore(name))

        bank = [top.enter_context(nc.psum_tensor(f"bank{i}", [P, 512], F32)) for i in range(8)]

        rows = sb("rows", [P, SLOTS, ROW])
        s2 = sb("small2_sb", [P, S2N])
        stage = sb("stage", [P, 2, STAGE])
        mH = sb("mH", [P, 4 * CA], F32R)
        mL = sb("mL", [P, 2 * CA], F32R)
        vwH = sb("vwH", [P, 2 * C], F32R)
        vwL = sb("vwL", [P, C], F32R)
        tri_sb = sb("tri_sb", [P, 2 * P], BF16)
        eps_c = sb("eps_c", [P, 1])
        run = sb("run", [P, EXPERTS])
        posi = sb("posi", [P, TILES], I32)

        def c2(name):
            return s2[:, S2[name][0]:S2[name][1]]

        ident = c2("id")

        early = ExitStack()
        early.enter_context(nc.sbuf_tensor("early_gap", [P, WALL], F32R))
        bandH = sb("bandH", [P, PAIR * C], F32R, early)
        bandL = sb("bandL", [P, PAIR * C], F32R, early)
        xcm = sb("xcm", [P, IMAGES, 2, PIX], ctx=early)
        s1 = sb("small1_sb", [P, S1N], ctx=early)
        f32t = sb("f32t", [P, 2, 2, PIX], ctx=early)
        fsq = sb("fsq", [P, 2, 2, PIX], ctx=early)
        fH = sb("fH", [P, 2, 2, WIDE], F32R, early)
        fL = sb("fL", [P, 2, 2, WIDE], F32R, early)
        fQ = sb("fQ", [P, 2, WIDE], F32R, early)
        gram = sb("gram", [P, PAIR, WINDOWS], ctx=early)
        gs = sb("gs", [P, 2, CHUNK * WINDOWS], ctx=early)
        gsH = sb("gsH", [P, 2, CHUNK * WINDOWS], F32R, early)
        gsL = sb("gsL", [P, 2, CHUNK * WINDOWS], F32R, early)
        co = sb("co", [WINDOWS, 2, CHUNK, C], ctx=early)
        cfH = sb("cfH", [P, 2 * C], F32R, early)
        cfL = sb("cfL", [P, C], F32R, early)
        bias2 = sb("bias2", [CB, C], F32R, early)
        ones2 = sb("ones2", [CB, P], F32R, early)
        onesc = sb("onesc", [P, 1], ctx=early)
        wsum = sb("wsum", [P, C], ctx=early)
        gst = sb("gst", [P, IMAGES, 2, 6], ctx=early)
        mq = sb("mq", [P, IMAGES, 2, 2, 2], ctx=early)
        msq = sb("msq", [P, IMAGES, 2, 2], ctx=early)
        mv = sb("mv", [P, 2, 2, IMAGES // 2, 2], ctx=early)
        gvar = sb("gvar", [P, 2, 2, IMAGES // 2], ctx=early)
        grs = sb("grs", [P, 2, 2, IMAGES // 2], ctx=early)
        gnb = sb("gnb", [P, 2, 2, IMAGES // 2], ctx=early)
        ssq = sb("ssq", [P, TILES], ctx=early)
        rn = sb("rn", [P, TILES], ctx=early)
        cc = sb("cc", [P, TILES], ctx=early)
        rwin = sb("rwin", [P, IMAGES, PAIRS], ctx=early)
        rT = sb("rT", [TILES, P], ctx=early)
        rbk = sb("rbk", [WINDOWS, PAIR], ctx=early)
        emptyt = sb("emptyt", [P, ROW], ctx=early)
        early.close()

        middle = ExitStack()
        middle.enter_context(nc.sbuf_tensor("middle_gap", [P, (EXPERTS - 1) * WALL], F32R))
        xn = sb("xn", [P, HALVES, 2 * CA], ctx=middle)
        XH = sb("XH", [P, 2, 2, PIX], F32R, middle)
        XL = sb("XL", [P, 2, 2, PIX], F32R, middle)
        UH = sb("UH", [P, 2, 2, PIX], F32R, middle)
        uAl = sb("uAl", [P, 2, PIX], F32R, middle)
        V = sb("V", [P, 2, HALVES, C], ctx=middle)
        sc_sb = sb("scores_sb", [P, 3 * P], ctx=middle)
        Pr = sb("probs", [P, 3 * P], ctx=middle)
        PT = sb("probs_t", [P, 3 * P], ctx=middle)
        xn2 = sb("xn2", [P, HALVES, C], ctx=middle)
        x2T = sb("x2T", [P, 2, PIX], ctx=middle)
        st = sb("st", [P, 2, 6], ctx=middle)
        lnv = sb("lnv", [P, 2, 2], ctx=middle)
        ln1 = sb("ln1", [P, 2, 2, 2], ctx=middle)
        ln2 = sb("ln2", [P, 2, 2, 2], ctx=middle)
        smx = sb("smx", [P, 2], ctx=middle)
        nmx = sb("nmx", [P, 2], ctx=middle)
        ssum = sb("ssum", [P, 2], ctx=middle)
        lg = sb("lg", [P, 2, EXPERTS], ctx=middle)
        gmx = sb("gmx", [P, 2], ctx=middle)
        oh = sb("oh", [P, 2, EXPERTS], BF16, middle)
        pos = sb("pos", [P, 2], ctx=middle)
        middle.close()

        wall = sb("wall", [P, EXPERTS, WALL], F32R)
        xf = sb("xf", [P, 2 * CA])
        FH = sb("FH", [P, 2, 2, P], F32R)
        FL = sb("FL", [P, 2, 2, P], F32R)
        gh = sb("gh", [P, 2, FT * P])
        HH = sb("HH", [P, 2, FT, P], F32R)
        HL = sb("HL", [P, 2, FT, P], F32R)
        yo = sb("yo", [P, 2, C])
        tiles_i = sb("tiles_i", [P, EXPERTS], I32)
        tiles_f = sb("tiles_f", [P, EXPERTS])
        ends = sb("ends", [P, 2, EXPERTS])
        started = sb("started", [P, SLOTS, EXPERTS])
        picked = sb("picked", [P, SLOTS, EXPERTS])
        per_slot = sb("per_slot", [P, 4, SLOTS])
        slot_expert = sb("slot_expert", [P, SLOTS], I32)
        slot_row = sb("slot_row", [P, SLOTS], I32)

        def c1(name):
            return s1[:, S1[name][0]:S1[name][1]]

        small1_in, small2_in, tm_in, rbk_in = sem("small1_in"), sem("small2_in"), sem("tm_in"), sem("rbk_in")
        cm_in = [sem("cm_in0"), sem("cm_in1")]
        stage_in = [sem("stage_in0"), sem("stage_in1")]
        stage_hi, stage_free = sem("stage_hi"), sem("stage_free")
        empty_out = sem("empty_out")
        corr_out = [sem("corr_out0"), sem("corr_out1")]
        corr_added = [sem(f"corr_added{q}") for q in range(4)]
        out_done = sem("out_done")
        dve, act = sem("dve_step"), sem("act_step")
        prep_ready, m_ready, m_split, wsplit_hi, small_split = sem("prep_ready"), sem("m_ready"), sem("m_split"), sem("wsplit_hi"), sem("small_split")
        gstat_in, gstat_ready, gvar_ready, gstd_ready, gnorm_ready = sem("gstat_in"), sem("gstat_ready"), sem("gvar_ready"), sem("gstd_ready"), sem("gnorm_ready")
        f_ready, fh_ready, fl_ready, fq_ready, fsq_ready = sem("f_ready"), sem("fh_ready"), sem("fl_ready"), sem("fq_ready"), sem("fsq_ready")
        conv_ready, conv_taken, gram_ready, gram_taken, ss_ready = sem("conv_ready"), sem("conv_taken"), sem("gram_ready"), sem("gram_taken"), sem("ss_ready")
        ssq_ready, nrm_ready, rn_ready, cc_ready, rwin_ready, rt_ready, rt_copied = sem("ssq_ready"), sem("nrm_ready"), sem("rn_ready"), sem("cc_ready"), sem("rwin_ready"), sem("rt_ready"), sem("rt_copied")
        gs_ready, gsh_ready, gsl_ready, class_ready, co_ready = sem("gs_ready"), sem("gsh_ready"), sem("gsl_ready"), sem("class_ready"), sem("co_ready")
        center_added = sem("center_added")
        iota_done = sem("iota_done")
        empty_ready = sem("empty_ready")
        (stats_ready, xn_ready, xt_ready, xh_ready, xl_ready, u_ready, uh_ready, ul_ready, v_ready, v_copied, s_ready, max_ready,
         exp_ready, pt_ready, pt_copied, o_ready, t2_ready, xn2_ready, t2t_ready, x2_copied, g_ready, oh_ready, pf_ready,
         pos_ready, rs1_ready, rs2_ready, ln_ready, dve2, wall_hi, wall_lo, wall_dve) = (sem(n) for n in (
             "stats_ready", "xn_ready", "xt_ready", "xh_ready", "xl_ready", "u_ready", "uh_ready", "ul_ready", "v_ready", "v_copied",
             "s_ready", "max_ready", "exp_ready", "pt_ready", "pt_copied", "o_ready", "t2_ready", "xn2_ready", "t2t_ready",
             "x2_copied", "g_ready", "oh_ready", "pf_ready", "pos_ready", "rs1_ready", "rs2_ready", "ln_ready", "dve2", "wall_hi", "wall_lo", "wall_dve"))
        factors_ready, held, wall_q = sem("factors_ready"), sem("held"), sem("wall_q")
        scattered, table_ready = sem("scattered"), sem("table_ready")
        slot_in = [sem("slot_in0"), sem("slot_in1")]
        out_sent = [sem("out_sent0"), sem("out_sent1")]
        (fx_ready, fxt_ready, fh2_ready, fl2_ready, h_ready, silu_ready, gh_ready, gt_ready, hh_ready, hl_ready, y_ready,
         y_taken, yo_free, dve3) = (sem(n) for n in ("fx_ready", "fxt_ready", "fh2_ready", "fl2_ready", "h_ready", "silu_ready", "gh_ready",
                                            "gt_ready", "hh_ready", "hl_ready", "y_ready", "y_taken", "yo_free", "dve3"))

        block = top.enter_context(nc.Block())

        @block.sync
        def _(sp):
            sp.dma_start(s1[:], small1).then_inc(small1_in, 16)
            n2 = IMAGES // 2
            for h in range(2):
                sp.dma_start(xcm[:, n2 * h:n2 * (h + 1)].rearrange("p b t x -> p b (t x)"),
                             x_cm[n2 * h:n2 * (h + 1)].rearrange("b p x -> p b x")).then_inc(cm_in[h], 16)
            sp.dma_start(rows[:, 0:TILES, 0:C], x_tm).then_inc(tm_in, 16)
            sp.dma_start(s2[:], small2).then_inc(small2_in, 16)
            for n in range(CHUNKS):
                if n >= 2:
                    sp.wait_ge(stage_free, n - 1)
                sp.dma_start(stage[:, n % 2, 0:BAND_CHUNK], band[:, BAND_CHUNK * n:BAND_CHUNK * (n + 1)]).then_inc(stage_in[n % 2], 16)
            sp.wait_ge(empty_ready, 1)
            for e in range(EXPERTS + 1):
                sp.dma_start(xs[REGION * e:REGION * e + P, :], emptyt[:]).then_inc(empty_out, 16)
            sp.wait_ge(rt_copied, 1)
            for k in range(P // PAIR):
                sp.dma_start(rbk[k:WINDOWS:P // PAIR, :], rT[:, PAIR * k:PAIR * (k + 1)]).then_inc(rbk_in, 16)
            for c in range(CHUNKS):
                sp.wait_ge(co_ready, c + 1)
                sp.dma_start(corr.rearrange("(w p) c -> w p c", p=PAIR)[:, CHUNK * c:CHUNK * (c + 1), :], co[:, c % 2]).then_inc(corr_out[c % 2], 16)
            for e in range(EXPERTS):
                n = CHUNKS + e
                if e < 2:
                    sp.wait_ge(stage_free, n - 1)
                else:
                    sp.wait_ge(wall_lo, e - 1)
                    sp.wait_ge(wall_q, e - 1)
                sp.dma_start(stage[:, n % 2], w_all[e]).then_inc(stage_in[n % 2], 16)
            sp.wait_ge(scattered, 16 * TILES)
            sp.wait_ge(empty_out, 16 * (EXPERTS + 1))
            sp.wait_ge(table_ready, 1)

            def load_slot(j, par, k):
                if k is not None:
                    sp.wait_ge(slot_in[par], 16 * k)
                sp.wait_ge(table_ready, 1)
                off = sp.value_load(slot_row[0:1, bass.ds(j, 1)], min_val=0, max_val=EMPTY)
                sp.dma_start(rows[:, bass.ds(j, 1), :].rearrange("p a c -> p (a c)"), xs[bass.ds(off, P), :]).then_inc(slot_in[par], 16)

            for j in range(2):
                load_slot(j, j, None)
            with sp.Fori(1, SLOTS // 2) as i:
                for par in range(2):
                    load_slot(2 * i + par, par, i)
            load_slot(SLOTS - 1, (SLOTS - 1) % 2, (SLOTS - 1) // 2)
            for par in range(2):
                sp.wait_ge(out_sent[par], 16 * ((SLOTS + 1 - par) // 2))

        @block.gpsimd
        def _(pool):
            nc.gpsimd.memset(emptyt[:], 0.0).then_inc(iota_done, 1)
            pool.wait_ge(iota_done, 1)
            nc.gpsimd.iota(emptyt[:, C + 2:C + 3].bitcast(I32), pattern=[[0, 1]], base=NO_TOKEN, channel_multiplier=0).then_inc(empty_ready, 1)
            nc.gpsimd.iota(rows[:, 0:TILES, C + 2].bitcast(I32), pattern=[[P, TILES]], base=0, channel_multiplier=1).then_inc(iota_done, 1)
            nc.gpsimd.memset(rows[:, 0:TILES, C + 3], 0.0).then_inc(iota_done, 1)
            pool.sem_inc(fsq_ready, AHEAD)
            with pool.Fori(0, IMAGES // 2) as i:
                for par in range(2):
                    pool.wait_ge(ss_ready, 2 * i + (par - 1 + AHEAD))
                    pool.wait_ge(f_ready, 2 * i + (par + 1 + AHEAD))
                    nc.gpsimd.tensor_tensor(fsq[:, par], f32t[:, par], f32t[:, par], ALU.mult).then_inc(fsq_ready, 1)
                pool.wait_ge(stage_hi, i + 1)
                pool.wait_ge(tm_in, 16)
                at = bass.ds(i * BAND_CHUNK, BAND_CHUNK)
                nc.gpsimd.tensor_tensor(bandL[:, at], stage[:, bass.ds(i % 2, 1), 0:BAND_CHUNK].rearrange("p a b -> p (a b)"),
                                        bandH[:, at].bitcast(F32), ALU.subtract).then_inc(stage_free, 1)
            for s in corr_out:
                pool.wait_ge(s, 16 * (CHUNKS // 2))
            pool.wait_ge(center_added, 1)
            tok = corr.rearrange("(j p) c -> p j c", p=P)
            for q in range(4):
                n4 = TILES // 4
                pool.dma_start(rows[:, n4 * q:n4 * (q + 1), 0:C], tok[:, n4 * q:n4 * (q + 1), :], accum_op=ALU.add).then_inc(corr_added[q], 16)

            for s in corr_added:
                pool.wait_ge(s, 16)
            pool.wait_ge(empty_out, 16 * (EXPERTS + 1))
            pool.sem_inc(xn_ready, AHEAD)
            pool.sem_inc(xn2_ready, AHEAD)

            def norm_attn(b, par):
                pool.wait_ge(xt_ready, b + AHEAD)
                pool.wait_ge(rs1_ready, b + 1 + AHEAD)
                pool.wait_ge(tm_in, 16)
                for h in range(HALVES):
                    src = rows[:, 2 * b + h, 0:C]
                    mean, rs = ln1[:, par, h, 0:1], ln1[:, par, h, 1:2]
                    nc.gpsimd.tensor_scalar(xn[:, h, 0:C], src, mean, rs, ALU.subtract, ALU.mult)
                    ins = nc.gpsimd.tensor_scalar(xn[:, h, C:2 * CA], src[:, CA:C], mean, rs, ALU.subtract, ALU.mult)
                ins.then_inc(xn_ready, 1)

            def norm_gate(b):
                pool.wait_ge(t2t_ready, b + AHEAD)
                pool.wait_ge(rs2_ready, b + 1 + AHEAD)
                pool.wait_ge(tm_in, 16)
                par = b % 2
                for h in range(HALVES):
                    ins = nc.gpsimd.tensor_scalar(xn2[:, h], rows[:, 2 * b + h, 0:C], ln2[:, par, h, 0:1], ln2[:, par, h, 1:2], ALU.subtract, ALU.mult)
                ins.then_inc(xn2_ready, 1)
                nc.gpsimd.tensor_copy(rows[:, 2 * b:2 * b + 2, C:C + 2], ln2[:, par]).then_inc(factors_ready, 1)

            def scatter_tokens(b):
                pool.wait_ge(pos_ready, b + 1 + AHEAD)
                pool.wait_ge(factors_ready, b + 1)
                for h in range(HALVES):
                    j = 2 * b + h
                    pool.indirect_dma_start(out=xs, out_offset=bass.IndirectOffsetOnAxis(ap=posi[:, j:j + 1].bitcast(U32), axis=0),
                                            in_=rows[:, j], in_offset=None,
                                            bounds_check=EMPTY - 1, oob_is_err=False).then_inc(scattered, 16)

            def weights_lo(e, par):
                pool.wait_ge(wall_hi, e + 1)
                pool.wait_ge(tm_in, 16)
                w = wall[:, e]
                nc.gpsimd.tensor_tensor(w[:, W12:2 * W12], stage[:, par, 0:W12], w[:, 0:W12].bitcast(F32), ALU.subtract)
                w3 = w[:, 3 * W12:WALL].rearrange("p (k s c) -> p k s c", s=2, c=C)
                nc.gpsimd.tensor_tensor(w3[:, :, 1], stage[:, par, 2 * W12:STAGE].rearrange("p (k c) -> p k c", c=C),
                                        w3[:, :, 0].bitcast(F32), ALU.subtract).then_inc(wall_lo, 1)

            def step(t, par, mid, back, nxt, weights):
                if weights:
                    weights_lo(t - 1, 1 - par)
                if nxt:
                    norm_attn(t + 1, 1 - par)
                if mid:
                    norm_gate(t - 1)
                if back:
                    scatter_tokens(t - 2)

            norm_attn(0, 0)
            step(0, 0, False, False, True, False)
            step(1, 1, True, False, True, True)
            for t in range(2, IMAGES - 1):
                step(t, t % 2, True, True, True, True)
            step(IMAGES - 1, 1, True, True, False, True)
            step(IMAGES, 0, True, True, False, False)
            step(IMAGES + 1, 1, False, True, False, False)
            pool.sem_inc(fx_ready, AHEAD)
            pool.sem_inc(yo_free, AHEAD)

            def norm_ffn(j, par, loaded):
                pool.wait_ge(slot_in[par], 16 * loaded)
                pool.wait_ge(fxt_ready, j + AHEAD)
                pool.wait_ge(tm_in, 16)
                row = rows[:, j]
                mean, rs = row[:, C:C + 1], row[:, C + 1:C + 2]
                nc.gpsimd.tensor_scalar(xf[:, 0:C], row[:, 0:C], mean, rs, ALU.subtract, ALU.mult)
                nc.gpsimd.tensor_scalar(xf[:, C:2 * CA], row[:, CA:C], mean, rs, ALU.subtract, ALU.mult).then_inc(fx_ready, 1)

            def send_slot(j, par):
                if j:
                    pool.wait_ge(out_sent[1 - par], 16 * ((j + 1) // 2))
                    pool.sem_inc(yo_free, 1)
                pool.wait_ge(y_taken, j + 1 + AHEAD)
                pool.wait_ge(tm_in, 16)
                pool.indirect_dma_start(out=out, out_offset=bass.IndirectOffsetOnAxis(ap=rows[:, j, C + 2:C + 3].bitcast(U32), axis=0),
                                        in_=yo[:, par], in_offset=None, bounds_check=TILES * P - 1, oob_is_err=False).then_inc(out_sent[par], 16)

            for j in range(SLOTS + 3):
                if j < SLOTS:
                    norm_ffn(j, j % 2, j // 2 + 1)
                if j >= 3:
                    send_slot(j - 3, (j - 3) % 2)

        @block.scalar
        def _(sc):
            sc.wait_ge(m_ready, 1)
            nc.scalar.activation(mH[:], bank[4][:], ACT.Copy).then_inc(m_split, 1)
            sc.wait_ge(small1_in, 16)
            nc.scalar.activation(cfH[:], c1("cf"), ACT.Copy).then_inc(wsplit_hi, 1)
            nc.scalar.activation(vwH[:], c1("wv"), ACT.Copy).then_inc(wsplit_hi, 1)
            sc.wait_ge(prep_ready, 1)
            for h in range(2):
                sc.wait_ge(gvar_ready, h + 1)
                nc.scalar.activation(grs[:, h], gvar[:, h], ACT.Sqrt, bias=eps_c[:, 0:1]).then_inc(gstd_ready, 1)
            sc.sem_inc(f_ready, AHEAD)
            sc.sem_inc(gram_taken, AHEAD)

            def norm_image(b, par):
                half, at = (b // (IMAGES // 2), b % (IMAGES // 2))
                for t in range(2):
                    ins = nc.scalar.activation(f32t[:, par, t], xcm[:, bass.ds(b, 1), t, :].rearrange("p a x -> p (a x)"),
                                               ACT.Identity, scale=grs[:, bass.ds(half, 1), t, bass.ds(at, 1)].rearrange("p a b -> p (a b)"),
                                               bias=gnb[:, bass.ds(half, 1), t, bass.ds(at, 1)].rearrange("p a b -> p (a b)"))
                ins.then_inc(f_ready, 1)

            def take_gram(b, par):
                sc.wait_ge(gram_ready, b + 1 + AHEAD)
                sc.wait_ge(small1_in, 16)
                dst = gram[:, :, bass.ds(b * PAIRS, PAIRS)].rearrange("q c k -> q k c")
                nc.scalar.activation(dst, bank[2 + par][:, 0:PIX].rearrange("q (k c) -> q k c", c=PAIR), ACT.Copy).then_inc(gram_taken, 1)

            sc.wait_ge(gnorm_ready, 2)
            for b in range(2):
                norm_image(b, b)

            def band_hi(n, par):
                nc.scalar.activation(bandH[:, bass.ds(n * BAND_CHUNK, BAND_CHUNK)], stage[:, par, 0:BAND_CHUNK], ACT.Copy).then_inc(stage_hi, 1)

            for i in range(IMAGES // 2 - 1):
                for par in range(2):
                    sc.wait_ge(fl_ready, 2 * i + par + 1 + AHEAD)
                    sc.wait_ge(fsq_ready, 2 * i + par + 1 + AHEAD)
                    norm_image(2 * i + 2 + par, par)
                    take_gram(2 * i + par, par)
                sc.wait_ge(stage_in[i % 2], 16 * (i // 2 + 1))
                band_hi(i, i % 2)
            i = CHUNKS - 1
            sc.wait_ge(stage_in[i % 2], 16 * (i // 2 + 1))
            band_hi(i, i % 2)
            for b in (IMAGES - 2, IMAGES - 1):
                take_gram(b, b % 2)
            sc.wait_ge(ssq_ready, 1)
            nc.scalar.activation(rn[:], ssq[:], ACT.Sqrt).then_inc(nrm_ready, 1)
            for c in range(CHUNKS):
                sc.wait_ge(gs_ready, c + 1)
                if c >= 2:
                    sc.wait_ge(class_ready, c - 1)
                nc.scalar.activation(gsH[:, c % 2], gs[:, c % 2], ACT.Copy).then_inc(gsh_ready, 1)

            for s in corr_added:
                sc.wait_ge(s, 16)
            sc.wait_ge(empty_out, 16 * (EXPERTS + 1))
            for s in (rs1_ready, rs2_ready, xh_ready, exp_ready, x2_copied, uh_ready, pt_copied, v_copied):
                sc.sem_inc(s, AHEAD)

            def weights_hi(e, par, loaded):
                sc.wait_ge(stage_in[par], 16 * loaded)
                sc.wait_ge(small1_in, 16)
                w = wall[:, bass.ds(e, 1), :].rearrange("p a c -> p (a c)")
                nc.scalar.activation(w[:, 0:W12], stage[:, par, 0:W12], ACT.Copy)
                nc.scalar.activation(w[:, 2 * W12:3 * W12], stage[:, par, W12:2 * W12], ACT.Copy)
                w3 = w[:, 3 * W12:WALL].rearrange("p (k s c) -> p k s c", s=2, c=C)
                nc.scalar.activation(w3[:, :, 0], stage[:, par, 2 * W12:STAGE].rearrange("p (k c) -> p k c", c=C), ACT.Copy).then_inc(wall_hi, 1)

            def rsqrt(src, to, which, count):
                nc.scalar.activation(lnv[:, which], src, ACT.Ln, bias=eps_c[:, 0:1]).then_inc(ln_ready, 1)
                sc.wait_ge(ln_ready, count)
                sc.wait_ge(small1_in, 16)
                return nc.scalar.activation(to, lnv[:, which], ACT.Exp, scale=-0.5)

            def step(t, par, front, mid, back, nxt, loaded):
                if front:
                    sc.wait_ge(xt_ready, t + 1 + AHEAD)
                    nc.scalar.activation(XH[:, par].rearrange("p t x -> p (t x)"), bank[0][:], ACT.Copy).then_inc(xh_ready, 1)
                if mid:
                    sc.wait_ge(max_ready, t + AHEAD)
                    nc.scalar.activation(Pr[:, 0:P], sc_sb[:, 0:P], ACT.Exp, scale=SM_SCALE, bias=nmx[:, 0:1], accum_out=ssum[:, 0:1])
                    nc.scalar.activation(Pr[:, P:3 * P], sc_sb[:, P:3 * P], ACT.Exp, scale=SM_SCALE, bias=nmx[:, 1:2],
                                         accum_out=ssum[:, 1:2]).then_inc(exp_ready, 1)
                if back:
                    sc.wait_ge(t2t_ready, t - 1 + AHEAD)
                    nc.scalar.activation(x2T[:].rearrange("p t x -> p (t x)"), bank[6][:], ACT.Copy).then_inc(x2_copied, 1)
                if front:
                    sc.wait_ge(u_ready, t + 1 + AHEAD)
                    nc.scalar.activation(UH[:, par].rearrange("p t x -> p (t x)"), bank[1][:], ACT.Copy).then_inc(uh_ready, 1)
                if mid:
                    sc.wait_ge(pt_ready, t + AHEAD)
                    nc.scalar.activation(PT[:], bank[4][:, 0:3 * P], ACT.Copy).then_inc(pt_copied, 1)
                if front:
                    sc.wait_ge(v_ready, t + 1 + AHEAD)
                    nc.scalar.activation(V[:, par].rearrange("p h c -> p (h c)"), bank[2][:, 0:HALVES * C], ACT.Copy).then_inc(v_copied, 1)
                if nxt:
                    sc.wait_ge(stats_ready, t + 2 + AHEAD)
                    sc.wait_ge(rs1_ready, t + 1 + AHEAD)
                    rsqrt(ln1[:, 1 - par, :, 1], ln1[:, 1 - par, :, 1], 0, 2 * t + 3).then_inc(rs1_ready, 1)
                if loaded is not None:
                    weights_hi(t - 1, 1 - par, loaded)
                if mid:
                    sc.wait_ge(t2_ready, t + AHEAD)
                    sc.wait_ge(rs2_ready, t - 1 + AHEAD)
                    rsqrt(ln2[:, 1 - par, :, 1], ln2[:, 1 - par, :, 1], 1, 2 * t + 4).then_inc(rs2_ready, 1)

            step(-1, 1, False, False, False, True, None)
            sc.sem_inc(ln_ready, 1)
            step(0, 0, True, False, False, True, None)
            sc.sem_inc(ln_ready, 1)
            step(1, 1, True, True, False, True, 3)
            with sc.Fori(1, IMAGES // 2 - 1) as i:
                for par in range(2):
                    step(2 * i + par, par, True, True, True, True, i + 2 + par)
            step(IMAGES - 2, 0, True, True, True, True, IMAGES // 2 + 1)
            sc.sem_inc(ln_ready, 1)
            step(IMAGES - 1, 1, True, True, True, False, IMAGES // 2 + 2)
            sc.sem_inc(ln_ready, 1)
            step(IMAGES, 0, False, True, True, False, None)
            step(IMAGES + 1, 1, False, False, True, False, None)
            sc.wait_ge(pos_ready, IMAGES + AHEAD)
            weights_hi(EXPERTS - 1, (CHUNKS + EXPERTS - 1) % 2, (CHUNKS + EXPERTS) // 2)
            for s in (hh_ready, silu_ready, fh2_ready):
                sc.sem_inc(s, AHEAD)

            def ffn_step(j, par, back, mid, nxt):
                if back:
                    sc.wait_ge(gt_ready, j + AHEAD)
                    nc.scalar.activation(HH[:, 1 - par].rearrange("p k x -> p (k x)"), bank[5][:], ACT.Copy).then_inc(hh_ready, 1)
                if mid:
                    sc.wait_ge(h_ready, j + 1 + AHEAD)
                    nc.scalar.activation(gh[:, par, 0:FE], bank[1 + 2 * par][:, 0:FE], ACT.Silu).then_inc(silu_ready, 1)
                if nxt:
                    sc.wait_ge(fxt_ready, j + 2 + AHEAD)
                    nc.scalar.activation(FH[:, 1 - par].rearrange("p t x -> p (t x)"), bank[0][:, 0:2 * P], ACT.Copy).then_inc(fh2_ready, 1)

            ffn_step(-1, 1, False, False, True)
            ffn_step(0, 0, False, True, True)
            ffn_step(1, 1, True, True, True)
            with sc.Fori(1, SLOTS // 2) as i:
                for par in range(2):
                    ffn_step(2 * i + par, par, True, True, True)
            ffn_step(SLOTS - 1, 0, True, True, False)
            ffn_step(SLOTS, 1, True, False, False)

        @block.vector
        def _(ve):
            steps = [0]

            def link(ins):
                steps[0] += 1
                ins.then_inc(dve, 1)
                ve.wait_ge(dve, steps[0])

            nc.vector.memset(fH[:].rearrange("p a b w -> p (a b w)").bitcast(F32), 0.0)
            nc.vector.memset(fL[:].rearrange("p a b w -> p (a b w)").bitcast(F32), 0.0)
            nc.vector.memset(fQ[:].rearrange("p a w -> p (a w)").bitcast(F32), 0.0)
            nc.vector.memset(ones2[:].bitcast(F32), 1.0)
            nc.vector.memset(onesc[:], 1.0)
            nc.vector.memset(eps_c[:], EPS).then_inc(prep_ready, 1)
            link(nc.vector.memset(bias2[:].bitcast(F32), 0.0))
            ve.wait_ge(small1_in, 16)
            r4 = c1("rows").rearrange("p (r c) -> p r c", r=4)
            link(nc.vector.tensor_copy(bias2[0:1, :], r4[0:1, 0]))
            link(nc.vector.tensor_copy(bias2[32:33, :], r4[32:33, 0]))
            link(nc.vector.tensor_tensor(bias2[32:33, :], r4[32:33, 0], bias2[32:33, :].bitcast(F32), ALU.subtract))
            link(nc.vector.tensor_tensor(wsum[:], r4[:, 1], r4[:, 2], ALU.add))
            link(nc.vector.tensor_tensor(wsum[:], wsum[:], r4[:, 3], ALU.add))
            ve.wait_ge(m_split, 1)
            nc.vector.tensor_tensor(mL[:], bank[4][:, 0:2 * CA], mH[:, 0:2 * CA].bitcast(F32), ALU.subtract)
            nc.vector.tensor_tensor(mH[CB:P, 2 * CA:4 * CA], bank[4][CB:P, 2 * CA:4 * CA], mH[CB:P, 2 * CA:4 * CA].bitcast(F32), ALU.subtract)
            ve.wait_ge(wsplit_hi, 2)
            for hi, lo, raw in ((cfH, cfL, c1("cf")), (vwH, vwL, c1("wv"))):
                nc.vector.tensor_tensor(lo[:], raw[:, 0:C], hi[:, 0:C].bitcast(F32), ALU.subtract)
                last = nc.vector.tensor_tensor(hi[CB:P, C:2 * C], raw[CB:P, C:2 * C], hi[CB:P, C:2 * C].bitcast(F32), ALU.subtract)
            last.then_inc(small_split, 1)

            n2 = IMAGES // 2
            for h in range(2):
                at = slice(n2 * h, n2 * (h + 1))
                ve.wait_ge(cm_in[h], 16)
                for b in range(n2 * h, n2 * (h + 1)):
                    for t in range(2):
                        ins = nc.vector.bn_stats(gst[:, b, t], xcm[:, b, t])
                link(ins)
                st = gst[:, at].rearrange("p b t (e k) -> p (b t) e k", k=3)
                m = mq[:, at].rearrange("p b t e k -> p (b t) e k")
                s = msq[:, at].rearrange("p b t e -> p (b t) e")
                nc.vector.tensor_copy(m[:, :, :, 0], st[:, :, :, 1])
                link(nc.vector.tensor_tensor(s, st[:, :, :, 1], st[:, :, :, 1], ALU.mult))
                nc.vector.scalar_tensor_tensor(out=m[:, :, :, 1], in0=st[:, :, :, 2], scalar=2.0 / PIX, in1=s,
                                               op0=ALU.mult, op1=ALU.add).then_inc(gstat_in, 1)
                ve.wait_ge(gstat_ready, h + 1)
                link(nc.vector.tensor_copy(mv[:, h].rearrange("p t b k -> p (t b k)"), bank[7][:, 0:4 * n2]))
                link(nc.vector.tensor_tensor(gvar[:, h], mv[:, h, :, :, 0], mv[:, h, :, :, 0], ALU.mult))
                nc.vector.tensor_tensor(gvar[:, h], mv[:, h, :, :, 1], gvar[:, h], ALU.subtract).then_inc(gvar_ready, 1)
                ve.wait_ge(gstd_ready, h + 1)
                link(nc.vector.reciprocal(grs[:, h], grs[:, h]))
                nc.vector.scalar_tensor_tensor(out=gnb[:, h], in0=mv[:, h, :, :, 0], scalar=-1.0, in1=grs[:, h],
                                               op0=ALU.mult, op1=ALU.mult).then_inc(gnorm_ready, 1)
            for s in (fh_ready, fl_ready, fq_ready, conv_taken):
                ve.sem_inc(s, AHEAD)
            inner = slice(PAD_PIX, PAD_PIX + PIX)

            def split_image(b, par):
                ve.wait_ge(f_ready, b + 1 + AHEAD)
                ve.wait_ge(ss_ready, b - 1 + AHEAD)
                nc.vector.tensor_copy(fH[:, par, :, inner], f32t[:, par]).then_inc(fh_ready, 1)
                ve.wait_ge(fh_ready, b + 1 + AHEAD)
                nc.vector.tensor_tensor(fL[:, par, :, inner], f32t[:, par], fH[:, par, :, inner].bitcast(F32), ALU.subtract).then_inc(fl_ready, 1)
                nc.vector.tensor_copy(fQ[0:CB, par, inner], fH[0:CB, par, 1, inner].bitcast(F32))
                ve.wait_ge(fl_ready, b + 1 + AHEAD)
                nc.vector.tensor_copy(fQ[CB:P, par, inner], fL[CB:P, par, 1, inner].bitcast(F32)).then_inc(fq_ready, 1)

            def take_conv(b, par):
                ve.wait_ge(conv_ready, b + 1 + AHEAD)
                dst = rows[:, bass.ds(b * HALVES, HALVES), 0:C]
                ve.wait_ge(tm_in, 16)
                nc.vector.tensor_tensor(dst, bank[par][:, 0:HALVES * C].rearrange("p (h c) -> p h c", c=C), dst, ALU.add).then_inc(conv_taken, 1)

            for b in range(2):
                split_image(b, b)
            for i in range(IMAGES // 2 - 1):
                for par in range(2):
                    take_conv(2 * i + par, par)
                    split_image(2 * i + 2 + par, par)
            for b in (IMAGES - 2, IMAGES - 1):
                take_conv(b, b % 2)

            ve.wait_ge(ss_ready, IMAGES + AHEAD)
            nc.vector.tensor_copy(ssq[:], bank[6][:, 0:TILES]).then_inc(ssq_ready, 1)
            ve.wait_ge(nrm_ready, 1)
            link(nc.vector.tensor_scalar(rn[:], rn[:], EPS_NORM, None, ALU.max))
            nc.vector.reciprocal(rn[:], rn[:]).then_inc(rn_ready, 1)
            ve.wait_ge(rn_ready, 1)
            link(nc.vector.tensor_tensor(cc[:], ssq[:], rn[:], ALU.mult))
            nc.vector.tensor_tensor(cc[:], cc[:], rn[:], ALU.mult).then_inc(cc_ready, 1)
            ve.wait_ge(rt_ready, 1)
            nc.vector.tensor_copy(rT[:], bank[7][0:TILES, 0:P]).then_inc(rt_copied, 1)
            ve.wait_ge(rwin_ready, 1)
            link(nc.vector.tensor_copy(rwin[:].rearrange("q b k -> q k b"), bank[5][:, 0:WINDOWS].rearrange("q (k b) -> q k b", b=IMAGES)))

            def scale_gram(c):
                if c >= 2:
                    ve.wait_ge(gsl_ready, c - 1)
                nc.vector.tensor_tensor(gs[:, c % 2].rearrange("q (c w) -> q c w", w=WINDOWS), gram[:, CHUNK * c:CHUNK * (c + 1), :],
                                        rwin[:].rearrange("q b k -> q (b k)").rearrange("q (a w) -> q a w", a=1).to_broadcast([P, CHUNK, WINDOWS]),
                                        ALU.mult).then_inc(gs_ready, 1)
                ve.wait_ge(gsh_ready, c + 1)
                nc.vector.tensor_tensor(gsL[:, c % 2], gs[:, c % 2], gsH[:, c % 2].bitcast(F32), ALU.subtract).then_inc(gsl_ready, 1)

            def take_class(c):
                ve.wait_ge(class_ready, c + 1)
                if c >= 2:
                    ve.wait_ge(corr_out[c % 2], 16 * (c // 2))
                for q in range(CHUNK // 2):
                    a = CHUNK * c + 2 * q
                    ins = nc.vector.tensor_tensor(co[:, c % 2, 2 * q:2 * q + 2], bank[4 * (c % 2) + q][0:WINDOWS, 0:2 * C].rearrange("w (a c) -> w a c", a=2),
                                                  rbk[:, a:a + 2].rearrange("w (a c) -> w a c", c=1).to_broadcast([WINDOWS, 2, C]), ALU.mult)
                ins.then_inc(co_ready, 1)

            ve.wait_ge(cc_ready, 1)
            ve.wait_ge(gram_taken, IMAGES + AHEAD)
            scale_gram(0)
            ve.wait_ge(rbk_in, 16 * (P // PAIR))
            for c in range(CHUNKS):
                if c + 1 < CHUNKS:
                    scale_gram(c + 1)
                take_class(c)
                for j in range(4 * c, 4 * c + 4):
                    ins = nc.vector.scalar_tensor_tensor(out=rows[:, j, 0:C], in0=wsum[:], scalar=cc[:, j:j + 1], in1=rows[:, j, 0:C],
                                                         op0=ALU.mult, op1=ALU.add)
            ins.then_inc(center_added, 1)

            for s in corr_added:
                ve.wait_ge(s, 16)
            ve.wait_ge(empty_out, 16 * (EXPERTS + 1))
            for s in (stats_ready, xl_ready, max_ready, ul_ready, oh_ready, t2_ready, pos_ready):
                ve.sem_inc(s, AHEAD)
            ve.wait_ge(small2_in, 16)
            nc.vector.tensor_copy(tri_sb[:], c2("tri"))
            nc.vector.tensor_copy(run[:], c2("base"))

            LINKS = 13

            def hold():
                ve.sem_inc(held, 1)


            def step(t, par, front, mid, back, nxt, weights=True):
                done = [0]

                def link(ins):
                    done[0] += 1
                    ins.then_inc(dve2, 1)
                    ve.wait_ge(dve2, LINKS * t + (LINKS + done[0]))

                def moments(j, to):
                    hold()
                    for h in range(HALVES):
                        ins = nc.vector.bn_stats(st[:, h], rows[:, bass.ds(j + h, 1), 0:C].rearrange("p a c -> p (a c)"))
                    link(ins)
                    hold()
                    for h in range(HALVES):
                        ins = nc.vector.bn_aggr(to[h], st[:, h])
                    return ins

                if front:
                    ve.wait_ge(xh_ready, t + 1 + AHEAD)
                    nc.vector.tensor_tensor(XL[:, par].rearrange("p t x -> p (t x)"), bank[0][:],
                                            XH[:, par].rearrange("p t x -> p (t x)").bitcast(F32), ALU.subtract).then_inc(xl_ready, 1)
                if mid:
                    ve.wait_ge(s_ready, t + AHEAD)
                    hold()
                    nc.vector.tensor_tensor_reduce(out=sc_sb[:, 0:P], in0=bank[3][:, 0:P], in1=c2("mask")[:, 0:P], scale=1.0, scalar=NEG,
                                                   op0=ALU.add, op1=ALU.max, accum_out=smx[:, 0:1])
                    link(nc.vector.tensor_tensor_reduce(out=sc_sb[:, P:3 * P], in0=bank[3][:, P:3 * P], in1=c2("mask")[:, P:3 * P], scale=1.0,
                                                        scalar=NEG, op0=ALU.add, op1=ALU.max, accum_out=smx[:, 1:2]))
                    nc.vector.tensor_scalar(nmx[:], smx[:], -SM_SCALE, None, ALU.mult).then_inc(max_ready, 1)
                if front:
                    ve.wait_ge(uh_ready, t + 1 + AHEAD)
                    nc.vector.tensor_tensor(uAl[:, par], bank[1][:, 0:PIX], UH[:, par, 0].bitcast(F32), ALU.subtract)
                    nc.vector.tensor_tensor(UH[CB:P, par, 1], bank[1][CB:P, PIX:2 * PIX], UH[CB:P, par, 1].bitcast(F32), ALU.subtract).then_inc(ul_ready, 1)
                if nxt:
                    moments(2 * t + 2, [ln1[:, 1 - par, h] for h in range(HALVES)]).then_inc(stats_ready, 1)
                if back:
                    ve.wait_ge(g_ready, t - 1 + AHEAD)
                    desc = c2("desc").rearrange("p (h e) -> p h e", h=2)
                    wide = [P, 2, EXPERTS]
                    link(nc.vector.tensor_tensor(lg[:], bank[7][:, 0:2 * EXPERTS].rearrange("p (h e) -> p h e", h=2),
                                                 c2("bg").rearrange("p (h e) -> p h e", h=2), ALU.add))
                    link(nc.vector.tensor_reduce(gmx[:], lg[:], AX_X, ALU.max))
                    link(nc.vector.tensor_tensor(lg[:], lg[:], gmx[:].rearrange("p (h a) -> p h a", a=1).to_broadcast(wide), ALU.is_ge))
                    link(nc.vector.tensor_tensor(lg[:], lg[:], desc, ALU.mult))
                    link(nc.vector.tensor_reduce(gmx[:], lg[:], AX_X, ALU.max))
                    nc.vector.tensor_tensor(oh[:], lg[:], gmx[:].rearrange("p (h a) -> p h a", a=1).to_broadcast(wide), ALU.is_equal).then_inc(oh_ready, 1)
                if mid:
                    ve.wait_ge(o_ready, t + AHEAD)
                    link(nc.vector.reciprocal(smx[:], ssum[:]))
                    for h in range(HALVES):
                        row = rows[:, bass.ds(2 * t + (h - 2), 1), 0:C].rearrange("p a c -> p (a c)")
                        ins = nc.vector.scalar_tensor_tensor(out=row, in0=bank[5][:, C * h:C * (h + 1)], scalar=smx[:, h:h + 1], in1=row,
                                                             op0=ALU.mult, op1=ALU.add)
                    link(ins)
                    moments(2 * t - 2, [ln2[:, 1 - par, h] for h in range(HALVES)]).then_inc(t2_ready, 1)
                if back:
                    ve.wait_ge(pf_ready, t - 1 + AHEAD)
                    r1 = run[:].rearrange("p (h e) -> p h e", h=1).to_broadcast(wide)
                    link(nc.vector.tensor_tensor(lg[:], bank[7][:, 2 * EXPERTS:4 * EXPERTS].rearrange("p (h e) -> p h e", h=2), r1, ALU.add))
                    link(nc.vector.tensor_tensor(lg[:], lg[:], oh[:], ALU.mult))
                    nc.vector.tensor_tensor(run[:], run[:], bank[7][:, 4 * EXPERTS:5 * EXPERTS], ALU.add)
                    link(nc.vector.tensor_reduce(pos[:], lg[:], AX_X, ALU.add))
                    hold()
                    nc.vector.tensor_copy(posi[:, bass.ds(2 * t - 4, 2)], pos[:]).then_inc(pos_ready, 1)
                if weights:
                    ve.wait_ge(wall_hi, t)
                    w = wall[CB:P, bass.ds(t - 1, 1), 2 * W12:3 * W12].rearrange("p a c -> p (a c)")
                    nc.vector.tensor_tensor(w, stage[CB:P, 1 - par, W12:2 * W12], w.bitcast(F32), ALU.subtract).then_inc(wall_q, 1)
                if done[0] < LINKS:
                    ve.sem_inc(dve2, LINKS - done[0])
                assert done[0] <= LINKS

            step(-1, 1, False, False, False, True, False)
            step(0, 0, True, False, False, True, False)
            step(1, 1, True, True, False, True)
            with ve.Fori(1, IMAGES // 2 - 1) as i:
                for par in range(2):
                    step(2 * i + par, par, True, True, True, True)
            step(IMAGES - 2, 0, True, True, True, True)
            step(IMAGES - 1, 1, True, True, True, False)
            step(IMAGES, 0, False, True, True, False, False)
            step(IMAGES + 1, 1, False, False, True, False, False)
            ve.wait_ge(pos_ready, IMAGES + AHEAD)
            link(nc.vector.tensor_tensor(tiles_f[:], run[:], c2("base"), ALU.subtract))
            link(nc.vector.tensor_scalar(tiles_f[:], tiles_f[:], float(P - 1), None, ALU.add))
            link(nc.vector.tensor_copy(tiles_i[:], tiles_f[:]))
            link(nc.vector.tensor_scalar(tiles_i[:], tiles_i[:], P.bit_length() - 1, None, ALU.logical_shift_right))
            link(nc.vector.tensor_copy(tiles_f[:], tiles_i[:]))
            link(nc.vector.tensor_copy(ends[:, 0], tiles_f[:]))
            for n, d in enumerate((1, 2, 4)):
                a, z = n % 2, 1 - n % 2
                nc.vector.tensor_copy(ends[:, z, 0:d], ends[:, a, 0:d])
                link(nc.vector.tensor_tensor(ends[:, z, d:EXPERTS], ends[:, a, d:EXPERTS], ends[:, a, 0:EXPERTS - d], ALU.add))
            starts = ends[:, 0]
            link(nc.vector.tensor_tensor(starts, ends[:, 1], tiles_f[:], ALU.subtract))
            wide = [P, SLOTS, EXPERTS]
            slot = c2("slot")[:, 0:SLOTS]
            slot3 = slot.rearrange("p (j a) -> p j a", a=1).to_broadcast(wide)

            def over_slots(v):
                return v.rearrange("p (a e) -> p a e", a=1).to_broadcast(wide)

            link(nc.vector.tensor_tensor(started[:], slot3, over_slots(starts), ALU.is_ge))
            nc.vector.tensor_reduce(per_slot[:, 0], started[:], AX_X, ALU.add)
            link(nc.vector.tensor_tensor(picked[:], started[:], over_slots(starts), ALU.mult))
            link(nc.vector.tensor_reduce(per_slot[:, 1], picked[:], AX_X, ALU.max))
            link(nc.vector.tensor_tensor(picked[:], started[:], over_slots(run[:]), ALU.mult))
            link(nc.vector.tensor_reduce(per_slot[:, 2], picked[:], AX_X, ALU.max))
            link(nc.vector.tensor_scalar(per_slot[:, 0], per_slot[:, 0], -1.0, None, ALU.add))
            nc.vector.tensor_copy(slot_expert[:], per_slot[:, 0])
            link(nc.vector.tensor_tensor(per_slot[:, 1], per_slot[:, 1], slot, ALU.subtract))
            link(nc.vector.tensor_scalar(per_slot[:, 1], per_slot[:, 1], -1.0, float(P), ALU.add, ALU.mult))
            link(nc.vector.tensor_tensor(per_slot[:, 2], per_slot[:, 2], per_slot[:, 1], ALU.add))
            link(nc.vector.tensor_scalar(per_slot[:, 3], slot, ends[:, 1, EXPERTS - 1:EXPERTS], 1e6, ALU.is_ge, ALU.mult))
            link(nc.vector.tensor_tensor(per_slot[:, 2], per_slot[:, 2], per_slot[:, 3], ALU.add))
            link(nc.vector.tensor_scalar(per_slot[:, 2], per_slot[:, 2], float(EMPTY), None, ALU.min))
            nc.vector.tensor_copy(slot_row[:], per_slot[:, 2]).then_inc(table_ready, 1)
            nc.vector.memset(gh[:, :, FE:FT * P], 0.0)
            ve.wait_ge(wall_hi, EXPERTS)
            raw, w = stage[:, (CHUNKS + EXPERTS - 1) % 2], wall[:, EXPERTS - 1]
            nc.vector.tensor_tensor(w[:, W12:2 * W12], raw[:, 0:W12], w[:, 0:W12].bitcast(F32), ALU.subtract)
            nc.vector.tensor_tensor(w[CB:P, 2 * W12:3 * W12], raw[CB:P, W12:2 * W12], w[CB:P, 2 * W12:3 * W12].bitcast(F32), ALU.subtract)
            w3 = w[:, 3 * W12:WALL].rearrange("p (k s c) -> p k s c", s=2, c=C)
            nc.vector.tensor_tensor(w3[:, :, 1], raw[:, 2 * W12:STAGE].rearrange("p (k c) -> p k c", c=C),
                                    w3[:, :, 0].bitcast(F32), ALU.subtract).then_inc(wall_dve, 1)
            for s in (fl2_ready, gh_ready, hl_ready, y_taken):
                ve.sem_inc(s, AHEAD)

            def ffn_step(j, par, back, mid, nxt):
                if back:
                    ve.wait_ge(hh_ready, j + AHEAD)
                    nc.vector.tensor_tensor(HL[:, 1 - par].rearrange("p k x -> p (k x)"), bank[5][:],
                                            HH[:, 1 - par].rearrange("p k x -> p (k x)").bitcast(F32), ALU.subtract).then_inc(hl_ready, 1)
                if mid:
                    ve.wait_ge(silu_ready, j + 1 + AHEAD)
                    nc.vector.tensor_tensor(gh[:, par, 0:FE], gh[:, par, 0:FE], bank[2 + 2 * par][:, 0:FE], ALU.mult).then_inc(gh_ready, 1)
                if nxt:
                    ve.wait_ge(fh2_ready, j + 2 + AHEAD)
                    nc.vector.tensor_tensor(FL[:, 1 - par].rearrange("p t x -> p (t x)"), bank[0][:, 0:2 * P],
                                            FH[:, 1 - par].rearrange("p t x -> p (t x)").bitcast(F32), ALU.subtract).then_inc(fl2_ready, 1)
                if back:
                    y = bank[7 - par]
                    ve.wait_ge(y_ready, j + AHEAD)
                    ve.wait_ge(yo_free, j - 2 + AHEAD)
                    row = rows[:, bass.ds(j - 1, 1), 0:C].rearrange("p a c -> p (a c)")
                    nc.vector.tensor_tensor(yo[:, 1 - par], y[:, C:2 * C], row, ALU.add).then_inc(dve3, 1)
                    ve.wait_ge(dve3, j)
                    nc.vector.tensor_tensor(yo[:, 1 - par], yo[:, 1 - par], y[:, 0:C], ALU.add).then_inc(y_taken, 1)

            ffn_step(-1, 1, False, False, True)
            ffn_step(0, 0, False, True, True)
            ffn_step(1, 1, True, True, True)
            with ve.Fori(1, SLOTS // 2) as i:
                for par in range(2):
                    ffn_step(2 * i + par, par, True, True, True)
            ffn_step(SLOTS - 1, 0, True, True, False)
            ffn_step(SLOTS, 1, True, False, False)

        @block.tensor
        def _(pe):
            pe.wait_ge(small1_in, 16)
            wq, wk = (c1(n).rearrange("p (t n) -> p t n", t=2) for n in ("wq", "wk"))
            for m in range(2):
                for t, k in ((0, P), (1, CB)):
                    mm = nc.tensor.matmul(bank[4][:, 2 * CA * m:2 * CA * (m + 1)], wq[0:k, t, CA * m:CA * (m + 1)], wk[0:k, t, :], start=(t == 0), stop=(t == 1))
            mm.then_inc(m_ready, 1)
            n2 = IMAGES // 2
            gm = c1("gm").rearrange("p (t n) -> p t n", t=2)
            for h in range(2):
                pe.wait_ge(gstat_in, h + 1)
                if h:
                    pe.wait_ge(gvar_ready, h)
                for m in range(2):
                    n = 0
                    for t, k in ((0, P), (1, CB)):
                        for eo in range(2):
                            mm = nc.tensor.matmul(bank[7][:, 2 * n2 * m:2 * n2 * (m + 1)], gm[0:k, t, CA * m:CA * (m + 1)],
                                                  mq[0:k, n2 * h:n2 * (h + 1), t, eo, :], start=(n == 0), stop=(n == 3))
                            n += 1
                mm.then_inc(gstat_ready, 1)

            for s in (conv_ready, gram_ready, ss_ready):
                pe.sem_inc(s, AHEAD)
            pe.wait_ge(small_split, 1)

            def products(dst, xh_a, xl_a, xh_b, xl_b, y_a, yl_a, y_q, y_q64, more=False):
                nc.tensor.matmul(dst, xh_a, y_a, start=True, stop=False)
                nc.tensor.matmul(dst, xh_a, yl_a, start=False, stop=False)
                nc.tensor.matmul(dst, xl_a, y_a, start=False, stop=False)
                nc.tensor.matmul(dst, xh_b, y_q, start=False, stop=False)
                return nc.tensor.matmul(dst, xl_b, y_q64, start=False, stop=not more)

            with pe.Fori(0, IMAGES // 2) as i:
                for par in range(2):
                    pe.wait_ge(fq_ready, 2 * i + (par + 1 + AHEAD))
                    pe.wait_ge(conv_taken, 2 * i + (par - 1 + AHEAD))
                    for h in range(HALVES):
                        t = slice(PAD_PIX + P * h, PAD_PIX + P * (h + 1))
                        dst = bank[par][:, C * h:C * (h + 1)]
                        products(dst, fH[:, par, 0, t], fL[:, par, 0, t], fH[:, par, 1, t], fL[0:CB, par, 1, t],
                                 cfH[:, 0:C], cfL[:, :], cfH[:, C:2 * C], cfH[0:CB, C:2 * C], more=True)
                        mm = nc.tensor.matmul(dst, ones2[:], bias2[:], start=False, stop=True)
                    mm.then_inc(conv_ready, 1)
                    pe.wait_ge(gram_taken, 2 * i + (par - 1 + AHEAD))
                    for k in range(PAIRS):
                        q = slice(PAIR * k, PAIR * k + P)
                        p = slice(PAD_PIX + PAIR * k, PAD_PIX + PAIR * (k + 1))
                        mm = products(bank[2 + par][:, PAIR * k:PAIR * (k + 1)], fH[:, par, 0, q], fL[:, par, 0, q], fH[:, par, 1, q], fL[0:CB, par, 1, q],
                                      fH[:, par, 0, p], fL[:, par, 0, p], fQ[:, par, p], fQ[0:CB, par, p])
                    mm.then_inc(gram_ready, 1)
                    pe.wait_ge(fsq_ready, 2 * i + (par + 1 + AHEAD))
                    for h in range(HALVES):
                        dst = bank[6][:, bass.ds(HALVES * (2 * i + par) + h, 1)]
                        nc.tensor.matmul(dst, fsq[:, par, 0, P * h:P * (h + 1)], onesc[:], start=True, stop=False)
                        mm = nc.tensor.matmul(dst, fsq[0:CB, par, 1, P * h:P * (h + 1)], onesc[0:CB], start=False, stop=True)
                    mm.then_inc(ss_ready, 1)

            pe.wait_ge(rn_ready, 1)
            pe.wait_ge(small2_in, 16)
            nc.tensor.transpose(bank[7][0:TILES, 0:P], rn[:], ident).then_inc(rt_ready, 1)
            rnv = rn[:].rearrange("p (b h) -> p h b", h=HALVES)
            for k in range(PAIRS):
                for h in range(HALVES):
                    off = SHIFT0 - P * h + PAIR * k - PAD_PIX
                    mm = nc.tensor.matmul(bank[5][:, IMAGES * k:IMAGES * (k + 1)], c1("shift")[:, off:off + P], rnv[:, h], start=(h == 0), stop=(h == HALVES - 1))
            mm.then_inc(rwin_ready, 1)
            pe.wait_ge(stage_free, CHUNKS)
            for c in range(CHUNKS):
                pe.wait_ge(gsl_ready, c + 1)
                if c == 1:
                    pe.wait_ge(gs_ready, 1)
                if c >= 2:
                    pe.wait_ge(co_ready, c - 1)
                for a in range(CHUNK):
                    dst = bank[4 * (c % 2) + a // 2][0:WINDOWS, C * (a % 2):C * (a % 2 + 1)]
                    w = slice(WINDOWS * a, WINDOWS * (a + 1))
                    n = slice(C * (CHUNK * c + a), C * (CHUNK * c + a + 1))
                    nc.tensor.matmul(dst, gsH[:, c % 2, w], bandH[:, n], start=True, stop=False)
                    nc.tensor.matmul(dst, gsH[:, c % 2, w], bandL[:, n], start=False, stop=False)
                    mm = nc.tensor.matmul(dst, gsL[:, c % 2, w], bandH[:, n], start=False, stop=True)
                mm.then_inc(class_ready, 1)

            pe.wait_ge(co_ready, CHUNKS)
            pe.wait_ge(corr_added[0], 16)
            for s in (xt_ready, u_ready, v_ready, s_ready, pt_ready, o_ready, t2t_ready, g_ready, pf_ready):
                pe.sem_inc(s, AHEAD)

            def step(t, par, front, mid, back):
                old = 1 - par
                if front:
                    pe.wait_ge(xn_ready, t + 1 + AHEAD)
                    pe.wait_ge(xl_ready, t + AHEAD)
                    for part in range(2):
                        for h in range(HALVES):
                            at = PIX * part + P * h
                            mm = nc.tensor.transpose(bank[0][:, at:at + P], xn[:, h, CA * part:CA * (part + 1)], ident)
                    mm.then_inc(xt_ready, 1)
                if mid:
                    pe.wait_ge(ul_ready, t + AHEAD)
                    pe.wait_ge(max_ready, t - 1 + AHEAD)
                    for h in range(HALVES):
                        q, k = slice(P * h, P * (h + 1)), slice(0, P * (h + 1))
                        dst = bank[3][:, P * h:P * h + P * (h + 1)]
                        xh_a, xl_a, xh_b, xl_b = XH[:, old, 0, k], XL[:, old, 0, k], XH[:, old, 1, k], XL[0:CB, old, 1, k]
                        nc.tensor.matmul(dst, UH[:, old, 0, q], xh_a, start=True, stop=False)
                        nc.tensor.matmul(dst, UH[:, old, 0, q], xl_a, start=False, stop=False)
                        nc.tensor.matmul(dst, uAl[:, old, q], xh_a, start=False, stop=False)
                        nc.tensor.matmul(dst, UH[:, old, 1, q], xh_b, start=False, stop=False)
                        mm = nc.tensor.matmul(dst, UH[0:CB, old, 1, q], xl_b, start=False, stop=True)
                    mm.then_inc(s_ready, 1)
                if back:
                    pe.wait_ge(xn2_ready, t - 1 + AHEAD)
                    pe.wait_ge(x2_copied, t - 2 + AHEAD)
                    for part in range(2):
                        for h in range(HALVES):
                            at = PIX * part + P * h
                            mm = nc.tensor.transpose(bank[6][:, at:at + P], xn2[:, h, CB * part:CB * part + P], ident)
                    mm.then_inc(t2t_ready, 1)
                if front:
                    pe.wait_ge(xl_ready, t + 1 + AHEAD)
                    pe.wait_ge(ul_ready, t + AHEAD)
                    for m in range(2):
                        dst = bank[1][:, PIX * m:PIX * (m + 1)]
                        c = slice(CA * m, CA * (m + 1))
                        q = slice(2 * CA + CA * m, 2 * CA + CA * (m + 1))
                        nc.tensor.matmul(dst, mH[:, c], XH[:, par, 0], start=True, stop=False)
                        nc.tensor.matmul(dst, mH[:, c], XL[:, par, 0], start=False, stop=False)
                        nc.tensor.matmul(dst, mL[:, c], XH[:, par, 0], start=False, stop=False)
                        nc.tensor.matmul(dst, mH[:, q], XH[:, par, 1], start=False, stop=False)
                        mm = nc.tensor.matmul(dst, mH[0:CB, q], XL[0:CB, par, 1], start=False, stop=True)
                    mm.then_inc(u_ready, 1)
                if mid:
                    pe.wait_ge(exp_ready, t + AHEAD)
                    pe.wait_ge(pt_copied, t - 1 + AHEAD)
                    for k in range(3):
                        mm = nc.tensor.transpose(bank[4][:, P * k:P * (k + 1)], Pr[:, P * k:P * (k + 1)], ident)
                    mm.then_inc(pt_ready, 1)
                if front:
                    pe.wait_ge(v_copied, t + AHEAD)
                    for h in range(HALVES):
                        q = slice(P * h, P * (h + 1))
                        mm = products(bank[2][:, C * h:C * (h + 1)], XH[:, par, 0, q], XL[:, par, 0, q], XH[:, par, 1, q], XL[0:CB, par, 1, q],
                                      vwH[:, 0:C], vwL[:], vwH[:, C:2 * C], vwH[0:CB, C:2 * C])
                    mm.then_inc(v_ready, 1)
                if back:
                    pe.wait_ge(x2_copied, t - 1 + AHEAD)
                    pe.wait_ge(pos_ready, t - 2 + AHEAD)
                    wg = c2("wg")
                    for h in range(HALVES):
                        dst = bank[7][:, EXPERTS * h:EXPERTS * (h + 1)]
                        nc.tensor.matmul(dst, x2T[:, 0, P * h:P * (h + 1)], wg[:, 0:EXPERTS], start=True, stop=False)
                        mm = nc.tensor.matmul(dst, x2T[CB:P, 1, P * h:P * (h + 1)], wg[CB:P, EXPERTS:2 * EXPERTS], start=False, stop=True)
                    mm.then_inc(g_ready, 1)
                if mid:
                    pe.wait_ge(pt_copied, t + AHEAD)
                    pe.wait_ge(v_copied, t + AHEAD)
                    pe.wait_ge(t2_ready, t - 1 + AHEAD)
                    nc.tensor.matmul(bank[5][:, 0:C], PT[:, 0:P], V[:, old, 0], start=True, stop=True)
                    nc.tensor.matmul(bank[5][:, C:2 * C], PT[:, P:2 * P], V[:, old, 0], start=True, stop=False)
                    nc.tensor.matmul(bank[5][:, C:2 * C], PT[:, 2 * P:3 * P], V[:, old, 1], start=False, stop=True).then_inc(o_ready, 1)
                if back:
                    pe.wait_ge(oh_ready, t - 1 + AHEAD)
                    before, all_ = tri_sb[:, 0:P], tri_sb[:, P:2 * P]
                    e = 2 * EXPERTS
                    nc.tensor.matmul(bank[7][:, e:e + EXPERTS], before, oh[:, 0], start=True, stop=True)
                    e += EXPERTS
                    nc.tensor.matmul(bank[7][:, e:e + EXPERTS], before, oh[:, 1], start=True, stop=False)
                    nc.tensor.matmul(bank[7][:, e:e + EXPERTS], all_, oh[:, 0], start=False, stop=True)
                    e += EXPERTS
                    nc.tensor.matmul(bank[7][:, e:e + EXPERTS], all_, oh[:, 0], start=True, stop=False)
                    nc.tensor.matmul(bank[7][:, e:e + EXPERTS], all_, oh[:, 1], start=False, stop=True).then_inc(pf_ready, 1)

            step(0, 0, True, False, False)
            step(1, 1, True, True, False)
            with pe.Fori(1, IMAGES // 2) as i:
                for par in range(2):
                    step(2 * i + par, par, True, True, True)
            step(IMAGES, 0, False, True, True)
            step(IMAGES + 1, 1, False, False, True)
            for s in (fxt_ready, h_ready, gt_ready, y_ready):
                pe.sem_inc(s, AHEAD)

            def ffn_step(j, par, back, mid, nxt):
                def expert(j):
                    pe.wait_ge(table_ready, 1)
                    e = pe.value_load(slot_expert[0:1, bass.ds(j, 1)], min_val=0, max_val=EXPERTS - 1)

                    def cols(p0, p1, c0, c1):
                        return wall[p0:p1, bass.ds(e, 1), c0:c1].rearrange("p a c -> p (a c)")
                    return cols

                if back:
                    pe.wait_ge(gh_ready, j + AHEAD)
                    for k in range(FT):
                        mm = nc.tensor.transpose(bank[5][:, P * k:P * (k + 1)], gh[:, 1 - par, P * k:P * (k + 1)], ident)
                    mm.then_inc(gt_ready, 1)
                if mid:
                    w = expert(j)
                    pe.wait_ge(fl2_ready, j + 1 + AHEAD)
                    for m in range(2):
                        dst = bank[1 + 2 * par + m][:, 0:FE]
                        a, q = FE * m, 2 * W12 + FE * m
                        mm = products(dst, FH[:, par, 0], FL[:, par, 0], FH[:, par, 1], FL[0:CB, par, 1],
                                      w(0, P, a, a + FE), w(0, P, W12 + a, W12 + a + FE), w(0, P, q, q + FE), w(0, CB, q, q + FE))
                    mm.then_inc(h_ready, 1)
                if nxt:
                    pe.wait_ge(fx_ready, j + 2 + AHEAD)
                    pe.wait_ge(fl2_ready, j + 1 + AHEAD)
                    for part in range(2):
                        mm = nc.tensor.transpose(bank[0][:, P * part:P * (part + 1)], xf[:, CA * part:CA * (part + 1)], ident)
                    mm.then_inc(fxt_ready, 1)
                if back:
                    w = expert(j - 1)
                    pe.wait_ge(hl_ready, j + AHEAD)
                    pe.wait_ge(y_taken, j - 2 + AHEAD)
                    dst = bank[7 - par]
                    for k in range(FT):
                        c0 = 3 * W12 + 2 * C * k
                        nc.tensor.matmul(dst[:, 0:2 * C], HH[:, 1 - par, k], w(0, P, c0, c0 + 2 * C), start=(k == 0), stop=False)
                        mm = nc.tensor.matmul(dst[:, 0:C], HL[:, 1 - par, k], w(0, P, c0, c0 + C), start=False, stop=(k == FT - 1))
                    mm.then_inc(y_ready, 1)

            ffn_step(-1, 1, False, False, True)
            pe.wait_ge(wall_lo, EXPERTS - 1)
            pe.wait_ge(wall_q, EXPERTS - 1)
            pe.wait_ge(wall_dve, 1)
            ffn_step(0, 0, False, True, True)
            ffn_step(1, 1, True, True, True)
            with pe.Fori(1, SLOTS // 2) as i:
                for par in range(2):
                    ffn_step(2 * i + par, par, True, True, True)
            ffn_step(SLOTS - 1, 0, True, True, False)
            ffn_step(SLOTS, 1, True, False, False)


def lay_out(x, conv_w, conv_b, wq, wk, wv, Wg, bg, W1, W2, W3):
    import numpy as np

    f = np.float32

    def a_bb(m):
        return np.stack([m[:CA], np.concatenate([m[CA:], m[CA:]])], 1)

    def cols_a_bb(m):
        return np.concatenate([m[:, :CA], m[:, CA:], m[:, CA:]], 1)

    xt = x.reshape(IMAGES, C, PIX)
    x_cm = np.stack([xt[:, :CA], np.concatenate([xt[:, CA:], xt[:, CA:]], 1)], 2).reshape(IMAGES, P, 2 * PIX)
    x_tm = xt.transpose(0, 2, 1).reshape(TILES, P, C).transpose(1, 0, 2)

    group = np.arange(C) // (C // GROUPS)
    gm = (group[:, None] == group[None, :]).astype(f) / (2 * C // GROUPS)
    shift = (np.arange(480)[None, :] == np.arange(P)[:, None] + SHIFT0).astype(f)
    offs = [(i, i) for i in range(KERNEL)] + [(i, REACH) for i in range(KERNEL)]
    offs += [(i, KERNEL - 1 - i) for i in range(KERNEL)] + [(REACH, i) for i in range(KERNEL)]
    centers = [n for n, o in enumerate(offs) if o == (REACH, REACH)]
    rows4 = np.stack([conv_b] + [conv_w[:, C + n] for n in centers[1:]])
    s1 = [a_bb(conv_w[:, :C].T), a_bb(cols_a_bb(gm)), np.broadcast_to(rows4, (P, 4, C)),
          a_bb(cols_a_bb(wq.T)), a_bb(cols_a_bb(wk.T)), a_bb(wv), shift]
    small1 = np.concatenate([a.reshape(P, -1) for a in s1], 1)
    assert small1.shape[1] == S1N

    band = np.zeros((P, PAIR, C), f)
    for n, (r, cx) in enumerate(offs):
        if n in centers[1:]:
            continue
        for p in range(PAIR):
            q = p % SIDE + cx - REACH
            if 0 <= q < SIDE:
                band[(p // SIDE + r) * SIDE + q, p] = conv_w[:, C + n]
    band = band.reshape(P, PAIR * C)

    k = np.arange(P)
    causal = np.where(k[None, :] <= k[:, None], 0.0, NEG).astype(f)
    mask = np.concatenate([causal, np.zeros((P, P), f), causal], 1)
    desc = np.broadcast_to(np.arange(EXPERTS, 0, -1).astype(f), (P, 2, EXPERTS))
    base = np.broadcast_to((np.arange(EXPERTS) * REGION + PAD).astype(f), (P, EXPERTS))
    slot = np.broadcast_to(np.arange(SLOTS + 1).astype(f), (P, SLOTS + 1))
    s2 = [np.eye(P, dtype=f), mask, a_bb(Wg.T), np.broadcast_to(bg, (P, 2, EXPERTS)), desc, base, slot,
          (k[:, None] < k[None, :]).astype(f), np.ones((P, P), f)]
    small2 = np.concatenate([a.reshape(P, -1) for a in s2], 1)
    assert small2.shape[1] == S2N

    w12 = np.zeros((EXPERTS, C, 2, FE), f)
    w12[:, :, 0, :F] = W1.transpose(0, 2, 1)
    w12[:, :, 1, :F] = W2.transpose(0, 2, 1)
    w12 = w12.reshape(EXPERTS, C, W12)
    w3 = np.zeros((EXPERTS, FT * P, C), f)
    w3[:, :F] = W3.transpose(0, 2, 1)
    w3 = w3.reshape(EXPERTS, FT, P, C).transpose(0, 2, 1, 3).reshape(EXPERTS, P, W3C)
    w_all = np.concatenate([w12[:, :CA], np.concatenate([w12[:, CA:], w12[:, CA:]], 1), w3], 2)
    return [("x_cm", x_cm), ("x_tm", x_tm), ("small1", small1), ("small2", small2), ("band", band), ("w_all", w_all)]


def kernel(x, L0_conv_conv_w, L0_conv_conv_b, L1_attn_wq, L1_attn_wk, L1_attn_wv, L1_ffn_Wg, L1_ffn_bg, L1_ffn_W1, L1_ffn_W2, L1_ffn_W3):
    import numpy as np
    import concourse.bacc as bacc
    from concourse.bass_utils import run_bass_kernel_spmd as run

    ins = lay_out(*(np.asarray(a) for a in (x, L0_conv_conv_w, L0_conv_conv_b, L1_attn_wq, L1_attn_wk, L1_attn_wv,
                                            L1_ffn_Wg, L1_ffn_bg, L1_ffn_W1, L1_ffn_W2, L1_ffn_W3)))
    nc = bacc.Bacc("TRN2", target_bir_lowering=False, num_devices=1)
    arrays, args = {}, []
    for name, a in ins:
        arrays["in_" + name] = np.ascontiguousarray(a)
        args.append(nc.dram_tensor("in_" + name, a.shape, mybir.dt.from_np(a.dtype), kind="ExternalInput").ap())
    out = nc.dram_tensor("out_rows", (TILES * P, C), F32, kind="ExternalOutput").ap()
    build(nc, *args, out)
    res = run(nc, [arrays], core_ids=[0])
    t = res.results[0]["out_rows"]
    return np.ascontiguousarray(t.reshape(IMAGES, PIX, C).transpose(0, 2, 1).reshape(IMAGES, C, SIDE, SIDE))
```

```python
from contextlib import ExitStack

import concourse.bass as bass
from concourse import mybir

F32 = mybir.dt.float32
F32R = mybir.dt.float32r
BF16 = mybir.dt.bfloat16
I32 = mybir.dt.int32
U32 = mybir.dt.uint32
ALU = mybir.AluOpType
ACT = mybir.ActivationFunctionType
AX_X = mybir.AxisListType.X

P = 128
IMAGES = 8
SIDE = 16
PIX = SIDE * SIDE
C = 192
CA, CB = P, C - P
HALVES = PIX // P
TILES = IMAGES * HALVES
GROUPS = 32
KERNEL = 7
REACH = KERNEL // 2
PAD_PIX = REACH * SIDE
NEAR = P + 4 * SIDE
PAIR = 2 * SIDE
PAIRS = PIX // PAIR
WINDOWS = IMAGES * PAIRS
CHUNK = 8
CHUNKS = PAIR // CHUNK
BAND_CHUNK = CHUNK * C

EXPERTS = 8
F = 469
FE = F + 1
FT = 4
W12 = 2 * FE
W3C = FT * C
STAGE = 2 * W12 + W3C
WALL = 3 * W12 + 2 * W3C
SLOTS = TILES + EXPERTS - 1
PAD = P
REGION = TILES * P + PAD
EMPTY = EXPERTS * REGION
NO_TOKEN = 1 << 20
ROW = C + 4

EPS_NORM = 1e-12
EPS = 1e-5
NEG = -1e30
SM_SCALE = float(C) ** -0.5
AHEAD = 2
GUESS = float(0x5F3759DF)

S1 = {}
S2 = {}
_at = 0
for _n, _w in (("cf", 2 * C), ("gm", 4 * CA), ("rows", 4 * C), ("wq", 4 * CA), ("wk", 4 * CA), ("wv", 2 * C), ("shift", 480)):
    S1[_n] = (_at, _at + _w)
    _at += _w
S1N = _at
_at = 0
for _n, _w in (("id", P), ("mask", 3 * P), ("wg", 2 * EXPERTS), ("bg", 2 * EXPERTS), ("desc", 2 * EXPERTS), ("base", EXPERTS), ("slot", SLOTS + 1), ("tri", 2 * P)):
    S2[_n] = (_at, _at + _w)
    _at += _w
S2N = _at
SHIFT0 = 176


def build(nc, x_cm, x_tm, small1, small2, band, w_all, out):
    xs = nc.dram_tensor("token_rows", (EMPTY + P, ROW), F32).ap()
    corr = nc.dram_tensor("corr_rows", (TILES * P, C), F32).ap()

    top = ExitStack()
    with top:
        def sb(name, shape, dt=F32, ctx=top):
            return ctx.enter_context(nc.sbuf_tensor(name, shape, dt))

        def sem(name):
            return top.enter_context(nc.semaphore(name))

        bank = [top.enter_context(nc.psum_tensor(f"bank{i}", [P, 512], F32)) for i in range(8)]

        rows = sb("rows", [P, SLOTS, ROW])
        s2 = sb("small2_sb", [P, S2N])
        stage = sb("stage", [P, 2, STAGE])
        mH = sb("mH", [P, 4 * CA], F32R)
        mL = sb("mL", [P, 2 * CA], F32R)
        vwH = sb("vwH", [P, 2 * C], F32R)
        vwL = sb("vwL", [P, C], F32R)
        tri_sb = sb("tri_sb", [P, 2 * P], BF16)
        eps_c = sb("eps_c", [P, 1])
        run = sb("run", [P, EXPERTS])
        posi = sb("posi", [P, TILES], I32)

        def c2(name):
            return s2[:, S2[name][0]:S2[name][1]]

        ident = c2("id")

        early = ExitStack()
        early.enter_context(nc.sbuf_tensor("early_gap", [P, WALL], F32R))
        bandH = sb("bandH", [P, PAIR * C], F32R, early)
        bandL = sb("bandL", [P, PAIR * C], F32R, early)
        xcm = sb("xcm", [P, IMAGES, 2, PIX], ctx=early)
        s1 = sb("small1_sb", [P, S1N], ctx=early)
        f32t = sb("f32t", [P, 2, 2, PIX], ctx=early)
        f2 = sb("f2", [P, 2, 2, 2, PIX], F32R, early)
        fQ = sb("fQ", [P, 2, PIX], F32R, early)
        gram = sb("gram", [P, IMAGES, HALVES, NEAR], ctx=early)
        around = sb("around", [P, IMAGES, PAIRS, PAIR], ctx=early)
        gs = sb("gs", [P, 2, CHUNK * WINDOWS], ctx=early)
        gsH = sb("gsH", [P, 2, CHUNK * WINDOWS], F32R, early)
        gsL = sb("gsL", [P, 2, CHUNK * WINDOWS], F32R, early)
        co = sb("co", [WINDOWS, 2, CHUNK, C], ctx=early)
        cfH = sb("cfH", [P, 2 * C], F32R, early)
        cfL = sb("cfL", [P, C], F32R, early)
        bias2 = sb("bias2", [CB, C], F32R, early)
        ones2 = sb("ones2", [CB, P], F32R, early)
        wsum = sb("wsum", [P, C], ctx=early)
        gst = sb("gst", [P, IMAGES, 2, 6], ctx=early)
        mq = sb("mq", [P, IMAGES, 2, 2, 2], ctx=early)
        msq = sb("msq", [P, IMAGES, 2, 2], ctx=early)
        mv = sb("mv", [P, 2, 2, IMAGES // 2, 2], ctx=early)
        gvar = sb("gvar", [P, 2, 2, IMAGES // 2], ctx=early)
        grs = sb("grs", [P, 2, 2, IMAGES // 2], ctx=early)
        gnb = sb("gnb", [P, 2, 2, IMAGES // 2], ctx=early)
        ssq = sb("ssq", [P, TILES], ctx=early)
        rn = sb("rn", [P, TILES], ctx=early)
        cc = sb("cc", [P, TILES], ctx=early)
        rwin = sb("rwin", [P, IMAGES, PAIRS], ctx=early)
        rT = sb("rT", [TILES, P], ctx=early)
        rbk = sb("rbk", [WINDOWS, PAIR], ctx=early)
        emptyt = sb("emptyt", [P, ROW], ctx=early)
        early.close()

        middle = ExitStack()
        middle.enter_context(nc.sbuf_tensor("middle_gap", [P, (EXPERTS - 1) * WALL], F32R))
        xn = sb("xn", [P, HALVES, 2 * CA], ctx=middle)
        XH = sb("XH", [P, 2, 2, PIX], F32R, middle)
        XL = sb("XL", [P, 2, 2, PIX], F32R, middle)
        UH = sb("UH", [P, 2, 2, PIX], F32R, middle)
        uAl = sb("uAl", [P, 2, PIX], F32R, middle)
        V = sb("V", [P, 2, HALVES, C], ctx=middle)
        sc_sb = sb("scores_sb", [P, 3 * P], ctx=middle)
        Pr = sb("probs", [P, 3 * P], ctx=middle)
        PT = sb("probs_t", [P, 3 * P], ctx=middle)
        xn2 = sb("xn2", [P, HALVES, C], ctx=middle)
        x2T = sb("x2T", [P, 2, PIX], ctx=middle)
        tstat = sb("tstat", [P, TILES, 6], ctx=middle)
        ln1 = sb("ln1", [P, TILES, 2], ctx=middle)
        ln2 = sb("ln2", [P, HALVES, 2], ctx=middle)
        newt = sb("newt", [P, 2, TILES], ctx=middle)
        smx = sb("smx", [P, 2], ctx=middle)
        nmx = sb("nmx", [P, 2], ctx=middle)
        ssum = sb("ssum", [P, 2], ctx=middle)
        lg = sb("lg", [P, 2, EXPERTS], ctx=middle)
        gmx = sb("gmx", [P, 2], ctx=middle)
        oh = sb("oh", [P, 2, EXPERTS], BF16, middle)
        pos = sb("pos", [P, 2], ctx=middle)
        middle.close()

        wall = sb("wall", [P, EXPERTS, WALL], F32R)
        xf = sb("xf", [P, 2 * CA])
        FH = sb("FH", [P, 2, 2, P], F32R)
        FL = sb("FL", [P, 2, 2, P], F32R)
        gh = sb("gh", [P, 2, FT * P])
        HH = sb("HH", [P, 2, FT, P], F32R)
        HL = sb("HL", [P, 2, FT, P], F32R)
        yo = sb("yo", [P, 2, C])
        tiles_i = sb("tiles_i", [P, EXPERTS], I32)
        tiles_f = sb("tiles_f", [P, EXPERTS])
        ends = sb("ends", [P, 2, EXPERTS])
        started = sb("started", [P, SLOTS, EXPERTS])
        picked = sb("picked", [P, SLOTS, EXPERTS])
        per_slot = sb("per_slot", [P, 4, SLOTS])
        slot_expert = sb("slot_expert", [P, SLOTS], I32)
        slot_row = sb("slot_row", [P, SLOTS], I32)

        pieces = []
        for k in range(PAIRS):
            q0 = PAIR * k - PAD_PIX
            for h in range(HALVES):
                a, z = max(q0, P * h), min(q0 + P, P * (h + 1))
                if a < z:
                    c0 = PAIR * k - (PIX - NEAR) * h
                    pieces.append((k, h, slice(a - P * h, z - P * h), slice(a - q0, z - q0), slice(c0, c0 + PAIR)))

        def c1(name):
            return s1[:, S1[name][0]:S1[name][1]]

        small1_in, small2_in, tm_in, rbk_in = sem("small1_in"), sem("small2_in"), sem("tm_in"), sem("rbk_in")
        cm_in = [sem("cm_in0"), sem("cm_in1")]
        stage_in = [sem("stage_in0"), sem("stage_in1")]
        stage_hi, stage_free = sem("stage_hi"), sem("stage_free")
        empty_out = sem("empty_out")
        corr_out = [sem("corr_out0"), sem("corr_out1")]
        corr_added = [sem(f"corr_added{q}") for q in range(4)]
        out_done = sem("out_done")
        dve, act = sem("dve_step"), sem("act_step")
        prep_ready, m_ready, m_split, wsplit_hi, small_split = sem("prep_ready"), sem("m_ready"), sem("m_split"), sem("wsplit_hi"), sem("small_split")
        gstat_in, gstat_ready, gvar_ready, gstd_ready, gnorm_ready = sem("gstat_in"), sem("gstat_ready"), sem("gvar_ready"), sem("gstd_ready"), sem("gnorm_ready")
        f_ready, fh_ready, fl_ready, fq_ready = sem("f_ready"), sem("fh_ready"), sem("fl_ready"), sem("fq_ready")
        conv_ready, conv_taken, gram_ready, gram_taken = sem("conv_ready"), sem("conv_taken"), sem("gram_ready"), sem("gram_taken")
        ssq_ready, nrm_ready, rn_ready, cc_ready, rwin_ready, rt_ready, rt_copied = sem("ssq_ready"), sem("nrm_ready"), sem("rn_ready"), sem("cc_ready"), sem("rwin_ready"), sem("rt_ready"), sem("rt_copied")
        gs_ready, gsh_ready, gsl_ready, class_ready, co_ready = sem("gs_ready"), sem("gsh_ready"), sem("gsl_ready"), sem("class_ready"), sem("co_ready")
        center_added = sem("center_added")
        iota_done = sem("iota_done")
        empty_ready = sem("empty_ready")
        (xn_ready, xt_ready, xh_ready, xl_ready, u_ready, uh_ready, ul_ready, v_ready, v_copied, s_ready, max_ready,
         exp_ready, pt_ready, pt_copied, o_ready, t2_ready, xn2_ready, t2t_ready, x2_copied, g_ready, oh_ready, pf_ready,
         pos_ready, dve2, wall_hi, wall_lo, wall_dve) = (sem(n) for n in (
             "xn_ready", "xt_ready", "xh_ready", "xl_ready", "u_ready", "uh_ready", "ul_ready", "v_ready", "v_copied",
             "s_ready", "max_ready", "exp_ready", "pt_ready", "pt_copied", "o_ready", "t2_ready", "xn2_ready", "t2t_ready",
             "x2_copied", "g_ready", "oh_ready", "pf_ready", "pos_ready", "dve2", "wall_hi", "wall_lo", "wall_dve"))
        gram_half, diag_read, zeroed, held, wall_q = sem("gram_half"), sem("diag_read"), sem("zeroed"), sem("held"), sem("wall_q")
        windows_in = [sem("windows_in0"), sem("windows_in1")]
        scattered, table_ready = sem("scattered"), sem("table_ready")
        slot_in = [sem("slot_in0"), sem("slot_in1")]
        out_sent = [sem("out_sent0"), sem("out_sent1")]
        (fx_ready, fxt_ready, fh2_ready, fl2_ready, h_ready, silu_ready, gh_ready, gt_ready, hh_ready, hl_ready, y_ready,
         y_taken, yo_free, dve3) = (sem(n) for n in ("fx_ready", "fxt_ready", "fh2_ready", "fl2_ready", "h_ready", "silu_ready", "gh_ready",
                                            "gt_ready", "hh_ready", "hl_ready", "y_ready", "y_taken", "yo_free", "dve3"))

        block = top.enter_context(nc.Block())

        @block.sync
        def _(sp):
            sp.dma_start(s1[:], small1).then_inc(small1_in, 16)
            n2 = IMAGES // 2
            for h in range(2):
                sp.dma_start(xcm[:, n2 * h:n2 * (h + 1)].rearrange("p b t x -> p b (t x)"),
                             x_cm[n2 * h:n2 * (h + 1)].rearrange("b p x -> p b x")).then_inc(cm_in[h], 16)
            sp.dma_start(rows[:, 0:TILES, 0:C], x_tm).then_inc(tm_in, 16)
            sp.dma_start(s2[:], small2).then_inc(small2_in, 16)
            for n in range(CHUNKS):
                if n >= 2:
                    sp.wait_ge(stage_free, n - 1)
                sp.dma_start(stage[:, n % 2, 0:BAND_CHUNK], band[:, BAND_CHUNK * n:BAND_CHUNK * (n + 1)]).then_inc(stage_in[n % 2], 16)
            sp.wait_ge(empty_ready, 1)
            for e in range(EXPERTS + 1):
                sp.dma_start(xs[REGION * e:REGION * e + P, :], emptyt[:]).then_inc(empty_out, 16)
            sp.wait_ge(zeroed, 1)
            n2 = IMAGES // 2
            for half in range(2):
                sp.wait_ge(gram_taken, n2 * (half + 1) + AHEAD)
                b4 = slice(n2 * half, n2 * (half + 1))
                for k, h, src, dst, cols in pieces:
                    sp.dma_start(around[dst, b4, k], gram[src, b4, h, cols]).then_inc(windows_in[half], 16)
            sp.wait_ge(rt_copied, 1)
            for k in range(P // PAIR):
                sp.dma_start(rbk[k:WINDOWS:P // PAIR, :], rT[:, PAIR * k:PAIR * (k + 1)]).then_inc(rbk_in, 16)
            for c in range(CHUNKS):
                sp.wait_ge(co_ready, c + 1)
                sp.dma_start(corr.rearrange("(w p) c -> w p c", p=PAIR)[:, CHUNK * c:CHUNK * (c + 1), :], co[:, c % 2]).then_inc(corr_out[c % 2], 16)
            for e in range(EXPERTS):
                n = CHUNKS + e
                if e < 2:
                    sp.wait_ge(stage_free, n - 1)
                else:
                    sp.wait_ge(wall_lo, e - 1)
                    sp.wait_ge(wall_q, e - 1)
                sp.dma_start(stage[:, n % 2], w_all[e]).then_inc(stage_in[n % 2], 16)
            sp.wait_ge(scattered, 16 * TILES)
            sp.wait_ge(empty_out, 16 * (EXPERTS + 1))
            sp.wait_ge(table_ready, 1)

            def load_slot(j, par, k):
                if k is not None:
                    sp.wait_ge(slot_in[par], 16 * k)
                sp.wait_ge(table_ready, 1)
                off = sp.value_load(slot_row[0:1, bass.ds(j, 1)], min_val=0, max_val=EMPTY)
                sp.dma_start(rows[:, bass.ds(j, 1), :].rearrange("p a c -> p (a c)"), xs[bass.ds(off, P), :]).then_inc(slot_in[par], 16)

            for j in range(2):
                load_slot(j, j, None)
            with sp.Fori(1, SLOTS // 2) as i:
                for par in range(2):
                    load_slot(2 * i + par, par, i)
            load_slot(SLOTS - 1, (SLOTS - 1) % 2, (SLOTS - 1) // 2)
            for par in range(2):
                sp.wait_ge(out_sent[par], 16 * ((SLOTS + 1 - par) // 2))

        @block.gpsimd
        def _(pool):
            nc.gpsimd.memset(emptyt[:], 0.0).then_inc(iota_done, 1)
            pool.wait_ge(iota_done, 1)
            nc.gpsimd.iota(emptyt[:, C + 2:C + 3].bitcast(I32), pattern=[[0, 1]], base=NO_TOKEN, channel_multiplier=0).then_inc(empty_ready, 1)
            nc.gpsimd.iota(rows[:, 0:TILES, C + 2].bitcast(I32), pattern=[[P, TILES]], base=0, channel_multiplier=1).then_inc(iota_done, 1)
            nc.gpsimd.memset(rows[:, 0:TILES, C + 3], 0.0).then_inc(iota_done, 1)
            nc.gpsimd.memset(around[:].rearrange("q b k c -> q (b k c)"), 0.0).then_inc(zeroed, 1)
            with pool.Fori(0, CHUNKS) as i:
                pool.wait_ge(stage_hi, i + 1)
                pool.wait_ge(tm_in, 16)
                at = bass.ds(i * BAND_CHUNK, BAND_CHUNK)
                nc.gpsimd.tensor_tensor(bandL[:, at], stage[:, bass.ds(i % 2, 1), 0:BAND_CHUNK].rearrange("p a b -> p (a b)"),
                                        bandH[:, at].bitcast(F32), ALU.subtract).then_inc(stage_free, 1)
            for s in corr_out:
                pool.wait_ge(s, 16 * (CHUNKS // 2))
            pool.wait_ge(center_added, 1)
            tok = corr.rearrange("(j p) c -> p j c", p=P)
            for q in range(4):
                n4 = TILES // 4
                pool.dma_start(rows[:, n4 * q:n4 * (q + 1), 0:C], tok[:, n4 * q:n4 * (q + 1), :], accum_op=ALU.add).then_inc(corr_added[q], 16)

            for s in corr_added:
                pool.wait_ge(s, 16)
            pool.wait_ge(empty_out, 16 * (EXPERTS + 1))

            def scatter_tokens(b):
                pool.wait_ge(pos_ready, b + 1 + AHEAD)
                for h in range(HALVES):
                    j = 2 * b + h
                    pool.indirect_dma_start(out=xs, out_offset=bass.IndirectOffsetOnAxis(ap=posi[:, j:j + 1].bitcast(U32), axis=0),
                                            in_=rows[:, j], in_offset=None,
                                            bounds_check=EMPTY - 1, oob_is_err=False).then_inc(scattered, 16)

            def weights_lo(e, par):
                pool.wait_ge(wall_hi, e + 1)
                pool.wait_ge(tm_in, 16)
                w = wall[:, e]
                nc.gpsimd.tensor_tensor(w[:, W12:2 * W12], stage[:, par, 0:W12], w[:, 0:W12].bitcast(F32), ALU.subtract)
                w3 = w[:, 3 * W12:WALL].rearrange("p (k s c) -> p k s c", s=2, c=C)
                nc.gpsimd.tensor_tensor(w3[:, :, 1], stage[:, par, 2 * W12:STAGE].rearrange("p (k c) -> p k c", c=C),
                                        w3[:, :, 0].bitcast(F32), ALU.subtract).then_inc(wall_lo, 1)

            for t in range(1, IMAGES + 2):
                if t < EXPERTS:
                    weights_lo(t - 1, 1 - t % 2)
                if t >= 2:
                    scatter_tokens(t - 2)
            pool.sem_inc(yo_free, AHEAD)

            def send_slot(j, par):
                if j:
                    pool.wait_ge(out_sent[1 - par], 16 * ((j + 1) // 2))
                    pool.sem_inc(yo_free, 1)
                pool.wait_ge(y_taken, j + 1 + AHEAD)
                pool.wait_ge(tm_in, 16)
                pool.indirect_dma_start(out=out, out_offset=bass.IndirectOffsetOnAxis(ap=rows[:, j, C + 2:C + 3].bitcast(U32), axis=0),
                                        in_=yo[:, par], in_offset=None, bounds_check=TILES * P - 1, oob_is_err=False).then_inc(out_sent[par], 16)

            for j in range(SLOTS):
                send_slot(j, j % 2)

        @block.scalar
        def _(sc):
            sc.wait_ge(m_ready, 1)
            nc.scalar.activation(mH[:], bank[4][:], ACT.Copy).then_inc(m_split, 1)
            sc.wait_ge(small1_in, 16)
            nc.scalar.activation(cfH[:], c1("cf"), ACT.Copy).then_inc(wsplit_hi, 1)
            nc.scalar.activation(vwH[:], c1("wv"), ACT.Copy).then_inc(wsplit_hi, 1)
            sc.wait_ge(prep_ready, 1)
            for h in range(2):
                sc.wait_ge(gvar_ready, h + 1)
                nc.scalar.activation(grs[:, h], gvar[:, h], ACT.Sqrt, bias=eps_c[:, 0:1]).then_inc(gstd_ready, 1)
            sc.sem_inc(f_ready, AHEAD)

            def norm_image(b, par):
                half, at = (b // (IMAGES // 2), b % (IMAGES // 2))
                for t in range(2):
                    ins = nc.scalar.activation(f32t[:, par, t], xcm[:, bass.ds(b, 1), t, :].rearrange("p a x -> p (a x)"),
                                               ACT.Identity, scale=grs[:, bass.ds(half, 1), t, bass.ds(at, 1)].rearrange("p a b -> p (a b)"),
                                               bias=gnb[:, bass.ds(half, 1), t, bass.ds(at, 1)].rearrange("p a b -> p (a b)"))
                ins.then_inc(f_ready, 1)

            sc.wait_ge(gnorm_ready, 2)
            for b in range(2):
                norm_image(b, b)

            def band_hi(n, par):
                nc.scalar.activation(bandH[:, bass.ds(n * BAND_CHUNK, BAND_CHUNK)], stage[:, par, 0:BAND_CHUNK], ACT.Copy).then_inc(stage_hi, 1)

            for i in range(IMAGES // 2 - 1):
                for par in range(2):
                    sc.wait_ge(fl_ready, 2 * i + par + 1 + AHEAD)
                    norm_image(2 * i + 2 + par, par)
                sc.wait_ge(stage_in[i % 2], 16 * (i // 2 + 1))
                band_hi(i, i % 2)
            i = CHUNKS - 1
            sc.wait_ge(stage_in[i % 2], 16 * (i // 2 + 1))
            band_hi(i, i % 2)
            sc.wait_ge(ssq_ready, 1)
            nc.scalar.activation(rn[:], ssq[:], ACT.Sqrt).then_inc(nrm_ready, 1)
            for c in range(CHUNKS):
                sc.wait_ge(gs_ready, c + 1)
                if c >= 2:
                    sc.wait_ge(class_ready, c - 1)
                nc.scalar.activation(gsH[:, c % 2], gs[:, c % 2], ACT.Copy).then_inc(gsh_ready, 1)

            for s in corr_added:
                sc.wait_ge(s, 16)
            sc.wait_ge(empty_out, 16 * (EXPERTS + 1))
            for s in (xh_ready, exp_ready, x2_copied, uh_ready, pt_copied, v_copied):
                sc.sem_inc(s, AHEAD)

            def weights_hi(e, par, loaded):
                sc.wait_ge(stage_in[par], 16 * loaded)
                sc.wait_ge(small1_in, 16)
                w = wall[:, bass.ds(e, 1), :].rearrange("p a c -> p (a c)")
                nc.scalar.activation(w[:, 0:W12], stage[:, par, 0:W12], ACT.Copy)
                nc.scalar.activation(w[:, 2 * W12:3 * W12], stage[:, par, W12:2 * W12], ACT.Copy)
                w3 = w[:, 3 * W12:WALL].rearrange("p (k s c) -> p k s c", s=2, c=C)
                nc.scalar.activation(w3[:, :, 0], stage[:, par, 2 * W12:STAGE].rearrange("p (k c) -> p k c", c=C), ACT.Copy).then_inc(wall_hi, 1)

            def step(t, par, front, mid, back, loaded):
                if front:
                    sc.wait_ge(xt_ready, t + 1 + AHEAD)
                    nc.scalar.activation(XH[:, par].rearrange("p t x -> p (t x)"), bank[0][:], ACT.Copy).then_inc(xh_ready, 1)
                if mid:
                    sc.wait_ge(max_ready, t + AHEAD)
                    nc.scalar.activation(Pr[:, 0:P], sc_sb[:, 0:P], ACT.Exp, scale=SM_SCALE, bias=nmx[:, 0:1], accum_out=ssum[:, 0:1])
                    nc.scalar.activation(Pr[:, P:3 * P], sc_sb[:, P:3 * P], ACT.Exp, scale=SM_SCALE, bias=nmx[:, 1:2],
                                         accum_out=ssum[:, 1:2]).then_inc(exp_ready, 1)
                if back:
                    sc.wait_ge(t2t_ready, t - 1 + AHEAD)
                    nc.scalar.activation(x2T[:].rearrange("p t x -> p (t x)"), bank[6][:], ACT.Copy).then_inc(x2_copied, 1)
                if front:
                    sc.wait_ge(u_ready, t + 1 + AHEAD)
                    nc.scalar.activation(UH[:, par].rearrange("p t x -> p (t x)"), bank[1][:], ACT.Copy).then_inc(uh_ready, 1)
                if mid:
                    sc.wait_ge(pt_ready, t + AHEAD)
                    nc.scalar.activation(PT[:], bank[4][:, 0:3 * P], ACT.Copy).then_inc(pt_copied, 1)
                if front:
                    sc.wait_ge(v_ready, t + 1 + AHEAD)
                    nc.scalar.activation(V[:, par].rearrange("p h c -> p (h c)"), bank[2][:, 0:HALVES * C], ACT.Copy).then_inc(v_copied, 1)
                if loaded is not None:
                    weights_hi(t - 1, 1 - par, loaded)

            step(0, 0, True, False, False, None)
            step(1, 1, True, True, False, 3)
            with sc.Fori(1, IMAGES // 2) as i:
                for par in range(2):
                    step(2 * i + par, par, True, True, True, i + 2 + par)
            step(IMAGES, 0, False, True, True, None)
            step(IMAGES + 1, 1, False, False, True, None)
            sc.wait_ge(pos_ready, IMAGES + AHEAD)
            weights_hi(EXPERTS - 1, (CHUNKS + EXPERTS - 1) % 2, (CHUNKS + EXPERTS) // 2)
            for s in (hh_ready, silu_ready, fh2_ready):
                sc.sem_inc(s, AHEAD)

            def ffn_step(j, par, back, mid, nxt):
                if back:
                    sc.wait_ge(gt_ready, j + AHEAD)
                    nc.scalar.activation(HH[:, 1 - par].rearrange("p k x -> p (k x)"), bank[5][:], ACT.Copy).then_inc(hh_ready, 1)
                if mid:
                    sc.wait_ge(h_ready, j + 1 + AHEAD)
                    nc.scalar.activation(gh[:, par, 0:FE], bank[1 + 2 * par][:, 0:FE], ACT.Silu).then_inc(silu_ready, 1)
                if nxt:
                    sc.wait_ge(fxt_ready, j + 2 + AHEAD)
                    nc.scalar.activation(FH[:, 1 - par].rearrange("p t x -> p (t x)"), bank[0][:, 0:2 * P], ACT.Copy).then_inc(fh2_ready, 1)

            ffn_step(-1, 1, False, False, True)
            ffn_step(0, 0, False, True, True)
            ffn_step(1, 1, True, True, True)
            with sc.Fori(1, SLOTS // 2) as i:
                for par in range(2):
                    ffn_step(2 * i + par, par, True, True, True)
            ffn_step(SLOTS - 1, 0, True, True, False)
            ffn_step(SLOTS, 1, True, False, False)

        @block.vector
        def _(ve):
            steps = [0]

            def link(ins):
                steps[0] += 1
                ins.then_inc(dve, 1)
                ve.wait_ge(dve, steps[0])

            nc.vector.memset(ones2[:].bitcast(F32), 1.0)
            nc.vector.memset(eps_c[:], EPS).then_inc(prep_ready, 1)
            link(nc.vector.memset(bias2[:].bitcast(F32), 0.0))
            ve.wait_ge(small1_in, 16)
            r4 = c1("rows").rearrange("p (r c) -> p r c", r=4)
            link(nc.vector.tensor_copy(bias2[0:1, :], r4[0:1, 0]))
            link(nc.vector.tensor_copy(bias2[32:33, :], r4[32:33, 0]))
            link(nc.vector.tensor_tensor(bias2[32:33, :], r4[32:33, 0], bias2[32:33, :].bitcast(F32), ALU.subtract))
            link(nc.vector.tensor_tensor(wsum[:], r4[:, 1], r4[:, 2], ALU.add))
            link(nc.vector.tensor_tensor(wsum[:], wsum[:], r4[:, 3], ALU.add))
            ve.wait_ge(m_split, 1)
            nc.vector.tensor_tensor(mL[:], bank[4][:, 0:2 * CA], mH[:, 0:2 * CA].bitcast(F32), ALU.subtract)
            nc.vector.tensor_tensor(mH[CB:P, 2 * CA:4 * CA], bank[4][CB:P, 2 * CA:4 * CA], mH[CB:P, 2 * CA:4 * CA].bitcast(F32), ALU.subtract)
            ve.wait_ge(wsplit_hi, 2)
            for hi, lo, raw in ((cfH, cfL, c1("cf")), (vwH, vwL, c1("wv"))):
                nc.vector.tensor_tensor(lo[:], raw[:, 0:C], hi[:, 0:C].bitcast(F32), ALU.subtract)
                last = nc.vector.tensor_tensor(hi[CB:P, C:2 * C], raw[CB:P, C:2 * C], hi[CB:P, C:2 * C].bitcast(F32), ALU.subtract)
            last.then_inc(small_split, 1)

            n2 = IMAGES // 2
            for h in range(2):
                at = slice(n2 * h, n2 * (h + 1))
                ve.wait_ge(cm_in[h], 16)
                for b in range(n2 * h, n2 * (h + 1)):
                    for t in range(2):
                        ins = nc.vector.bn_stats(gst[:, b, t], xcm[:, b, t])
                link(ins)
                st = gst[:, at].rearrange("p b t (e k) -> p (b t) e k", k=3)
                m = mq[:, at].rearrange("p b t e k -> p (b t) e k")
                s = msq[:, at].rearrange("p b t e -> p (b t) e")
                nc.vector.tensor_copy(m[:, :, :, 0], st[:, :, :, 1])
                link(nc.vector.tensor_tensor(s, st[:, :, :, 1], st[:, :, :, 1], ALU.mult))
                nc.vector.scalar_tensor_tensor(out=m[:, :, :, 1], in0=st[:, :, :, 2], scalar=2.0 / PIX, in1=s,
                                               op0=ALU.mult, op1=ALU.add).then_inc(gstat_in, 1)
                ve.wait_ge(gstat_ready, h + 1)
                link(nc.vector.tensor_copy(mv[:, h].rearrange("p t b k -> p (t b k)"), bank[7][:, 0:4 * n2]))
                link(nc.vector.tensor_tensor(gvar[:, h], mv[:, h, :, :, 0], mv[:, h, :, :, 0], ALU.mult))
                nc.vector.tensor_tensor(gvar[:, h], mv[:, h, :, :, 1], gvar[:, h], ALU.subtract).then_inc(gvar_ready, 1)
                ve.wait_ge(gstd_ready, h + 1)
                link(nc.vector.reciprocal(grs[:, h], grs[:, h]))
                nc.vector.scalar_tensor_tensor(out=gnb[:, h], in0=mv[:, h, :, :, 0], scalar=-1.0, in1=grs[:, h],
                                               op0=ALU.mult, op1=ALU.mult).then_inc(gnorm_ready, 1)
            for s in (fh_ready, fl_ready, fq_ready, conv_taken, gram_taken):
                ve.sem_inc(s, AHEAD)
            def split_image(b, par):
                ve.wait_ge(f_ready, b + 1 + AHEAD)
                ve.wait_ge(gram_ready, b - 1 + AHEAD)
                nc.vector.tensor_copy(f2[:, par, :, 0], f32t[:, par]).then_inc(fh_ready, 1)
                ve.wait_ge(fh_ready, b + 1 + AHEAD)
                nc.vector.tensor_tensor(f2[:, par, :, 1], f32t[:, par], f2[:, par, :, 0].bitcast(F32), ALU.subtract).then_inc(fl_ready, 1)
                nc.vector.tensor_copy(fQ[0:CB, par], f2[0:CB, par, 1, 0].bitcast(F32))
                ve.wait_ge(fl_ready, b + 1 + AHEAD)
                nc.vector.tensor_copy(fQ[CB:P, par], f2[CB:P, par, 1, 1].bitcast(F32)).then_inc(fq_ready, 1)

            def take_conv(b, par):
                ve.wait_ge(conv_ready, b + 1 + AHEAD)
                dst = rows[:, bass.ds(b * HALVES, HALVES), 0:C]
                ve.wait_ge(tm_in, 16)
                nc.vector.tensor_tensor(dst, bank[par][:, 0:HALVES * C].rearrange("p (h c) -> p h c", c=C), dst, ALU.add).then_inc(conv_taken, 1)

            def take_gram(b, par):
                ve.wait_ge(gram_ready, b + 1 + AHEAD)
                for h in range(HALVES):
                    g = bank[2 + 2 * par + h]
                    nc.vector.tensor_copy(gram[:, b, h], g[:, 0:NEAR]).then_inc(gram_half, 1)
                    ve.wait_ge(gram_half, 2 * b + h + 1)
                    ins = nc.vector.tensor_tensor(gram[:, b, h], gram[:, b, h], g[:, NEAR:2 * NEAR], ALU.add)
                ins.then_inc(gram_taken, 1)
                ve.wait_ge(gram_taken, b + 1 + AHEAD)
                ve.wait_ge(small2_in, 16)
                for h in range(HALVES):
                    at = h * (NEAR - P)
                    ins = nc.vector.tensor_tensor_reduce(out=gs[:, 0, 0:P], in0=gram[:, b, h, at:at + P], in1=ident, scale=1.0, scalar=0.0,
                                                         op0=ALU.mult, op1=ALU.add, accum_out=ssq[:, 2 * b + h:2 * b + h + 1])
                    ins.then_inc(diag_read, 1)
                    ve.wait_ge(diag_read, 2 * b + h + 1)

            for b in range(2):
                split_image(b, b)
            for i in range(IMAGES // 2 - 1):
                for par in range(2):
                    take_conv(2 * i + par, par)
                    split_image(2 * i + 2 + par, par)
                    take_gram(2 * i + par, par)
            for b in (IMAGES - 2, IMAGES - 1):
                take_conv(b, b % 2)
                take_gram(b, b % 2)

            ve.sem_inc(ssq_ready, 1)
            ve.wait_ge(nrm_ready, 1)
            link(nc.vector.tensor_scalar(rn[:], rn[:], EPS_NORM, None, ALU.max))
            nc.vector.reciprocal(rn[:], rn[:]).then_inc(rn_ready, 1)
            ve.wait_ge(rn_ready, 1)
            link(nc.vector.tensor_tensor(cc[:], ssq[:], rn[:], ALU.mult))
            nc.vector.tensor_tensor(cc[:], cc[:], rn[:], ALU.mult).then_inc(cc_ready, 1)
            ve.wait_ge(rt_ready, 1)
            nc.vector.tensor_copy(rT[:], bank[7][0:TILES, 0:P]).then_inc(rt_copied, 1)
            ve.wait_ge(rwin_ready, 1)
            link(nc.vector.tensor_copy(rwin[:].rearrange("q b k -> q k b"), bank[5][:, 0:WINDOWS].rearrange("q (k b) -> q k b", b=IMAGES)))

            def scale_gram(c):
                if c >= 2:
                    ve.wait_ge(gsl_ready, c - 1)
                nc.vector.tensor_tensor(gs[:, c % 2].rearrange("q (c w) -> q w c", w=WINDOWS),
                                        around[:].rearrange("q b k c -> q (b k) c")[:, :, CHUNK * c:CHUNK * (c + 1)],
                                        rwin[:].rearrange("q b k -> q (b k)").rearrange("q (w a) -> q w a", a=1).to_broadcast([P, WINDOWS, CHUNK]),
                                        ALU.mult).then_inc(gs_ready, 1)
                ve.wait_ge(gsh_ready, c + 1)
                nc.vector.tensor_tensor(gsL[:, c % 2], gs[:, c % 2], gsH[:, c % 2].bitcast(F32), ALU.subtract).then_inc(gsl_ready, 1)

            def take_class(c):
                ve.wait_ge(class_ready, c + 1)
                if c >= 2:
                    ve.wait_ge(corr_out[c % 2], 16 * (c // 2))
                for q in range(CHUNK // 2):
                    a = CHUNK * c + 2 * q
                    ins = nc.vector.tensor_tensor(co[:, c % 2, 2 * q:2 * q + 2], bank[4 * (c % 2) + q][0:WINDOWS, 0:2 * C].rearrange("w (a c) -> w a c", a=2),
                                                  rbk[:, a:a + 2].rearrange("w (a c) -> w a c", c=1).to_broadcast([WINDOWS, 2, C]), ALU.mult)
                ins.then_inc(co_ready, 1)

            ve.wait_ge(cc_ready, 1)
            for s in windows_in:
                ve.wait_ge(s, 16 * len(pieces))
            scale_gram(0)
            ve.wait_ge(rbk_in, 16 * (P // PAIR))
            for c in range(CHUNKS):
                if c + 1 < CHUNKS:
                    scale_gram(c + 1)
                take_class(c)
                for j in range(4 * c, 4 * c + 4):
                    ins = nc.vector.scalar_tensor_tensor(out=rows[:, j, 0:C], in0=wsum[:], scalar=cc[:, j:j + 1], in1=rows[:, j, 0:C],
                                                         op0=ALU.mult, op1=ALU.add)
            ins.then_inc(center_added, 1)

            ve.wait_ge(corr_added[0], 16)
            ve.wait_ge(empty_out, 16 * (EXPERTS + 1))
            for s in (xn_ready, xn2_ready, xl_ready, max_ready, ul_ready, oh_ready, t2_ready, pos_ready):
                ve.sem_inc(s, AHEAD)
            ve.wait_ge(small2_in, 16)
            nc.vector.tensor_copy(tri_sb[:], c2("tri"))
            nc.vector.tensor_copy(run[:], c2("base"))

            LINKS = 26

            def hold():
                ve.sem_inc(held, 1)


            def rsqrt(link, x, y, t):
                link(nc.vector.tensor_scalar(x, x, EPS, None, ALU.add))
                link(nc.vector.tensor_scalar(y.bitcast(I32), x.bitcast(I32), 1, None, ALU.logical_shift_right))
                link(nc.vector.tensor_scalar(y.bitcast(I32), y.bitcast(I32), -1.0, GUESS, ALU.mult, ALU.add))
                for _ in range(3):
                    link(nc.vector.tensor_tensor(t, y, y, ALU.mult))
                    link(nc.vector.scalar_tensor_tensor(out=t, in0=t, scalar=-0.5, in1=x, op0=ALU.mult, op1=ALU.mult))
                    last = nc.vector.scalar_tensor_tensor(out=y, in0=t, scalar=1.5, in1=y, op0=ALU.add, op1=ALU.mult)
                    if _ < 2:
                        link(last)
                return last

            for q in range(4):
                ve.wait_ge(corr_added[q], 16)
                for j in range(TILES // 4 * q, TILES // 4 * (q + 1)):
                    ins = nc.vector.bn_stats(tstat[:, j], rows[:, j, 0:C])
            link(ins)
            for j in range(TILES):
                ins = nc.vector.bn_aggr(ln1[:, j], tstat[:, j])
            link(ins)
            link(nc.vector.tensor_copy(newt[:, 0], ln1[:, :, 1]))
            link(rsqrt(link, newt[:, 0], ln1[:, :, 1], newt[:, 1]))

            def step(t, par, front, mid, back, nxt, weights=True):
                done = [0]

                def link(ins):
                    done[0] += 1
                    ins.then_inc(dve2, 1)
                    ve.wait_ge(dve2, LINKS * t + (LINKS + done[0]))

                def normed(to, src, mean, rs, twice):
                    ins = nc.vector.tensor_scalar(to[:, 0:C], src, mean, rs, ALU.subtract, ALU.mult)
                    if twice:
                        ins = nc.vector.tensor_scalar(to[:, C:2 * CA], src[:, CA:C], mean, rs, ALU.subtract, ALU.mult)
                    return ins

                if front:
                    ve.wait_ge(xh_ready, t + 1 + AHEAD)
                    nc.vector.tensor_tensor(XL[:, par].rearrange("p t x -> p (t x)"), bank[0][:],
                                            XH[:, par].rearrange("p t x -> p (t x)").bitcast(F32), ALU.subtract).then_inc(xl_ready, 1)
                if mid:
                    ve.wait_ge(s_ready, t + AHEAD)
                    hold()
                    nc.vector.tensor_tensor_reduce(out=sc_sb[:, 0:P], in0=bank[3][:, 0:P], in1=c2("mask")[:, 0:P], scale=1.0, scalar=NEG,
                                                   op0=ALU.add, op1=ALU.max, accum_out=smx[:, 0:1])
                    link(nc.vector.tensor_tensor_reduce(out=sc_sb[:, P:3 * P], in0=bank[3][:, P:3 * P], in1=c2("mask")[:, P:3 * P], scale=1.0,
                                                        scalar=NEG, op0=ALU.add, op1=ALU.max, accum_out=smx[:, 1:2]))
                    nc.vector.tensor_scalar(nmx[:], smx[:], -SM_SCALE, None, ALU.mult).then_inc(max_ready, 1)
                if front:
                    ve.wait_ge(uh_ready, t + 1 + AHEAD)
                    nc.vector.tensor_tensor(uAl[:, par], bank[1][:, 0:PIX], UH[:, par, 0].bitcast(F32), ALU.subtract)
                    nc.vector.tensor_tensor(UH[CB:P, par, 1], bank[1][CB:P, PIX:2 * PIX], UH[CB:P, par, 1].bitcast(F32), ALU.subtract).then_inc(ul_ready, 1)
                if nxt:
                    ve.wait_ge(xt_ready, t + 1 + AHEAD)
                    for h in range(HALVES):
                        j = 2 * t + (2 + h)
                        mean, rs = (ln1[:, bass.ds(j, 1), k:k + 1].rearrange("p a k -> p (a k)") for k in range(2))
                        ins = normed(xn[:, h], rows[:, bass.ds(j, 1), 0:C].rearrange("p a c -> p (a c)"), mean, rs, True)
                    ins.then_inc(xn_ready, 1)
                if back:
                    ve.wait_ge(g_ready, t - 1 + AHEAD)
                    desc = c2("desc").rearrange("p (h e) -> p h e", h=2)
                    wide = [P, 2, EXPERTS]
                    link(nc.vector.tensor_tensor(lg[:], bank[7][:, 0:2 * EXPERTS].rearrange("p (h e) -> p h e", h=2),
                                                 c2("bg").rearrange("p (h e) -> p h e", h=2), ALU.add))
                    link(nc.vector.tensor_reduce(gmx[:], lg[:], AX_X, ALU.max))
                    link(nc.vector.tensor_tensor(lg[:], lg[:], gmx[:].rearrange("p (h a) -> p h a", a=1).to_broadcast(wide), ALU.is_ge))
                    link(nc.vector.tensor_tensor(lg[:], lg[:], desc, ALU.mult))
                    link(nc.vector.tensor_reduce(gmx[:], lg[:], AX_X, ALU.max))
                    nc.vector.tensor_tensor(oh[:], lg[:], gmx[:].rearrange("p (h a) -> p h a", a=1).to_broadcast(wide), ALU.is_equal).then_inc(oh_ready, 1)
                if mid:
                    ve.wait_ge(o_ready, t + AHEAD)
                    link(nc.vector.reciprocal(smx[:], ssum[:]))
                    for h in range(HALVES):
                        row = rows[:, bass.ds(2 * t + (h - 2), 1), 0:C].rearrange("p a c -> p (a c)")
                        ins = nc.vector.scalar_tensor_tensor(out=row, in0=bank[5][:, C * h:C * (h + 1)], scalar=smx[:, h:h + 1], in1=row,
                                                             op0=ALU.mult, op1=ALU.add)
                    link(ins)
                    hold()
                    for h in range(HALVES):
                        ins = nc.vector.bn_stats(tstat[:, h], rows[:, bass.ds(2 * t + (h - 2), 1), 0:C].rearrange("p a c -> p (a c)"))
                    link(ins)
                    hold()
                    for h in range(HALVES):
                        ins = nc.vector.bn_aggr(ln2[:, h], tstat[:, h])
                    link(ins)
                    link(nc.vector.tensor_copy(newt[:, 0, 0:2], ln2[:, :, 1]))
                    link(rsqrt(link, newt[:, 0, 0:2], ln2[:, :, 1], newt[:, 1, 0:2]))
                    hold()
                    nc.vector.tensor_copy(rows[:, bass.ds(2 * t - 2, 2), C:C + 2], ln2[:]).then_inc(t2_ready, 1)
                    ve.wait_ge(t2t_ready, t - 1 + AHEAD)
                    for h in range(HALVES):
                        ins = normed(xn2[:, h], rows[:, bass.ds(2 * t + (h - 2), 1), 0:C].rearrange("p a c -> p (a c)"),
                                     ln2[:, h, 0:1], ln2[:, h, 1:2], False)
                    ins.then_inc(xn2_ready, 1)
                if back:
                    ve.wait_ge(pf_ready, t - 1 + AHEAD)
                    r1 = run[:].rearrange("p (h e) -> p h e", h=1).to_broadcast(wide)
                    link(nc.vector.tensor_tensor(lg[:], bank[7][:, 2 * EXPERTS:4 * EXPERTS].rearrange("p (h e) -> p h e", h=2), r1, ALU.add))
                    link(nc.vector.tensor_tensor(lg[:], lg[:], oh[:], ALU.mult))
                    nc.vector.tensor_tensor(run[:], run[:], bank[7][:, 4 * EXPERTS:5 * EXPERTS], ALU.add)
                    link(nc.vector.tensor_reduce(pos[:], lg[:], AX_X, ALU.add))
                    hold()
                    nc.vector.tensor_copy(posi[:, bass.ds(2 * t - 4, 2)], pos[:]).then_inc(pos_ready, 1)
                if weights:
                    ve.wait_ge(wall_hi, t)
                    w = wall[CB:P, bass.ds(t - 1, 1), 2 * W12:3 * W12].rearrange("p a c -> p (a c)")
                    nc.vector.tensor_tensor(w, stage[CB:P, 1 - par, W12:2 * W12], w.bitcast(F32), ALU.subtract).then_inc(wall_q, 1)
                if done[0] < LINKS:
                    ve.sem_inc(dve2, LINKS - done[0])
                assert done[0] <= LINKS

            step(-1, 1, False, False, False, True, False)
            step(0, 0, True, False, False, True, False)
            step(1, 1, True, True, False, True)
            with ve.Fori(1, IMAGES // 2 - 1) as i:
                for par in range(2):
                    step(2 * i + par, par, True, True, True, True)
            step(IMAGES - 2, 0, True, True, True, True)
            step(IMAGES - 1, 1, True, True, True, False)
            step(IMAGES, 0, False, True, True, False, False)
            step(IMAGES + 1, 1, False, False, True, False, False)
            ve.wait_ge(pos_ready, IMAGES + AHEAD)
            link(nc.vector.tensor_tensor(tiles_f[:], run[:], c2("base"), ALU.subtract))
            link(nc.vector.tensor_scalar(tiles_f[:], tiles_f[:], float(P - 1), None, ALU.add))
            link(nc.vector.tensor_copy(tiles_i[:], tiles_f[:]))
            link(nc.vector.tensor_scalar(tiles_i[:], tiles_i[:], P.bit_length() - 1, None, ALU.logical_shift_right))
            link(nc.vector.tensor_copy(tiles_f[:], tiles_i[:]))
            link(nc.vector.tensor_copy(ends[:, 0], tiles_f[:]))
            for n, d in enumerate((1, 2, 4)):
                a, z = n % 2, 1 - n % 2
                nc.vector.tensor_copy(ends[:, z, 0:d], ends[:, a, 0:d])
                link(nc.vector.tensor_tensor(ends[:, z, d:EXPERTS], ends[:, a, d:EXPERTS], ends[:, a, 0:EXPERTS - d], ALU.add))
            starts = ends[:, 0]
            link(nc.vector.tensor_tensor(starts, ends[:, 1], tiles_f[:], ALU.subtract))
            wide = [P, SLOTS, EXPERTS]
            slot = c2("slot")[:, 0:SLOTS]
            slot3 = slot.rearrange("p (j a) -> p j a", a=1).to_broadcast(wide)

            def over_slots(v):
                return v.rearrange("p (a e) -> p a e", a=1).to_broadcast(wide)

            link(nc.vector.tensor_tensor(started[:], slot3, over_slots(starts), ALU.is_ge))
            nc.vector.tensor_reduce(per_slot[:, 0], started[:], AX_X, ALU.add)
            link(nc.vector.tensor_tensor(picked[:], started[:], over_slots(starts), ALU.mult))
            link(nc.vector.tensor_reduce(per_slot[:, 1], picked[:], AX_X, ALU.max))
            link(nc.vector.tensor_tensor(picked[:], started[:], over_slots(run[:]), ALU.mult))
            link(nc.vector.tensor_reduce(per_slot[:, 2], picked[:], AX_X, ALU.max))
            link(nc.vector.tensor_scalar(per_slot[:, 0], per_slot[:, 0], -1.0, None, ALU.add))
            nc.vector.tensor_copy(slot_expert[:], per_slot[:, 0])
            link(nc.vector.tensor_tensor(per_slot[:, 1], per_slot[:, 1], slot, ALU.subtract))
            link(nc.vector.tensor_scalar(per_slot[:, 1], per_slot[:, 1], -1.0, float(P), ALU.add, ALU.mult))
            link(nc.vector.tensor_tensor(per_slot[:, 2], per_slot[:, 2], per_slot[:, 1], ALU.add))
            link(nc.vector.tensor_scalar(per_slot[:, 3], slot, ends[:, 1, EXPERTS - 1:EXPERTS], 1e6, ALU.is_ge, ALU.mult))
            link(nc.vector.tensor_tensor(per_slot[:, 2], per_slot[:, 2], per_slot[:, 3], ALU.add))
            link(nc.vector.tensor_scalar(per_slot[:, 2], per_slot[:, 2], float(EMPTY), None, ALU.min))
            nc.vector.tensor_copy(slot_row[:], per_slot[:, 2]).then_inc(table_ready, 1)
            nc.vector.memset(gh[:, :, FE:FT * P], 0.0)
            ve.wait_ge(wall_hi, EXPERTS)
            raw, w = stage[:, (CHUNKS + EXPERTS - 1) % 2], wall[:, EXPERTS - 1]
            nc.vector.tensor_tensor(w[:, W12:2 * W12], raw[:, 0:W12], w[:, 0:W12].bitcast(F32), ALU.subtract)
            nc.vector.tensor_tensor(w[CB:P, 2 * W12:3 * W12], raw[CB:P, W12:2 * W12], w[CB:P, 2 * W12:3 * W12].bitcast(F32), ALU.subtract)
            w3 = w[:, 3 * W12:WALL].rearrange("p (k s c) -> p k s c", s=2, c=C)
            nc.vector.tensor_tensor(w3[:, :, 1], raw[:, 2 * W12:STAGE].rearrange("p (k c) -> p k c", c=C),
                                    w3[:, :, 0].bitcast(F32), ALU.subtract).then_inc(wall_dve, 1)
            for s in (fx_ready, fl2_ready, gh_ready, hl_ready, y_taken):
                ve.sem_inc(s, AHEAD)

            def norm_slot(j, par, loaded):
                ve.wait_ge(slot_in[par], 16 * loaded)
                ve.wait_ge(fxt_ready, j + AHEAD)
                row = rows[:, bass.ds(j, 1), :].rearrange("p a c -> p (a c)")
                mean, rs = row[:, C:C + 1], row[:, C + 1:C + 2]
                nc.vector.tensor_scalar(xf[:, 0:C], row[:, 0:C], mean, rs, ALU.subtract, ALU.mult)
                nc.vector.tensor_scalar(xf[:, C:2 * CA], row[:, CA:C], mean, rs, ALU.subtract, ALU.mult).then_inc(fx_ready, 1)

            def ffn_step(j, par, back, mid, nxt, after=None):
                if back:
                    ve.wait_ge(hh_ready, j + AHEAD)
                    nc.vector.tensor_tensor(HL[:, 1 - par].rearrange("p k x -> p (k x)"), bank[5][:],
                                            HH[:, 1 - par].rearrange("p k x -> p (k x)").bitcast(F32), ALU.subtract).then_inc(hl_ready, 1)
                if mid:
                    ve.wait_ge(silu_ready, j + 1 + AHEAD)
                    nc.vector.tensor_tensor(gh[:, par, 0:FE], gh[:, par, 0:FE], bank[2 + 2 * par][:, 0:FE], ALU.mult).then_inc(gh_ready, 1)
                if nxt:
                    ve.wait_ge(fh2_ready, j + 2 + AHEAD)
                    nc.vector.tensor_tensor(FL[:, 1 - par].rearrange("p t x -> p (t x)"), bank[0][:, 0:2 * P],
                                            FH[:, 1 - par].rearrange("p t x -> p (t x)").bitcast(F32), ALU.subtract).then_inc(fl2_ready, 1)
                if after is not None:
                    norm_slot(j + 2, par, after)
                if back:
                    y = bank[7 - par]
                    ve.wait_ge(y_ready, j + AHEAD)
                    ve.wait_ge(yo_free, j - 2 + AHEAD)
                    row = rows[:, bass.ds(j - 1, 1), 0:C].rearrange("p a c -> p (a c)")
                    nc.vector.tensor_tensor(yo[:, 1 - par], y[:, C:2 * C], row, ALU.add).then_inc(dve3, 1)
                    ve.wait_ge(dve3, j)
                    nc.vector.tensor_tensor(yo[:, 1 - par], yo[:, 1 - par], y[:, 0:C], ALU.add).then_inc(y_taken, 1)

            norm_slot(0, 0, 1)
            ffn_step(-1, 1, False, False, True, 1)
            ffn_step(0, 0, False, True, True, 2)
            ffn_step(1, 1, True, True, True, 2)
            with ve.Fori(1, SLOTS // 2 - 1) as i:
                for par in range(2):
                    ffn_step(2 * i + par, par, True, True, True, i + 2)
            ffn_step(SLOTS - 3, 0, True, True, True, SLOTS // 2 + 1)
            ffn_step(SLOTS - 2, 1, True, True, True)
            ffn_step(SLOTS - 1, 0, True, True, False)
            ffn_step(SLOTS, 1, True, False, False)

        @block.tensor
        def _(pe):
            pe.wait_ge(small1_in, 16)
            wq, wk = (c1(n).rearrange("p (t n) -> p t n", t=2) for n in ("wq", "wk"))
            for m in range(2):
                for t, k in ((0, P), (1, CB)):
                    mm = nc.tensor.matmul(bank[4][:, 2 * CA * m:2 * CA * (m + 1)], wq[0:k, t, CA * m:CA * (m + 1)], wk[0:k, t, :], start=(t == 0), stop=(t == 1))
            mm.then_inc(m_ready, 1)
            n2 = IMAGES // 2
            gm = c1("gm").rearrange("p (t n) -> p t n", t=2)
            for h in range(2):
                pe.wait_ge(gstat_in, h + 1)
                if h:
                    pe.wait_ge(gvar_ready, h)
                for m in range(2):
                    n = 0
                    for t, k in ((0, P), (1, CB)):
                        for eo in range(2):
                            mm = nc.tensor.matmul(bank[7][:, 2 * n2 * m:2 * n2 * (m + 1)], gm[0:k, t, CA * m:CA * (m + 1)],
                                                  mq[0:k, n2 * h:n2 * (h + 1), t, eo, :], start=(n == 0), stop=(n == 3))
                            n += 1
                mm.then_inc(gstat_ready, 1)

            for s in (conv_ready, gram_ready):
                pe.sem_inc(s, AHEAD)
            pe.wait_ge(small_split, 1)

            def products(dst, xh_a, xl_a, xh_b, xl_b, y_a, yl_a, y_q, y_q64, more=False):
                nc.tensor.matmul(dst, xh_a, y_a, start=True, stop=False)
                nc.tensor.matmul(dst, xh_a, yl_a, start=False, stop=False)
                nc.tensor.matmul(dst, xl_a, y_a, start=False, stop=False)
                nc.tensor.matmul(dst, xh_b, y_q, start=False, stop=False)
                return nc.tensor.matmul(dst, xl_b, y_q64, start=False, stop=not more)

            with pe.Fori(0, IMAGES // 2) as i:
                for par in range(2):
                    pe.wait_ge(fq_ready, 2 * i + (par + 1 + AHEAD))
                    pe.wait_ge(conv_taken, 2 * i + (par - 1 + AHEAD))
                    for h in range(HALVES):
                        t = slice(P * h, P * (h + 1))
                        dst = bank[par][:, C * h:C * (h + 1)]
                        products(dst, f2[:, par, 0, 0, t], f2[:, par, 0, 1, t], f2[:, par, 1, 0, t], f2[0:CB, par, 1, 1, t],
                                 cfH[:, 0:C], cfL[:, :], cfH[:, C:2 * C], cfH[0:CB, C:2 * C], more=True)
                        mm = nc.tensor.matmul(dst, ones2[:], bias2[:], start=False, stop=True)
                    mm.then_inc(conv_ready, 1)
                    pe.wait_ge(gram_taken, 2 * i + (par - 1 + AHEAD))
                    for h in range(HALVES):
                        q, p = slice(P * h, P * (h + 1)), slice((PIX - NEAR) * h, (PIX - NEAR) * h + NEAR)
                        dst = bank[2 + 2 * par + h][:, 0:2 * NEAR]
                        nc.tensor.matmul(dst, f2[:, par, 0, 0, q], f2[:, par, 0, :, p], start=True, stop=False)
                        nc.tensor.matmul(dst, f2[:, par, 0, 1, q], f2[:, par, 0, :, p], start=False, stop=False)
                        mm = nc.tensor.matmul(dst, fQ[:, par, q], f2[:, par, 1, :, p], start=False, stop=True)
                    mm.then_inc(gram_ready, 1)

            pe.wait_ge(rn_ready, 1)
            pe.wait_ge(small2_in, 16)
            nc.tensor.transpose(bank[7][0:TILES, 0:P], rn[:], ident).then_inc(rt_ready, 1)
            rnv = rn[:].rearrange("p (b h) -> p h b", h=HALVES)
            for k in range(PAIRS):
                for h in range(HALVES):
                    off = SHIFT0 - P * h + PAIR * k - PAD_PIX
                    mm = nc.tensor.matmul(bank[5][:, IMAGES * k:IMAGES * (k + 1)], c1("shift")[:, off:off + P], rnv[:, h], start=(h == 0), stop=(h == HALVES - 1))
            mm.then_inc(rwin_ready, 1)
            pe.wait_ge(stage_free, CHUNKS)
            for c in range(CHUNKS):
                pe.wait_ge(gsl_ready, c + 1)
                if c == 1:
                    pe.wait_ge(gs_ready, 1)
                if c >= 2:
                    pe.wait_ge(co_ready, c - 1)
                for a in range(CHUNK):
                    dst = bank[4 * (c % 2) + a // 2][0:WINDOWS, C * (a % 2):C * (a % 2 + 1)]
                    w = slice(WINDOWS * a, WINDOWS * (a + 1))
                    n = slice(C * (CHUNK * c + a), C * (CHUNK * c + a + 1))
                    nc.tensor.matmul(dst, gsH[:, c % 2, w], bandH[:, n], start=True, stop=False)
                    nc.tensor.matmul(dst, gsH[:, c % 2, w], bandL[:, n], start=False, stop=False)
                    mm = nc.tensor.matmul(dst, gsL[:, c % 2, w], bandH[:, n], start=False, stop=True)
                mm.then_inc(class_ready, 1)

            pe.wait_ge(co_ready, CHUNKS)
            pe.wait_ge(corr_added[0], 16)
            for s in (xt_ready, u_ready, v_ready, s_ready, pt_ready, o_ready, t2t_ready, g_ready, pf_ready):
                pe.sem_inc(s, AHEAD)

            def step(t, par, front, mid, back):
                old = 1 - par
                if front:
                    pe.wait_ge(xn_ready, t + 1 + AHEAD)
                    pe.wait_ge(xl_ready, t + AHEAD)
                    for part in range(2):
                        for h in range(HALVES):
                            at = PIX * part + P * h
                            mm = nc.tensor.transpose(bank[0][:, at:at + P], xn[:, h, CA * part:CA * (part + 1)], ident)
                    mm.then_inc(xt_ready, 1)
                if mid:
                    pe.wait_ge(ul_ready, t + AHEAD)
                    pe.wait_ge(max_ready, t - 1 + AHEAD)
                    for h in range(HALVES):
                        q, k = slice(P * h, P * (h + 1)), slice(0, P * (h + 1))
                        dst = bank[3][:, P * h:P * h + P * (h + 1)]
                        xh_a, xl_a, xh_b, xl_b = XH[:, old, 0, k], XL[:, old, 0, k], XH[:, old, 1, k], XL[0:CB, old, 1, k]
                        nc.tensor.matmul(dst, UH[:, old, 0, q], xh_a, start=True, stop=False)
                        nc.tensor.matmul(dst, UH[:, old, 0, q], xl_a, start=False, stop=False)
                        nc.tensor.matmul(dst, uAl[:, old, q], xh_a, start=False, stop=False)
                        nc.tensor.matmul(dst, UH[:, old, 1, q], xh_b, start=False, stop=False)
                        mm = nc.tensor.matmul(dst, UH[0:CB, old, 1, q], xl_b, start=False, stop=True)
                    mm.then_inc(s_ready, 1)
                if back:
                    pe.wait_ge(xn2_ready, t - 1 + AHEAD)
                    pe.wait_ge(x2_copied, t - 2 + AHEAD)
                    for part in range(2):
                        for h in range(HALVES):
                            at = PIX * part + P * h
                            mm = nc.tensor.transpose(bank[6][:, at:at + P], xn2[:, h, CB * part:CB * part + P], ident)
                    mm.then_inc(t2t_ready, 1)
                if front:
                    pe.wait_ge(xl_ready, t + 1 + AHEAD)
                    pe.wait_ge(ul_ready, t + AHEAD)
                    for m in range(2):
                        dst = bank[1][:, PIX * m:PIX * (m + 1)]
                        c = slice(CA * m, CA * (m + 1))
                        q = slice(2 * CA + CA * m, 2 * CA + CA * (m + 1))
                        nc.tensor.matmul(dst, mH[:, c], XH[:, par, 0], start=True, stop=False)
                        nc.tensor.matmul(dst, mH[:, c], XL[:, par, 0], start=False, stop=False)
                        nc.tensor.matmul(dst, mL[:, c], XH[:, par, 0], start=False, stop=False)
                        nc.tensor.matmul(dst, mH[:, q], XH[:, par, 1], start=False, stop=False)
                        mm = nc.tensor.matmul(dst, mH[0:CB, q], XL[0:CB, par, 1], start=False, stop=True)
                    mm.then_inc(u_ready, 1)
                if mid:
                    pe.wait_ge(exp_ready, t + AHEAD)
                    pe.wait_ge(pt_copied, t - 1 + AHEAD)
                    for k in range(3):
                        mm = nc.tensor.transpose(bank[4][:, P * k:P * (k + 1)], Pr[:, P * k:P * (k + 1)], ident)
                    mm.then_inc(pt_ready, 1)
                if front:
                    pe.wait_ge(v_copied, t + AHEAD)
                    for h in range(HALVES):
                        q = slice(P * h, P * (h + 1))
                        mm = products(bank[2][:, C * h:C * (h + 1)], XH[:, par, 0, q], XL[:, par, 0, q], XH[:, par, 1, q], XL[0:CB, par, 1, q],
                                      vwH[:, 0:C], vwL[:], vwH[:, C:2 * C], vwH[0:CB, C:2 * C])
                    mm.then_inc(v_ready, 1)
                if back:
                    pe.wait_ge(x2_copied, t - 1 + AHEAD)
                    pe.wait_ge(pos_ready, t - 2 + AHEAD)
                    wg = c2("wg")
                    for h in range(HALVES):
                        dst = bank[7][:, EXPERTS * h:EXPERTS * (h + 1)]
                        nc.tensor.matmul(dst, x2T[:, 0, P * h:P * (h + 1)], wg[:, 0:EXPERTS], start=True, stop=False)
                        mm = nc.tensor.matmul(dst, x2T[CB:P, 1, P * h:P * (h + 1)], wg[CB:P, EXPERTS:2 * EXPERTS], start=False, stop=True)
                    mm.then_inc(g_ready, 1)
                if mid:
                    pe.wait_ge(pt_copied, t + AHEAD)
                    pe.wait_ge(v_copied, t + AHEAD)
                    pe.wait_ge(t2_ready, t - 1 + AHEAD)
                    nc.tensor.matmul(bank[5][:, 0:C], PT[:, 0:P], V[:, old, 0], start=True, stop=True)
                    nc.tensor.matmul(bank[5][:, C:2 * C], PT[:, P:2 * P], V[:, old, 0], start=True, stop=False)
                    nc.tensor.matmul(bank[5][:, C:2 * C], PT[:, 2 * P:3 * P], V[:, old, 1], start=False, stop=True).then_inc(o_ready, 1)
                if back:
                    pe.wait_ge(oh_ready, t - 1 + AHEAD)
                    before, all_ = tri_sb[:, 0:P], tri_sb[:, P:2 * P]
                    e = 2 * EXPERTS
                    nc.tensor.matmul(bank[7][:, e:e + EXPERTS], before, oh[:, 0], start=True, stop=True)
                    e += EXPERTS
                    nc.tensor.matmul(bank[7][:, e:e + EXPERTS], before, oh[:, 1], start=True, stop=False)
                    nc.tensor.matmul(bank[7][:, e:e + EXPERTS], all_, oh[:, 0], start=False, stop=True)
                    e += EXPERTS
                    nc.tensor.matmul(bank[7][:, e:e + EXPERTS], all_, oh[:, 0], start=True, stop=False)
                    nc.tensor.matmul(bank[7][:, e:e + EXPERTS], all_, oh[:, 1], start=False, stop=True).then_inc(pf_ready, 1)

            step(0, 0, True, False, False)
            step(1, 1, True, True, False)
            with pe.Fori(1, IMAGES // 2) as i:
                for par in range(2):
                    step(2 * i + par, par, True, True, True)
            step(IMAGES, 0, False, True, True)
            step(IMAGES + 1, 1, False, False, True)
            for s in (fxt_ready, h_ready, gt_ready, y_ready):
                pe.sem_inc(s, AHEAD)

            def ffn_step(j, par, back, mid, nxt):
                def expert(j):
                    pe.wait_ge(table_ready, 1)
                    e = pe.value_load(slot_expert[0:1, bass.ds(j, 1)], min_val=0, max_val=EXPERTS - 1)

                    def cols(p0, p1, c0, c1):
                        return wall[p0:p1, bass.ds(e, 1), c0:c1].rearrange("p a c -> p (a c)")
                    return cols

                if back:
                    pe.wait_ge(gh_ready, j + AHEAD)
                    for k in range(FT):
                        mm = nc.tensor.transpose(bank[5][:, P * k:P * (k + 1)], gh[:, 1 - par, P * k:P * (k + 1)], ident)
                    mm.then_inc(gt_ready, 1)
                if mid:
                    w = expert(j)
                    pe.wait_ge(fl2_ready, j + 1 + AHEAD)
                    for m in range(2):
                        dst = bank[1 + 2 * par + m][:, 0:FE]
                        a, q = FE * m, 2 * W12 + FE * m
                        mm = products(dst, FH[:, par, 0], FL[:, par, 0], FH[:, par, 1], FL[0:CB, par, 1],
                                      w(0, P, a, a + FE), w(0, P, W12 + a, W12 + a + FE), w(0, P, q, q + FE), w(0, CB, q, q + FE))
                    mm.then_inc(h_ready, 1)
                if nxt:
                    pe.wait_ge(fx_ready, j + 2 + AHEAD)
                    pe.wait_ge(fl2_ready, j + 1 + AHEAD)
                    for part in range(2):
                        mm = nc.tensor.transpose(bank[0][:, P * part:P * (part + 1)], xf[:, CA * part:CA * (part + 1)], ident)
                    mm.then_inc(fxt_ready, 1)
                if back:
                    w = expert(j - 1)
                    pe.wait_ge(hl_ready, j + AHEAD)
                    pe.wait_ge(y_taken, j - 2 + AHEAD)
                    dst = bank[7 - par]
                    for k in range(FT):
                        c0 = 3 * W12 + 2 * C * k
                        nc.tensor.matmul(dst[:, 0:2 * C], HH[:, 1 - par, k], w(0, P, c0, c0 + 2 * C), start=(k == 0), stop=False)
                        mm = nc.tensor.matmul(dst[:, 0:C], HL[:, 1 - par, k], w(0, P, c0, c0 + C), start=False, stop=(k == FT - 1))
                    mm.then_inc(y_ready, 1)

            ffn_step(-1, 1, False, False, True)
            pe.wait_ge(wall_lo, EXPERTS - 1)
            pe.wait_ge(wall_q, EXPERTS - 1)
            pe.wait_ge(wall_dve, 1)
            ffn_step(0, 0, False, True, True)
            ffn_step(1, 1, True, True, True)
            with pe.Fori(1, SLOTS // 2) as i:
                for par in range(2):
                    ffn_step(2 * i + par, par, True, True, True)
            ffn_step(SLOTS - 1, 0, True, True, False)
            ffn_step(SLOTS, 1, True, False, False)


def lay_out(x, conv_w, conv_b, wq, wk, wv, Wg, bg, W1, W2, W3):
    import numpy as np

    f = np.float32

    def a_bb(m):
        return np.stack([m[:CA], np.concatenate([m[CA:], m[CA:]])], 1)

    def cols_a_bb(m):
        return np.concatenate([m[:, :CA], m[:, CA:], m[:, CA:]], 1)

    xt = x.reshape(IMAGES, C, PIX)
    x_cm = np.stack([xt[:, :CA], np.concatenate([xt[:, CA:], xt[:, CA:]], 1)], 2).reshape(IMAGES, P, 2 * PIX)
    x_tm = xt.transpose(0, 2, 1).reshape(TILES, P, C).transpose(1, 0, 2)

    group = np.arange(C) // (C // GROUPS)
    gm = (group[:, None] == group[None, :]).astype(f) / (2 * C // GROUPS)
    shift = (np.arange(480)[None, :] == np.arange(P)[:, None] + SHIFT0).astype(f)
    offs = [(i, i) for i in range(KERNEL)] + [(i, REACH) for i in range(KERNEL)]
    offs += [(i, KERNEL - 1 - i) for i in range(KERNEL)] + [(REACH, i) for i in range(KERNEL)]
    centers = [n for n, o in enumerate(offs) if o == (REACH, REACH)]
    rows4 = np.stack([conv_b] + [conv_w[:, C + n] for n in centers[1:]])
    s1 = [a_bb(conv_w[:, :C].T), a_bb(cols_a_bb(gm)), np.broadcast_to(rows4, (P, 4, C)),
          a_bb(cols_a_bb(wq.T)), a_bb(cols_a_bb(wk.T)), a_bb(wv), shift]
    small1 = np.concatenate([a.reshape(P, -1) for a in s1], 1)
    assert small1.shape[1] == S1N

    band = np.zeros((P, PAIR, C), f)
    for n, (r, cx) in enumerate(offs):
        if n in centers[1:]:
            continue
        for p in range(PAIR):
            q = p % SIDE + cx - REACH
            if 0 <= q < SIDE:
                band[(p // SIDE + r) * SIDE + q, p] = conv_w[:, C + n]
    band = band.reshape(P, PAIR * C)

    k = np.arange(P)
    causal = np.where(k[None, :] <= k[:, None], 0.0, NEG).astype(f)
    mask = np.concatenate([causal, np.zeros((P, P), f), causal], 1)
    desc = np.broadcast_to(np.arange(EXPERTS, 0, -1).astype(f), (P, 2, EXPERTS))
    base = np.broadcast_to((np.arange(EXPERTS) * REGION + PAD).astype(f), (P, EXPERTS))
    slot = np.broadcast_to(np.arange(SLOTS + 1).astype(f), (P, SLOTS + 1))
    s2 = [np.eye(P, dtype=f), mask, a_bb(Wg.T), np.broadcast_to(bg, (P, 2, EXPERTS)), desc, base, slot,
          (k[:, None] < k[None, :]).astype(f), np.ones((P, P), f)]
    small2 = np.concatenate([a.reshape(P, -1) for a in s2], 1)
    assert small2.shape[1] == S2N

    w12 = np.zeros((EXPERTS, C, 2, FE), f)
    w12[:, :, 0, :F] = W1.transpose(0, 2, 1)
    w12[:, :, 1, :F] = W2.transpose(0, 2, 1)
    w12 = w12.reshape(EXPERTS, C, W12)
    w3 = np.zeros((EXPERTS, FT * P, C), f)
    w3[:, :F] = W3.transpose(0, 2, 1)
    w3 = w3.reshape(EXPERTS, FT, P, C).transpose(0, 2, 1, 3).reshape(EXPERTS, P, W3C)
    w_all = np.concatenate([w12[:, :CA], np.concatenate([w12[:, CA:], w12[:, CA:]], 1), w3], 2)
    return [("x_cm", x_cm), ("x_tm", x_tm), ("small1", small1), ("small2", small2), ("band", band), ("w_all", w_all)]


def kernel(x, L0_conv_conv_w, L0_conv_conv_b, L1_attn_wq, L1_attn_wk, L1_attn_wv, L1_ffn_Wg, L1_ffn_bg, L1_ffn_W1, L1_ffn_W2, L1_ffn_W3):
    import numpy as np
    import concourse.bacc as bacc
    from concourse.bass_utils import run_bass_kernel_spmd as run

    ins = lay_out(*(np.asarray(a) for a in (x, L0_conv_conv_w, L0_conv_conv_b, L1_attn_wq, L1_attn_wk, L1_attn_wv,
                                            L1_ffn_Wg, L1_ffn_bg, L1_ffn_W1, L1_ffn_W2, L1_ffn_W3)))
    nc = bacc.Bacc("TRN2", target_bir_lowering=False, num_devices=1)
    arrays, args = {}, []
    for name, a in ins:
        arrays["in_" + name] = np.ascontiguousarray(a)
        args.append(nc.dram_tensor("in_" + name, a.shape, mybir.dt.from_np(a.dtype), kind="ExternalInput").ap())
    out = nc.dram_tensor("out_rows", (TILES * P, C), F32, kind="ExternalOutput").ap()
    build(nc, *args, out)
    res = run(nc, [arrays], core_ids=[0])
    t = res.results[0]["out_rows"]
    return np.ascontiguousarray(t.reshape(IMAGES, PIX, C).transpose(0, 2, 1).reshape(IMAGES, C, SIDE, SIDE))
```

```python
from contextlib import ExitStack

import concourse.bass as bass
from concourse import mybir

F32 = mybir.dt.float32
F32R = mybir.dt.float32r
BF16 = mybir.dt.bfloat16
I32 = mybir.dt.int32
U32 = mybir.dt.uint32
ALU = mybir.AluOpType
ACT = mybir.ActivationFunctionType
AX_X = mybir.AxisListType.X

P = 128
IMAGES = 8
SIDE = 16
PIX = SIDE * SIDE
C = 192
CA, CB = P, C - P
HALVES = PIX // P
TILES = IMAGES * HALVES
GROUPS = 32
KERNEL = 7
REACH = KERNEL // 2
PAD_PIX = REACH * SIDE
NEAR = P + 4 * SIDE
PAIR = 2 * SIDE
PAIRS = PIX // PAIR
QUARTER = TILES // 4
WINDOWS = IMAGES * PAIRS
CHUNK = 8
CHUNKS = PAIR // CHUNK
BAND_CHUNK = CHUNK * C

EXPERTS = 8
F = 469
FE = F + 1
FT = 4
W12 = 2 * FE
W3C = FT * C
STAGE = 2 * W12 + W3C
WALL = 3 * W12 + 2 * W3C
SLOTS = TILES + EXPERTS - 1
PAD = P
REGION = TILES * P + PAD
EMPTY = EXPERTS * REGION
NO_TOKEN = 1 << 20
ROW = C + 4

EPS_NORM = 1e-12
EPS = 1e-5
NEG = -1e30
SM_SCALE = float(C) ** -0.5
AHEAD = 2

S1 = {}
S2 = {}
_at = 0
for _n, _w in (("gm", 4 * CA), ("cf", 2 * C), ("rows", 4 * C), ("wq", 4 * CA), ("wk", 4 * CA), ("wv", 2 * C), ("shift", 480)):
    S1[_n] = (_at, _at + _w)
    _at += _w
S1N = _at
_at = 0
for _n, _w in (("id", P), ("mask", 3 * P), ("wg", 2 * EXPERTS), ("bg", 2 * EXPERTS), ("desc", 2 * EXPERTS), ("base", EXPERTS), ("slot", SLOTS + 1), ("tri", 2 * P)):
    S2[_n] = (_at, _at + _w)
    _at += _w
S2N = _at
SHIFT0 = 176


def build(nc, x_cm, x_tm, small1, small2, band, w_all, out):
    xs = nc.dram_tensor("token_rows", (EMPTY + P, ROW), F32).ap()
    corr = nc.dram_tensor("corr_rows", (TILES * P, C), F32).ap()

    top = ExitStack()
    with top:
        def sb(name, shape, dt=F32, ctx=top):
            return ctx.enter_context(nc.sbuf_tensor(name, shape, dt))

        def sem(name):
            return top.enter_context(nc.semaphore(name))

        bank = [top.enter_context(nc.psum_tensor(f"bank{i}", [P, 512], F32)) for i in range(8)]

        rows = sb("rows", [P, SLOTS, ROW])
        s2 = sb("small2_sb", [P, S2N])
        stage = sb("stage", [P, 2, STAGE])
        mH = sb("mH", [P, 4 * CA], F32R)
        mL = sb("mL", [P, 2 * CA], F32R)
        vwH = sb("vwH", [P, 2 * C], F32R)
        vwL = sb("vwL", [P, C], F32R)
        tri_sb = sb("tri_sb", [P, 2 * P], BF16)
        eps_c = sb("eps_c", [P, 1])
        run = sb("run", [P, EXPERTS])
        posi = sb("posi", [P, TILES], I32)

        def c2(name):
            return s2[:, S2[name][0]:S2[name][1]]

        ident = c2("id")

        early = ExitStack()
        early.enter_context(nc.sbuf_tensor("early_gap", [P, WALL], F32R))
        bandH = sb("bandH", [P, PAIR * C], F32R, early)
        bandL = sb("bandL", [P, PAIR * C], F32R, early)
        xcm = sb("xcm", [P, IMAGES, 2, PIX], ctx=early)
        s1 = sb("small1_sb", [P, S1N], ctx=early)
        f32t = sb("f32t", [P, 2, 2, PIX], ctx=early)
        f2 = sb("f2", [P, 2, 2, 2, PIX], F32R, early)
        fQ = sb("fQ", [P, 2, PIX], F32R, early)
        gram = sb("gram", [P, IMAGES, HALVES, NEAR], ctx=early)
        around = sb("around", [P, IMAGES, PAIRS, PAIR], ctx=early)
        gs = sb("gs", [P, 2, CHUNK * WINDOWS], ctx=early)
        gsH = sb("gsH", [P, 2, CHUNK * WINDOWS], F32R, early)
        gsL = sb("gsL", [P, 2, CHUNK * WINDOWS], F32R, early)
        co = sb("co", [WINDOWS, 2, CHUNK, C], ctx=early)
        cfH = sb("cfH", [P, 2 * C], F32R, early)
        cfL = sb("cfL", [P, C], F32R, early)
        bias2 = sb("bias2", [CB, C], F32R, early)
        ones2 = sb("ones2", [CB, P], F32R, early)
        wsum = sb("wsum", [P, C], ctx=early)
        gst = sb("gst", [P, IMAGES, 2, 6], ctx=early)
        mq = sb("mq", [P, IMAGES, 2, 2, 2], ctx=early)
        msq = sb("msq", [P, IMAGES, 2, 2], ctx=early)
        mv = sb("mv", [P, 2, 2, IMAGES // 2, 2], ctx=early)
        gvar = sb("gvar", [P, 2, 2, IMAGES // 2], ctx=early)
        grs = sb("grs", [P, 2, 2, IMAGES // 2], ctx=early)
        gnb = sb("gnb", [P, 2, 2, IMAGES // 2], ctx=early)
        ssq = sb("ssq", [P, TILES], ctx=early)
        rn = sb("rn", [P, TILES], ctx=early)
        cc = sb("cc", [P, TILES], ctx=early)
        rwin = sb("rwin", [P, IMAGES, PAIRS], ctx=early)
        rT = sb("rT", [TILES, P], ctx=early)
        rbk = sb("rbk", [WINDOWS, PAIR], ctx=early)
        emptyt = sb("emptyt", [P, ROW], ctx=early)
        early.close()

        middle = ExitStack()
        middle.enter_context(nc.sbuf_tensor("middle_gap", [P, (EXPERTS - 1) * WALL], F32R))
        xn = sb("xn", [P, HALVES, 2 * CA], ctx=middle)
        XH = sb("XH", [P, 2, 2, PIX], F32R, middle)
        XL = sb("XL", [P, 2, 2, PIX], F32R, middle)
        UH = sb("UH", [P, 2, 2, PIX], F32R, middle)
        uAl = sb("uAl", [P, 2, PIX], F32R, middle)
        V = sb("V", [P, 2, HALVES, C], ctx=middle)
        sc_sb = sb("scores_sb", [P, 3 * P], ctx=middle)
        Pr = sb("probs", [P, 3 * P], ctx=middle)
        PT = sb("probs_t", [P, 3 * P], ctx=middle)
        xn2 = sb("xn2", [P, HALVES, C], ctx=middle)
        x2T = sb("x2T", [P, 2, PIX], ctx=middle)
        tstat = sb("tstat", [P, TILES, 6], ctx=middle)
        ln1 = sb("ln1", [P, TILES, 2], ctx=middle)
        ln2 = sb("ln2", [P, HALVES, 2], ctx=middle)
        lnv = sb("lnv", [P, HALVES], ctx=middle)
        rs0 = sb("rs0", [P, HALVES], ctx=middle)
        newt = sb("newt", [P, 2, TILES], ctx=middle)
        logs = sb("logs", [P, TILES], ctx=middle)
        guess = sb("guess", [P, TILES], ctx=middle)
        smx = sb("smx", [P, 2], ctx=middle)
        rsum = sb("rsum", [P, 2], ctx=middle)
        nmx = sb("nmx", [P, 2], ctx=middle)
        ssum = sb("ssum", [P, 2], ctx=middle)
        lg = sb("lg", [P, 2, EXPERTS], ctx=middle)
        gmx = sb("gmx", [P, 2], ctx=middle)
        oh = sb("oh", [P, 2, EXPERTS], BF16, middle)
        pos = sb("pos", [P, 2], ctx=middle)
        middle.close()

        wall = sb("wall", [P, EXPERTS, WALL], F32R)
        xf = sb("xf", [P, 2 * CA])
        FH = sb("FH", [P, 2, 2, P], F32R)
        FL = sb("FL", [P, 2, 2, P], F32R)
        gh = sb("gh", [P, 2, FT * P])
        HH = sb("HH", [P, 2, FT, P], F32R)
        HL = sb("HL", [P, 2, FT, P], F32R)
        yo = sb("yo", [P, 2, C])
        tiles_i = sb("tiles_i", [P, EXPERTS], I32)
        tiles_f = sb("tiles_f", [P, EXPERTS])
        ends = sb("ends", [P, 2, EXPERTS])
        started = sb("started", [P, SLOTS, EXPERTS])
        picked = sb("picked", [P, SLOTS, EXPERTS])
        per_slot = sb("per_slot", [P, 3, SLOTS])
        slot_expert = sb("slot_expert", [P, SLOTS], I32)
        slot_row = sb("slot_row", [P, SLOTS], I32)

        corr_sb = xcm[:].rearrange("p b t x -> p (b t x)")[:, 0:TILES * C].rearrange("p (j c) -> p j c", c=C)

        pieces = []
        for k in range(PAIRS):
            q0 = PAIR * k - PAD_PIX
            for h in range(HALVES):
                a, z = max(q0, P * h), min(q0 + P, P * (h + 1))
                if a < z:
                    c0 = PAIR * k - (PIX - NEAR) * h
                    pieces.append((k, h, slice(a - P * h, z - P * h), slice(a - q0, z - q0), slice(c0, c0 + PAIR)))

        def on(t, k):
            return not isinstance(t, int) or 0 <= t - k < IMAGES

        def c1(name):
            return s1[:, S1[name][0]:S1[name][1]]

        small1_in, small2_in, tm_in, rbk_in = sem("small1_in"), sem("small2_in"), sem("tm_in"), sem("rbk_in")
        cm_in = [sem("cm_in0"), sem("cm_in1")]
        stage_in = [sem("stage_in0"), sem("stage_in1")]
        stage_hi, stage_free = sem("stage_hi"), sem("stage_free")
        empty_out = sem("empty_out")
        corr_out = [sem("corr_out0"), sem("corr_out1")]
        corr_in = [sem(f"corr_in{q}") for q in range(4)]
        corr_added = sem("corr_added")
        dve = sem("dve_step")
        prep_ready, m_ready, m_split, wsplit_hi, small_split = sem("prep_ready"), sem("m_ready"), sem("m_split"), sem("wsplit_hi"), sem("small_split")
        gstat_in, gstat_ready, gvar_ready, gstd_ready, gnorm_ready = sem("gstat_in"), sem("gstat_ready"), sem("gvar_ready"), sem("gstd_ready"), sem("gnorm_ready")
        f_ready, fh_ready, fl_ready, fq_ready = sem("f_ready"), sem("fh_ready"), sem("fl_ready"), sem("fq_ready")
        conv_ready, conv_taken, gram_ready, gram_taken = sem("conv_ready"), sem("conv_taken"), sem("gram_ready"), sem("gram_taken")
        ssq_ready, nrm_ready, rn_ready, cc_ready, rwin_ready, rt_ready, rt_copied = sem("ssq_ready"), sem("nrm_ready"), sem("rn_ready"), sem("cc_ready"), sem("rwin_ready"), sem("rt_ready"), sem("rt_copied")
        gs_ready, gsh_ready, gsl_ready, class_ready, co_ready = sem("gs_ready"), sem("gsh_ready"), sem("gsl_ready"), sem("class_ready"), sem("co_ready")
        iota_done = sem("iota_done")
        empty_ready = sem("empty_ready")
        (xn_ready, xt_ready, xh_ready, xl_ready, u_ready, uh_ready, ul_ready, v_ready, v_copied, s_ready, max_ready,
         exp_ready, pt_ready, pt_copied, o_ready, t2_ready, xn2_ready, t2t_ready, x2_copied, g_ready, oh_ready, pf_ready,
         pos_ready, var_ready, rs_ready, ln_ready, ln1_ready, o_taken, dve2, wall_hi, wall_lo) = (sem(n) for n in (
             "xn_ready", "xt_ready", "xh_ready", "xl_ready", "u_ready", "uh_ready", "ul_ready", "v_ready", "v_copied",
             "s_ready", "max_ready", "exp_ready", "pt_ready", "pt_copied", "o_ready", "t2_ready", "xn2_ready", "t2t_ready",
             "x2_copied", "g_ready", "oh_ready", "pf_ready", "pos_ready", "var_ready", "rs_ready", "ln_ready", "ln1_ready", "o_taken", "dve2", "wall_hi", "wall_lo"))
        group_in, attn_in, attn_split, co_high = sem("group_in"), sem("attn_in"), sem("attn_split"), sem("co_high")
        ln1_var, ln1_log, ln1_guess = sem("ln1_var"), sem("ln1_log"), sem("ln1_guess")
        gram_half, diag_read, zeroed, held, wall_q = sem("gram_half"), sem("diag_read"), sem("zeroed"), sem("held"), sem("wall_q")
        windows_in = [sem("windows_in0"), sem("windows_in1")]
        band_in = [sem("band_in0"), sem("band_in1")]
        scattered, table_ready = sem("scattered"), sem("table_ready")
        slot_in = [sem("slot_in0"), sem("slot_in1")]
        out_sent = [sem("out_sent0"), sem("out_sent1")]
        (fx_ready, fxt_ready, fh2_ready, fl2_ready, h1_ready, h_ready, silu_ready, gh_ready, gt_ready, hh_ready, hl_ready, y_ready,
         y_taken, yo_free, dve3) = (sem(n) for n in ("fx_ready", "fxt_ready", "fh2_ready", "fl2_ready", "h1_ready", "h_ready", "silu_ready", "gh_ready",
                                            "gt_ready", "hh_ready", "hl_ready", "y_ready", "y_taken", "yo_free", "dve3"))

        block = top.enter_context(nc.Block())

        @block.sync
        def _(sp):
            n2 = IMAGES // 2

            def load_images(h):
                sp.dma_start(xcm[:, n2 * h:n2 * (h + 1)].rearrange("p b t x -> p b (t x)"),
                             x_cm[n2 * h:n2 * (h + 1)].rearrange("b p x -> p b x")).then_inc(cm_in[h], 16)

            conv0, attn0 = S1["cf"][0], S1["wq"][0]
            load_images(0)
            sp.dma_start(s1[:, 0:conv0], small1[:, 0:conv0]).then_inc(group_in, 16)
            sp.dma_start(s1[:, conv0:attn0], small1[:, conv0:attn0]).then_inc(small1_in, 16)
            load_images(1)
            sp.dma_start(rows[:, 0:TILES, 0:C], x_tm).then_inc(tm_in, 16)
            sp.dma_start(s2[:], small2).then_inc(small2_in, 16)
            sp.dma_start(s1[:, attn0:S1N], small1[:, attn0:S1N]).then_inc(attn_in, 16)
            for n in range(2):
                sp.dma_start(stage[:, n % 2, 0:BAND_CHUNK], band[:, BAND_CHUNK * n:BAND_CHUNK * (n + 1)]).then_inc(stage_in[n % 2], 16)
            sp.wait_ge(empty_ready, 1)
            for e in range(EXPERTS + 1):
                sp.dma_start(xs[REGION * e:REGION * e + P, :], emptyt[:]).then_inc(empty_out, 16)
            sp.wait_ge(zeroed, 1)
            for s, images in zip(windows_in, (slice(0, n2 + 1), slice(n2 + 1, IMAGES))):
                sp.wait_ge(gram_taken, images.stop + AHEAD)
                for k, h, src, dst, cols in pieces:
                    sp.dma_start(around[dst, images, k], gram[src, images, h, cols]).then_inc(s, 16)
            sp.wait_ge(rt_copied, 1)
            for k in range(P // PAIR):
                sp.dma_start(rbk[k:WINDOWS:P // PAIR, :], rT[:, PAIR * k:PAIR * (k + 1)]).then_inc(rbk_in, 16)
            for c in range(CHUNKS):
                sp.wait_ge(co_ready, c + 1)
                sp.wait_ge(co_high, c + 1)
                sp.dma_start(corr.rearrange("(w p) c -> w p c", p=PAIR)[:, CHUNK * c:CHUNK * (c + 1), :], co[:, c % 2]).then_inc(corr_out[c % 2], 16)
            for s in corr_out:
                sp.wait_ge(s, 16 * (CHUNKS // 2))
            tok = corr.rearrange("(j p) c -> p j c", p=P)
            for q in range(4):
                sp.dma_start(corr_sb[:, QUARTER * q:QUARTER * (q + 1)], tok[:, QUARTER * q:QUARTER * (q + 1), :]).then_inc(corr_in[q], 16)
            for e in range(EXPERTS):
                n = CHUNKS + e
                if e < 2:
                    sp.wait_ge(stage_free, n - 1)
                else:
                    sp.wait_ge(wall_lo, e - 1)
                    sp.wait_ge(wall_q, e - 1)
                sp.dma_start(stage[:, n % 2], w_all[e]).then_inc(stage_in[n % 2], 16)
            sp.wait_ge(scattered, 16 * TILES)
            sp.wait_ge(empty_out, 16 * (EXPERTS + 1))
            sp.wait_ge(table_ready, 1)

            def load_slot(j, par, k):
                if k is not None:
                    sp.wait_ge(slot_in[par], 16 * k)
                sp.wait_ge(table_ready, 1)
                off = sp.value_load(slot_row[0:1, bass.ds(j, 1)], min_val=0, max_val=EMPTY)
                sp.dma_start(rows[:, bass.ds(j, 1), :].rearrange("p a c -> p (a c)"), xs[bass.ds(off, P), :]).then_inc(slot_in[par], 16)

            for j in range(2):
                load_slot(j, j, None)
            with sp.Fori(1, SLOTS // 2) as i:
                for par in range(2):
                    load_slot(2 * i + par, par, i)
            load_slot(SLOTS - 1, (SLOTS - 1) % 2, (SLOTS - 1) // 2)
            for par in range(2):
                sp.wait_ge(out_sent[par], 16 * ((SLOTS + 1 - par) // 2))

        @block.gpsimd
        def _(pool):
            nc.gpsimd.memset(emptyt[:], 0.0).then_inc(iota_done, 1)
            pool.wait_ge(iota_done, 1)
            nc.gpsimd.iota(emptyt[:, C + 2:C + 3].bitcast(I32), pattern=[[0, 1]], base=NO_TOKEN, channel_multiplier=0).then_inc(empty_ready, 1)
            nc.gpsimd.iota(rows[:, 0:TILES, C + 2].bitcast(I32), pattern=[[P, TILES]], base=0, channel_multiplier=1).then_inc(iota_done, 1)
            nc.gpsimd.memset(rows[:, 0:TILES, C + 3], 0.0).then_inc(iota_done, 1)
            nc.gpsimd.memset(around[:].rearrange("q b k c -> q (b k c)"), 0.0).then_inc(zeroed, 1)
            for n in range(CHUNKS):
                pool.wait_ge(stage_hi, n + 1)
                at = slice(n * BAND_CHUNK, (n + 1) * BAND_CHUNK)
                nc.gpsimd.tensor_tensor(bandL[:, at], stage[:, n % 2, 0:BAND_CHUNK], bandH[:, at].bitcast(F32), ALU.subtract).then_inc(stage_free, 1)
                if n < 2:
                    pool.wait_ge(stage_free, n + 1)
                    pool.dma_start(stage[:, n % 2, 0:BAND_CHUNK], band[:, BAND_CHUNK * (n + 2):BAND_CHUNK * (n + 3)]).then_inc(band_in[n], 16)
            pool.wait_ge(corr_added, 1)
            pool.wait_ge(empty_out, 16 * (EXPERTS + 1))

            def scatter_tokens(b):
                pool.wait_ge(pos_ready, b + 1 + AHEAD)
                for h in range(HALVES):
                    j = 2 * b + h
                    pool.indirect_dma_start(out=xs, out_offset=bass.IndirectOffsetOnAxis(ap=posi[:, j:j + 1].bitcast(U32), axis=0),
                                            in_=rows[:, j], in_offset=None,
                                            bounds_check=EMPTY - 1, oob_is_err=False).then_inc(scattered, 16)

            def weights_lo(e, par):
                pool.wait_ge(wall_hi, e + 1)
                pool.wait_ge(tm_in, 16)
                w = wall[:, e]
                nc.gpsimd.tensor_tensor(w[:, W12:2 * W12], stage[:, par, 0:W12], w[:, 0:W12].bitcast(F32), ALU.subtract)
                w3 = w[:, 3 * W12:WALL].rearrange("p (k s c) -> p k s c", s=2, c=C)
                nc.gpsimd.tensor_tensor(w3[:, :, 1], stage[:, par, 2 * W12:STAGE].rearrange("p (k c) -> p k c", c=C),
                                        w3[:, :, 0].bitcast(F32), ALU.subtract).then_inc(wall_lo, 1)

            for t in range(1, IMAGES + 3):
                if t < EXPERTS:
                    weights_lo(t - 1, 1 - t % 2)
                if t >= 3:
                    scatter_tokens(t - 3)
            weights_lo(EXPERTS - 1, (CHUNKS + EXPERTS - 1) % 2)
            pool.sem_inc(yo_free, AHEAD)

            def send_slot(j, par):
                if j:
                    pool.wait_ge(out_sent[1 - par], 16 * ((j + 1) // 2))
                    pool.sem_inc(yo_free, 1)
                pool.wait_ge(y_taken, j + 1 + AHEAD)
                pool.wait_ge(tm_in, 16)
                pool.indirect_dma_start(out=out, out_offset=bass.IndirectOffsetOnAxis(ap=rows[:, j, C + 2:C + 3].bitcast(U32), axis=0),
                                        in_=yo[:, par], in_offset=None, bounds_check=TILES * P - 1, oob_is_err=False).then_inc(out_sent[par], 16)

            for j in range(SLOTS):
                send_slot(j, j % 2)

        @block.scalar
        def _(sc):
            sc.wait_ge(small1_in, 16)
            nc.scalar.activation(cfH[:], c1("cf"), ACT.Copy).then_inc(wsplit_hi, 1)
            sc.wait_ge(prep_ready, 1)

            def group_root(h):
                sc.wait_ge(gvar_ready, h + 1)
                nc.scalar.activation(grs[:, h], gvar[:, h], ACT.Sqrt, bias=eps_c[:, 0:1]).then_inc(gstd_ready, 1)

            sc.sem_inc(f_ready, AHEAD)
            sc.sem_inc(fh_ready, AHEAD)

            def norm_image(b, par):
                half, at = (b // (IMAGES // 2), b % (IMAGES // 2))
                for t in range(2):
                    ins = nc.scalar.activation(f32t[:, par, t], xcm[:, bass.ds(b, 1), t, :].rearrange("p a x -> p (a x)"),
                                               ACT.Identity, scale=grs[:, bass.ds(half, 1), t, bass.ds(at, 1)].rearrange("p a b -> p (a b)"),
                                               bias=gnb[:, bass.ds(half, 1), t, bass.ds(at, 1)].rearrange("p a b -> p (a b)"))
                ins.then_inc(f_ready, 1)

            def high_image(b, par):
                sc.wait_ge(gram_ready, b - 1 + AHEAD)
                sc.wait_ge(f_ready, b + 1 + AHEAD)
                nc.scalar.activation(f2[:, par, :, 0], f32t[:, par], ACT.Copy)
                nc.scalar.activation(fQ[0:CB, par], f32t[0:CB, par, 1], ACT.Copy).then_inc(fh_ready, 1)

            def copy_gram(b, par):
                sc.wait_ge(gram_ready, b + 1 + AHEAD)
                for h in range(HALVES):
                    ins = nc.scalar.activation(gram[:, b, h], bank[2 + 2 * par + h][:, 0:NEAR], ACT.Copy)
                ins.then_inc(gram_half, 1)

            group_root(0)
            sc.wait_ge(gnorm_ready, 1)
            for b in range(2):
                norm_image(b, b)
                high_image(b, b)
            group_root(1)

            def band_hi(n, par):
                nc.scalar.activation(bandH[:, bass.ds(n * BAND_CHUNK, BAND_CHUNK)], stage[:, par, 0:BAND_CHUNK], ACT.Copy).then_inc(stage_hi, 1)

            for i in range(IMAGES // 2 - 1):
                for par in range(2):
                    sc.wait_ge(gnorm_ready, (2 * i + 2) // (IMAGES // 2) + 1)
                    sc.wait_ge(fl_ready, 2 * i + par + 1 + AHEAD)
                    norm_image(2 * i + 2 + par, par)
                    copy_gram(2 * i + par, par)
                    high_image(2 * i + 2 + par, par)
                sc.wait_ge(band_in[i % 2] if i >= 2 else stage_in[i], 16)
                band_hi(i, i % 2)
            i = CHUNKS - 1
            sc.wait_ge(band_in[i % 2], 16)
            band_hi(i, i % 2)
            for b in (IMAGES - 2, IMAGES - 1):
                copy_gram(b, b % 2)

            def take_class(c):
                sc.wait_ge(class_ready, c + 1)
                sc.wait_ge(rbk_in, 16 * (P // PAIR))
                if c >= 2:
                    sc.wait_ge(corr_out[c % 2], 16 * (c // 2))
                for a in range(CHUNK // 2, CHUNK):
                    src = bank[4 * (c % 2) + a // 2][0:WINDOWS, C * (a % 2):C * (a % 2 + 1)]
                    ins = nc.scalar.activation(co[:, c % 2, a], src, ACT.Copy, scale=rbk[:, CHUNK * c + a:CHUNK * c + a + 1])
                ins.then_inc(co_high, 1)

            sc.wait_ge(ssq_ready, 1)
            nc.scalar.activation(rn[:], ssq[:], ACT.Sqrt).then_inc(nrm_ready, 1)
            sc.wait_ge(m_ready, 1)
            nc.scalar.activation(mH[:], bank[6][:], ACT.Copy).then_inc(m_split, 1)
            sc.wait_ge(attn_in, 16)
            nc.scalar.activation(vwH[:], c1("wv"), ACT.Copy).then_inc(m_split, 1)
            for c in range(CHUNKS):
                sc.wait_ge(gs_ready, c + 1)
                if c >= 2:
                    sc.wait_ge(class_ready, c - 1)
                nc.scalar.activation(gsH[:, c % 2], gs[:, c % 2], ACT.Copy).then_inc(gsh_ready, 1)
                if c:
                    take_class(c - 1)
            take_class(CHUNKS - 1)

            sc.wait_ge(corr_added, 1)
            sc.wait_ge(empty_out, 16 * (EXPERTS + 1))
            for s in (xn_ready, rs_ready, xh_ready, exp_ready, x2_copied, uh_ready, pt_copied, v_copied):
                sc.sem_inc(s, AHEAD)

            def weights_hi(part, e, par, loaded):
                if part == 0:
                    sc.wait_ge(stage_in[par], 16 * loaded)
                    sc.sem_inc(held, 1)
                w = wall[:, bass.ds(e, 1), :].rearrange("p a c -> p (a c)")
                if part == 0:
                    nc.scalar.activation(w[:, 0:W12], stage[:, par, 0:W12], ACT.Copy)
                elif part == 1:
                    nc.scalar.activation(w[:, 2 * W12:3 * W12], stage[:, par, W12:2 * W12], ACT.Copy)
                else:
                    w3 = w[:, 3 * W12:WALL].rearrange("p (k s c) -> p k s c", s=2, c=C)
                    nc.scalar.activation(w3[:, :, 0], stage[:, par, 2 * W12:STAGE].rearrange("p (k c) -> p k c", c=C), ACT.Copy).then_inc(wall_hi, 1)

            def step(t, par, loaded):
                if isinstance(t, int) and t == 1:
                    sc.wait_ge(ln1_ready, 2)
                if on(t, 0):
                    sc.wait_ge(xt_ready, t + 1 + AHEAD)
                    nc.scalar.activation(XH[:, par].rearrange("p t x -> p (t x)"), bank[0][:], ACT.Copy).then_inc(xh_ready, 1)
                if on(t, 1):
                    sc.wait_ge(max_ready, t + AHEAD)
                    nc.scalar.activation(Pr[:, 0:P], sc_sb[:, 0:P], ACT.Exp, scale=SM_SCALE, bias=nmx[:, 0:1], accum_out=ssum[:, 0:1])
                    nc.scalar.activation(Pr[:, P:3 * P], sc_sb[:, P:3 * P], ACT.Exp, scale=SM_SCALE, bias=nmx[:, 1:2],
                                         accum_out=ssum[:, 1:2]).then_inc(exp_ready, 1)
                if on(t, 0):
                    sc.wait_ge(u_ready, t + 1 + AHEAD)
                    nc.scalar.activation(UH[:, par].rearrange("p t x -> p (t x)"), bank[1][:], ACT.Copy).then_inc(uh_ready, 1)
                if on(t, 2):
                    sc.wait_ge(var_ready, t - 1 + AHEAD)
                    sc.wait_ge(rs_ready, t - 2 + AHEAD)
                    nc.scalar.activation(lnv[:], ln2[:, :, 1], ACT.Ln, bias=eps_c[:, 0:1]).then_inc(ln_ready, 1)
                    sc.wait_ge(ln_ready, t - 1)
                    nc.scalar.activation(rs0[:], lnv[:], ACT.Exp, scale=-0.5).then_inc(rs_ready, 1)
                if on(t, 1):
                    sc.wait_ge(pt_ready, t + AHEAD)
                    nc.scalar.activation(PT[:], bank[4][:, 0:3 * P], ACT.Copy).then_inc(pt_copied, 1)
                if on(t, -1):
                    norm_image(t)
                if on(t, 0):
                    sc.wait_ge(v_ready, t + 1 + AHEAD)
                    nc.scalar.activation(V[:, par].rearrange("p h c -> p (h c)"), bank[2][:, 0:HALVES * C], ACT.Copy).then_inc(v_copied, 1)
                if loaded is not None:
                    weights_hi(0, t - 1, 1 - par, loaded)
                if loaded is not None:
                    weights_hi(1, t - 1, 1 - par, loaded)
                if on(t, 2):
                    sc.wait_ge(t2t_ready, t - 1 + AHEAD)
                    nc.scalar.activation(x2T[:].rearrange("p t x -> p (t x)"), bank[6][:], ACT.Copy).then_inc(x2_copied, 1)
                if loaded is not None:
                    weights_hi(2, t - 1, 1 - par, loaded)

            def norm_image(t):
                sc.wait_ge(xt_ready, t + 1 + AHEAD)
                sc.sem_inc(held, 1)
                for h in range(HALVES):
                    j = 2 * t + (2 + h)
                    src = rows[:, bass.ds(j, 1), 0:C].rearrange("p a c -> p (a c)")
                    nb, rs = (ln1[:, bass.ds(j, 1), k:k + 1].rearrange("p a k -> p (a k)") for k in range(2))
                    nc.scalar.activation(xn[:, h, 0:C], src, ACT.Identity, scale=rs, bias=nb)
                    ins = nc.scalar.activation(xn[:, h, C:2 * CA], src[:, CA:C], ACT.Identity, scale=rs, bias=nb)
                ins.then_inc(xn_ready, 1)

            def guess_factors(lo, hi, n):
                sc.wait_ge(ln1_var, n)
                nc.scalar.activation(logs[:, lo:hi], ln1[:, lo:hi, 1], ACT.Ln, bias=eps_c[:, 0:1]).then_inc(ln1_log, 1)
                sc.wait_ge(ln1_log, n)
                nc.scalar.activation(guess[:, lo:hi], logs[:, lo:hi], ACT.Exp, scale=-0.5).then_inc(ln1_guess, 1)

            sc.preload_act_table_set("natural_log_exp_and_others")
            guess_factors(0, QUARTER, 1)
            sc.wait_ge(ln1_ready, 1)
            norm_image(-1)
            for t in range(3):
                step(t, t % 2, (t - 1) // 2 + 2 if t else None)
                if t == 0:
                    guess_factors(QUARTER, TILES, 2)
            with sc.Fori(1, IMAGES // 2 - 1) as i:
                for u in range(2):
                    step(2 * i + (u + 1), 1 - u, i + 2)
            for t in range(IMAGES - 1, IMAGES + 3):
                step(t, t % 2, (t - 1) // 2 + 2 if t < IMAGES else None)
            sc.wait_ge(pos_ready, IMAGES + AHEAD)
            for part in range(3):
                weights_hi(part, EXPERTS - 1, (CHUNKS + EXPERTS - 1) % 2, EXPERTS // 2 + 1)
            sc.preload_act_table(ACT.Silu)
            for s in (hh_ready, silu_ready, fh2_ready):
                sc.sem_inc(s, AHEAD)

            def ffn_step(j, par, back, mid, nxt):
                if back:
                    sc.wait_ge(gt_ready, j + AHEAD)
                    nc.scalar.activation(HH[:, 1 - par].rearrange("p k x -> p (k x)"), bank[5][:], ACT.Copy).then_inc(hh_ready, 1)
                if mid:
                    sc.wait_ge(h1_ready, j + 1 + AHEAD)
                    nc.scalar.activation(gh[:, par, 0:FE], bank[1 + 2 * par][:, 0:FE], ACT.Silu).then_inc(silu_ready, 1)
                if nxt:
                    sc.wait_ge(fxt_ready, j + 2 + AHEAD)
                    nc.scalar.activation(FH[:, 1 - par].rearrange("p t x -> p (t x)"), bank[0][:, 0:2 * P], ACT.Copy).then_inc(fh2_ready, 1)

            ffn_step(-1, 1, False, False, True)
            ffn_step(0, 0, False, True, True)
            ffn_step(1, 1, True, True, True)
            with sc.Fori(0, SLOTS // 4) as i:
                for u in range(4):
                    ffn_step(4 * i + (2 + u), u % 2, True, True, True)
            ffn_step(SLOTS - 1, 0, True, True, False)
            ffn_step(SLOTS, 1, True, False, False)

        @block.vector
        def _(ve):
            steps = [0]

            def link(ins):
                steps[0] += 1
                ins.then_inc(dve, 1)
                ve.wait_ge(dve, steps[0])

            nc.vector.memset(ones2[:].bitcast(F32), 1.0)
            nc.vector.memset(eps_c[:], EPS).then_inc(prep_ready, 1)
            def low_parts(hi, lo, raw, width):
                nc.vector.tensor_tensor(lo[:], raw[:, 0:width], hi[:, 0:width].bitcast(F32), ALU.subtract)
                return nc.vector.tensor_tensor(hi[CB:P, width:2 * width], raw[CB:P, width:2 * width],
                                               hi[CB:P, width:2 * width].bitcast(F32), ALU.subtract)

            n2 = IMAGES // 2

            def moments(h):
                at = slice(n2 * h, n2 * (h + 1))
                ve.wait_ge(cm_in[h], 16)
                for b in range(n2 * h, n2 * (h + 1)):
                    for t in range(2):
                        ins = nc.vector.bn_stats(gst[:, b, t], xcm[:, b, t])
                link(ins)
                st = gst[:, at].rearrange("p b t (e k) -> p (b t) e k", k=3)
                m = mq[:, at].rearrange("p b t e k -> p (b t) e k")
                s = msq[:, at].rearrange("p b t e -> p (b t) e")
                nc.vector.tensor_copy(m[:, :, :, 0], st[:, :, :, 1])
                link(nc.vector.tensor_tensor(s, st[:, :, :, 1], st[:, :, :, 1], ALU.mult))
                nc.vector.scalar_tensor_tensor(out=m[:, :, :, 1], in0=st[:, :, :, 2], scalar=2.0 / PIX, in1=s,
                                               op0=ALU.mult, op1=ALU.add).then_inc(gstat_in, 1)

            def group_factors(h):
                ve.wait_ge(gstat_ready, h + 1)
                g = bank[7][:, 8 * n2 * h:8 * n2 * (h + 1)].rearrange("p (t b e k) -> p t b e k", t=2, b=n2, e=2)
                link(nc.vector.tensor_copy(mv[:, h], g[:, :, :, 0]))
                link(nc.vector.tensor_tensor(mv[:, h], mv[:, h], g[:, :, :, 1], ALU.add))
                link(nc.vector.tensor_tensor(gvar[:, h], mv[:, h, :, :, 0], mv[:, h, :, :, 0], ALU.mult))
                nc.vector.tensor_tensor(gvar[:, h], mv[:, h, :, :, 1], gvar[:, h], ALU.subtract).then_inc(gvar_ready, 1)
                ve.wait_ge(gstd_ready, h + 1)
                link(nc.vector.reciprocal(grs[:, h], grs[:, h]))
                nc.vector.scalar_tensor_tensor(out=gnb[:, h], in0=mv[:, h, :, :, 0], scalar=-1.0, in1=grs[:, h],
                                               op0=ALU.mult, op1=ALU.mult).then_inc(gnorm_ready, 1)

            moments(0)
            link(nc.vector.memset(bias2[:].bitcast(F32), 0.0))
            ve.wait_ge(small1_in, 16)
            r4 = c1("rows").rearrange("p (r c) -> p r c", r=4)
            link(nc.vector.tensor_copy(bias2[0:1, :], r4[0:1, 0]))
            link(nc.vector.tensor_copy(bias2[32:33, :], r4[32:33, 0]))
            link(nc.vector.tensor_tensor(bias2[32:33, :], r4[32:33, 0], bias2[32:33, :].bitcast(F32), ALU.subtract))
            link(nc.vector.tensor_tensor(wsum[:], r4[:, 1], r4[:, 2], ALU.add))
            link(nc.vector.tensor_tensor(wsum[:], wsum[:], r4[:, 3], ALU.add))
            ve.wait_ge(wsplit_hi, 1)
            low_parts(cfH, cfL, c1("cf"), C).then_inc(small_split, 1)
            group_factors(0)
            moments(1)
            for s in (fl_ready, fq_ready, conv_taken, gram_taken):
                ve.sem_inc(s, AHEAD)
            def split_image(b, par):
                ve.wait_ge(fh_ready, b + 1 + AHEAD)
                nc.vector.tensor_tensor(f2[:, par, :, 1], f32t[:, par], f2[:, par, :, 0].bitcast(F32), ALU.subtract).then_inc(fl_ready, 1)
                ve.wait_ge(fl_ready, b + 1 + AHEAD)
                nc.vector.tensor_copy(fQ[CB:P, par], f2[CB:P, par, 1, 1].bitcast(F32)).then_inc(fq_ready, 1)

            def take_conv(b, par):
                ve.wait_ge(conv_ready, b + 1 + AHEAD)
                dst = rows[:, bass.ds(b * HALVES, HALVES), 0:C]
                ve.wait_ge(tm_in, 16)
                nc.vector.tensor_tensor(dst, bank[par][:, 0:HALVES * C].rearrange("p (h c) -> p h c", c=C), dst, ALU.add).then_inc(conv_taken, 1)

            def take_gram(b, par):
                ve.wait_ge(gram_half, b + 1)
                for h in range(HALVES):
                    ins = nc.vector.tensor_tensor(gram[:, b, h], gram[:, b, h], bank[2 + 2 * par + h][:, NEAR:2 * NEAR], ALU.add)
                ins.then_inc(gram_taken, 1)
                ve.wait_ge(gram_taken, b + 1 + AHEAD)
                ve.wait_ge(small2_in, 16)
                for h in range(HALVES):
                    at = h * (NEAR - P)
                    ins = nc.vector.tensor_tensor_reduce(out=gs[:, 0, 0:P], in0=gram[:, b, h, at:at + P], in1=ident, scale=1.0, scalar=0.0,
                                                         op0=ALU.mult, op1=ALU.add, accum_out=ssq[:, 2 * b + h:2 * b + h + 1])
                    ins.then_inc(diag_read, 1)
                    ve.wait_ge(diag_read, 2 * b + h + 1)

            for b in range(2):
                split_image(b, b)
            group_factors(1)
            for i in range(IMAGES // 2 - 1):
                for par in range(2):
                    take_conv(2 * i + par, par)
                    split_image(2 * i + 2 + par, par)
                    take_gram(2 * i + par, par)
            for b in (IMAGES - 2, IMAGES - 1):
                take_conv(b, b % 2)
                take_gram(b, b % 2)

            ve.sem_inc(ssq_ready, 1)
            ve.wait_ge(nrm_ready, 1)
            link(nc.vector.tensor_scalar(rn[:], rn[:], EPS_NORM, None, ALU.max))
            nc.vector.reciprocal(rn[:], rn[:]).then_inc(rn_ready, 1)
            ve.wait_ge(rn_ready, 1)
            link(nc.vector.tensor_tensor(cc[:], ssq[:], rn[:], ALU.mult))
            nc.vector.tensor_tensor(cc[:], cc[:], rn[:], ALU.mult).then_inc(cc_ready, 1)
            ve.wait_ge(rt_ready, 1)
            nc.vector.tensor_copy(rT[:], bank[7][0:TILES, 0:P]).then_inc(rt_copied, 1)
            ve.wait_ge(rwin_ready, 1)
            link(nc.vector.tensor_copy(rwin[:].rearrange("q b k -> q k b"), bank[5][:, 0:WINDOWS].rearrange("q (k b) -> q k b", b=IMAGES)))

            def scale_gram(c):
                if c >= 2:
                    ve.wait_ge(gsl_ready, c - 1)
                nc.vector.tensor_tensor(gs[:, c % 2].rearrange("q (c w) -> q w c", w=WINDOWS),
                                        around[:].rearrange("q b k c -> q (b k) c")[:, :, CHUNK * c:CHUNK * (c + 1)],
                                        rwin[:].rearrange("q b k -> q (b k)").rearrange("q (w a) -> q w a", a=1).to_broadcast([P, WINDOWS, CHUNK]),
                                        ALU.mult).then_inc(gs_ready, 1)
                ve.wait_ge(gsh_ready, c + 1)
                nc.vector.tensor_tensor(gsL[:, c % 2], gs[:, c % 2], gsH[:, c % 2].bitcast(F32), ALU.subtract).then_inc(gsl_ready, 1)

            def take_class(c):
                ve.wait_ge(class_ready, c + 1)
                if c >= 2:
                    ve.wait_ge(corr_out[c % 2], 16 * (c // 2))
                for q in range(CHUNK // 4):
                    a = CHUNK * c + 2 * q
                    ins = nc.vector.tensor_tensor(co[:, c % 2, 2 * q:2 * q + 2], bank[4 * (c % 2) + q][0:WINDOWS, 0:2 * C].rearrange("w (a c) -> w a c", a=2),
                                                  rbk[:, a:a + 2].rearrange("w (a c) -> w a c", c=1).to_broadcast([WINDOWS, 2, C]), ALU.mult)
                ins.then_inc(co_ready, 1)

            ve.wait_ge(cc_ready, 1)

            for j in range(TILES):
                ins = nc.vector.scalar_tensor_tensor(out=rows[:, j, 0:C], in0=wsum[:], scalar=cc[:, j:j + 1], in1=rows[:, j, 0:C],
                                                     op0=ALU.mult, op1=ALU.add)
            link(ins)
            for s in windows_in:
                ve.wait_ge(s, 16 * len(pieces))
            scale_gram(0)
            ve.wait_ge(rbk_in, 16 * (P // PAIR))
            ve.wait_ge(m_split, 2)
            low_parts(mH, mL, bank[6], 2 * CA)
            low_parts(vwH, vwL, c1("wv"), C).then_inc(attn_split, 1)

            for c in range(CHUNKS):
                if c + 1 < CHUNKS:
                    scale_gram(c + 1)
                take_class(c)

            def add_corr(q):
                ve.wait_ge(corr_in[q], 16)
                at = slice(QUARTER * q, QUARTER * (q + 1))
                nc.vector.tensor_tensor(rows[:, at, 0:C], rows[:, at, 0:C], corr_sb[:, at], ALU.add).then_inc(corr_added, 1)

            add_corr(0)

            ve.wait_ge(empty_out, 16 * (EXPERTS + 1))
            for s in (var_ready, o_taken, xn2_ready, xl_ready, max_ready, ul_ready, oh_ready, t2_ready, pos_ready):
                ve.sem_inc(s, AHEAD)
            ve.wait_ge(small2_in, 16)
            nc.vector.tensor_copy(tri_sb[:], c2("tri"))
            nc.vector.tensor_copy(run[:], c2("base"))

            LINKS = 19

            def hold():
                ve.sem_inc(held, 1)


            def newton(link, x, y, to, t):
                link(nc.vector.tensor_tensor(t, y, y, ALU.mult))
                link(nc.vector.scalar_tensor_tensor(out=t, in0=t, scalar=-0.5, in1=x, op0=ALU.mult, op1=ALU.mult))
                return nc.vector.scalar_tensor_tensor(out=to, in0=t, scalar=1.5, in1=y, op0=ALU.add, op1=ALU.mult)

            def token_stats(lo, hi):
                for j in range(lo, hi):
                    ins = nc.vector.bn_stats(tstat[:, j], rows[:, j, 0:C])
                link(ins)
                for j in range(lo, hi):
                    ins = nc.vector.bn_aggr(ln1[:, j], tstat[:, j])
                ins.then_inc(ln1_var, 1)

            def token_factors(lo, hi, n):
                x, t, y = newt[:, 0, lo:hi], newt[:, 1, lo:hi], ln1[:, lo:hi, 1]
                ve.wait_ge(ln1_var, n)
                link(nc.vector.tensor_scalar(x, y, EPS, None, ALU.add))
                ve.wait_ge(ln1_guess, n)
                link(newton(link, x, guess[:, lo:hi], y, t))
                nc.vector.scalar_tensor_tensor(out=ln1[:, lo:hi, 0], in0=ln1[:, lo:hi, 0], scalar=-1.0, in1=y,
                                               op0=ALU.mult, op1=ALU.mult).then_inc(ln1_ready, 1)

            ve.wait_ge(corr_added, 1)
            token_stats(0, QUARTER)
            token_factors(0, QUARTER, 1)
            for q in range(1, 4):
                add_corr(q)
            ve.wait_ge(corr_added, 4)

            def step(t, par, weights=True):
                done = [0]

                def link(ins):
                    done[0] += 1
                    ins.then_inc(dve2, 1)
                    ve.wait_ge(dve2, LINKS * t + done[0])

                wide = [P, HALVES, EXPERTS]
                if on(t, 2):
                    ve.wait_ge(o_ready, t - 1 + AHEAD)
                    link(nc.vector.reciprocal(rsum[:], ssum[:]))
                if on(t, 0):
                    ve.wait_ge(xh_ready, t + 1 + AHEAD)
                    nc.vector.tensor_tensor(XL[:, par].rearrange("p t x -> p (t x)"), bank[0][:],
                                            XH[:, par].rearrange("p t x -> p (t x)").bitcast(F32), ALU.subtract).then_inc(xl_ready, 1)
                if isinstance(t, int) and t == 0:
                    token_stats(QUARTER, TILES)
                if on(t, 1):
                    ve.wait_ge(s_ready, t + AHEAD)
                    hold()
                    nc.vector.tensor_tensor_reduce(out=sc_sb[:, 0:P], in0=bank[3][:, 0:P], in1=c2("mask")[:, 0:P], scale=1.0, scalar=NEG,
                                                   op0=ALU.add, op1=ALU.max, accum_out=smx[:, 0:1])
                    link(nc.vector.tensor_tensor_reduce(out=sc_sb[:, P:3 * P], in0=bank[3][:, P:3 * P], in1=c2("mask")[:, P:3 * P], scale=1.0,
                                                        scalar=NEG, op0=ALU.add, op1=ALU.max, accum_out=smx[:, 1:2]))
                    nc.vector.tensor_scalar(nmx[:], smx[:], -SM_SCALE, None, ALU.mult).then_inc(max_ready, 1)
                if on(t, 2):
                    for h in range(HALVES):
                        row = rows[:, bass.ds(2 * t + (h - 4), 1), 0:C].rearrange("p a c -> p (a c)")
                        ins = nc.vector.scalar_tensor_tensor(out=row, in0=bank[5][:, C * h:C * (h + 1)], scalar=rsum[:, h:h + 1], in1=row,
                                                             op0=ALU.mult, op1=ALU.add)
                    ins.then_inc(o_taken, 1)
                    ve.wait_ge(o_taken, t - 1 + AHEAD)
                    hold()
                    for h in range(HALVES):
                        ins = nc.vector.bn_stats(tstat[:, h], rows[:, bass.ds(2 * t + (h - 4), 1), 0:C].rearrange("p a c -> p (a c)"))
                    link(ins)
                    hold()
                    for h in range(HALVES):
                        ins = nc.vector.bn_aggr(ln2[:, h], tstat[:, h])
                    ins.then_inc(var_ready, 1)
                if on(t, 0):
                    ve.wait_ge(uh_ready, t + 1 + AHEAD)
                    nc.vector.tensor_tensor(uAl[:, par], bank[1][:, 0:PIX], UH[:, par, 0].bitcast(F32), ALU.subtract)
                    nc.vector.tensor_tensor(UH[CB:P, par, 1], bank[1][CB:P, PIX:2 * PIX], UH[CB:P, par, 1].bitcast(F32), ALU.subtract).then_inc(ul_ready, 1)
                if on(t, 2):
                    ve.wait_ge(var_ready, t - 1 + AHEAD)
                    link(nc.vector.tensor_scalar(newt[:, 0, 0:2], ln2[:, :, 1], EPS, None, ALU.add))
                    ve.wait_ge(rs_ready, t - 1 + AHEAD)
                    link(newton(link, newt[:, 0, 0:2], rs0[:], ln2[:, :, 1], newt[:, 1, 0:2]))
                    hold()
                    nc.vector.tensor_copy(rows[:, bass.ds(2 * t - 4, 2), C:C + 2], ln2[:]).then_inc(t2_ready, 1)
                    ve.wait_ge(t2t_ready, t - 2 + AHEAD)
                    for h in range(HALVES):
                        row = rows[:, bass.ds(2 * t + (h - 4), 1), 0:C].rearrange("p a c -> p (a c)")
                        ins = nc.vector.tensor_scalar(xn2[:, h], row, ln2[:, h, 0:1], ln2[:, h, 1:2], ALU.subtract, ALU.mult)
                    ins.then_inc(xn2_ready, 1)
                if on(t, 3):
                    ve.wait_ge(g_ready, t - 2 + AHEAD)
                    desc = c2("desc").rearrange("p (h e) -> p h e", h=2)
                    link(nc.vector.tensor_tensor(lg[:], bank[7][:, 0:2 * EXPERTS].rearrange("p (h e) -> p h e", h=2),
                                                 c2("bg").rearrange("p (h e) -> p h e", h=2), ALU.add))
                    link(nc.vector.tensor_reduce(gmx[:], lg[:], AX_X, ALU.max))
                    link(nc.vector.tensor_tensor(lg[:], lg[:], gmx[:].rearrange("p (h a) -> p h a", a=1).to_broadcast(wide), ALU.is_ge))
                    link(nc.vector.tensor_tensor(lg[:], lg[:], desc, ALU.mult))
                    link(nc.vector.tensor_reduce(gmx[:], lg[:], AX_X, ALU.max))
                    nc.vector.tensor_tensor(oh[:], lg[:], gmx[:].rearrange("p (h a) -> p h a", a=1).to_broadcast(wide), ALU.is_equal).then_inc(oh_ready, 1)
                if weights:
                    ve.wait_ge(wall_hi, t - 1)
                    w = wall[CB:P, bass.ds(t - 2, 1), 2 * W12:3 * W12].rearrange("p a c -> p (a c)")
                    nc.vector.tensor_tensor(w, stage[CB:P, par, W12:2 * W12], w.bitcast(F32), ALU.subtract).then_inc(wall_q, 1)
                if on(t, 3):
                    ve.wait_ge(pf_ready, t - 2 + AHEAD)
                    r1 = run[:].rearrange("p (h e) -> p h e", h=1).to_broadcast(wide)
                    link(nc.vector.tensor_tensor(lg[:], bank[7][:, 2 * EXPERTS:4 * EXPERTS].rearrange("p (h e) -> p h e", h=2), r1, ALU.add))
                    link(nc.vector.tensor_tensor(lg[:], lg[:], oh[:], ALU.mult))
                    nc.vector.tensor_tensor(run[:], run[:], bank[7][:, 4 * EXPERTS:5 * EXPERTS], ALU.add)
                    link(nc.vector.tensor_reduce(pos[:], lg[:], AX_X, ALU.add))
                    hold()
                    nc.vector.tensor_copy(posi[:, bass.ds(2 * t - 6, 2)], pos[:]).then_inc(pos_ready, 1)
                if done[0] < LINKS:
                    ve.sem_inc(dve2, LINKS - done[0])
                assert done[0] <= LINKS

            for t in range(3):
                step(t, t % 2, t > 1)
                if t == 0:
                    token_factors(QUARTER, TILES, 2)
            with ve.Fori(1, IMAGES // 2 - 1) as i:
                for u in range(2):
                    step(2 * i + (u + 1), 1 - u)
            for t in range(IMAGES - 1, IMAGES + 3):
                step(t, t % 2, t <= IMAGES)
            ve.wait_ge(pos_ready, IMAGES + AHEAD)
            link(nc.vector.scalar_tensor_tensor(out=tiles_i[:], in0=run[:], scalar=float(P - 1), in1=c2("base"), op0=ALU.add, op1=ALU.subtract))
            link(nc.vector.tensor_scalar(tiles_i[:], tiles_i[:], P.bit_length() - 1, None, ALU.logical_shift_right))
            nc.vector.tensor_copy(tiles_f[:], tiles_i[:])
            link(nc.vector.tensor_copy(ends[:, 0], tiles_i[:]))
            for n, d in enumerate((1, 2, 4)):
                a, z = n % 2, 1 - n % 2
                nc.vector.tensor_copy(ends[:, z, 0:d], ends[:, a, 0:d])
                link(nc.vector.tensor_tensor(ends[:, z, d:EXPERTS], ends[:, a, d:EXPERTS], ends[:, a, 0:EXPERTS - d], ALU.add))
            starts = ends[:, 0]
            link(nc.vector.tensor_tensor(starts, ends[:, 1], tiles_f[:], ALU.subtract))
            wide = [P, SLOTS, EXPERTS]
            slot = c2("slot")[:, 0:SLOTS]
            slot3 = slot.rearrange("p (j a) -> p j a", a=1).to_broadcast(wide)

            def over_slots(v):
                return v.rearrange("p (a e) -> p a e", a=1).to_broadcast(wide)

            nc.vector.tensor_scalar(per_slot[:, 2], slot, ends[:, 1, EXPERTS - 1:EXPERTS], float(EMPTY), ALU.is_ge, ALU.mult)
            nc.vector.scalar_tensor_tensor(out=tiles_f[:], in0=starts, scalar=float(P), in1=run[:], op0=ALU.mult, op1=ALU.add)
            link(nc.vector.tensor_tensor(started[:], slot3, over_slots(starts), ALU.is_ge))
            link(nc.vector.tensor_tensor(picked[:], started[:], over_slots(tiles_f[:]), ALU.mult))
            link(nc.vector.tensor_reduce(per_slot[:, 1], picked[:], AX_X, ALU.max))
            nc.vector.tensor_reduce(per_slot[:, 0], started[:], AX_X, ALU.add)
            link(nc.vector.scalar_tensor_tensor(out=per_slot[:, 1], in0=c2("slot")[:, 1:SLOTS + 1], scalar=-float(P), in1=per_slot[:, 1],
                                                op0=ALU.mult, op1=ALU.add))
            nc.vector.tensor_scalar(slot_expert[:], per_slot[:, 0], -1.0, None, ALU.add)
            nc.vector.tensor_tensor(slot_row[:], per_slot[:, 1], per_slot[:, 2], ALU.max).then_inc(table_ready, 1)
            nc.vector.memset(gh[:, :, FE:FT * P], 0.0)
            ve.wait_ge(wall_hi, EXPERTS)
            raw, w = stage[:, (CHUNKS + EXPERTS - 1) % 2], wall[:, EXPERTS - 1]
            nc.vector.tensor_tensor(w[CB:P, 2 * W12:3 * W12], raw[CB:P, W12:2 * W12], w[CB:P, 2 * W12:3 * W12].bitcast(F32), ALU.subtract).then_inc(wall_q, 1)
            for s in (fx_ready, fl2_ready, gh_ready, hl_ready, y_taken):
                ve.sem_inc(s, AHEAD)

            def norm_slot(j, par, loaded):
                ve.wait_ge(slot_in[par], 16 * loaded)
                ve.wait_ge(fxt_ready, j + AHEAD)
                row = rows[:, bass.ds(j, 1), :].rearrange("p a c -> p (a c)")
                mean, rs = row[:, C:C + 1], row[:, C + 1:C + 2]
                nc.vector.tensor_scalar(xf[:, 0:C], row[:, 0:C], mean, rs, ALU.subtract, ALU.mult)
                nc.vector.tensor_scalar(xf[:, C:2 * CA], row[:, CA:C], mean, rs, ALU.subtract, ALU.mult).then_inc(fx_ready, 1)

            def ffn_step(j, par, back, mid, nxt, after=None):
                if back:
                    ve.wait_ge(hh_ready, j + AHEAD)
                    nc.vector.tensor_tensor(HL[:, 1 - par].rearrange("p k x -> p (k x)"), bank[5][:],
                                            HH[:, 1 - par].rearrange("p k x -> p (k x)").bitcast(F32), ALU.subtract).then_inc(hl_ready, 1)
                if mid:
                    ve.wait_ge(h_ready, j + 1 + AHEAD)
                    ve.wait_ge(silu_ready, j + 1 + AHEAD)
                    nc.vector.tensor_tensor(gh[:, par, 0:FE], gh[:, par, 0:FE], bank[2 + 2 * par][:, 0:FE], ALU.mult).then_inc(gh_ready, 1)
                if nxt:
                    ve.wait_ge(fh2_ready, j + 2 + AHEAD)
                    nc.vector.tensor_tensor(FL[:, 1 - par].rearrange("p t x -> p (t x)"), bank[0][:, 0:2 * P],
                                            FH[:, 1 - par].rearrange("p t x -> p (t x)").bitcast(F32), ALU.subtract).then_inc(fl2_ready, 1)
                if after is not None:
                    norm_slot(j + 2, par, after)
                if back:
                    y = bank[7 - par]
                    ve.wait_ge(y_ready, j + AHEAD)
                    ve.wait_ge(yo_free, j - 2 + AHEAD)
                    row = rows[:, bass.ds(j - 1, 1), 0:C].rearrange("p a c -> p (a c)")
                    nc.vector.tensor_tensor(yo[:, 1 - par], y[:, C:2 * C], row, ALU.add).then_inc(dve3, 1)
                    ve.wait_ge(dve3, j)
                    nc.vector.tensor_tensor(yo[:, 1 - par], yo[:, 1 - par], y[:, 0:C], ALU.add).then_inc(y_taken, 1)

            norm_slot(0, 0, 1)
            ffn_step(-1, 1, False, False, True, 1)
            ffn_step(0, 0, False, True, True, 2)
            ffn_step(1, 1, True, True, True, 2)
            with ve.Fori(0, SLOTS // 4 - 1) as i:
                for u in range(4):
                    ffn_step(4 * i + (2 + u), u % 2, True, True, True, 2 * i + (3 + u // 2))
            for j in range(SLOTS - 5, SLOTS - 1):
                ffn_step(j, j % 2, True, True, True, j // 2 + 2 if j + 2 < SLOTS else None)
            ffn_step(SLOTS - 1, 0, True, True, False)
            ffn_step(SLOTS, 1, True, False, False)

        @block.tensor
        def _(pe):
            n2 = IMAGES // 2
            gm = c1("gm").rearrange("p (t n) -> p t n", t=2)
            pe.wait_ge(group_in, 16)
            for h in range(2):
                pe.wait_ge(gstat_in, h + 1)
                for m in range(2):
                    for t, k in ((0, P), (1, CB)):
                        mm = nc.tensor.matmul(bank[7][:, 8 * n2 * h + 4 * n2 * m:8 * n2 * h + 4 * n2 * (m + 1)], gm[0:k, t, CA * m:CA * (m + 1)],
                                              mq[0:k, n2 * h:n2 * (h + 1), t, :, :].rearrange("p b e k -> p b (e k)"), start=(t == 0), stop=(t == 1))
                mm.then_inc(gstat_ready, 1)

            for s in (conv_ready, gram_ready):
                pe.sem_inc(s, AHEAD)
            pe.wait_ge(small_split, 1)

            def products(dst, xh_a, xl_a, xh_b, xl_b, y_a, yl_a, y_q, y_q64, more=False):
                nc.tensor.matmul(dst, xh_a, y_a, start=True, stop=False)
                nc.tensor.matmul(dst, xh_a, yl_a, start=False, stop=False)
                nc.tensor.matmul(dst, xl_a, y_a, start=False, stop=False)
                nc.tensor.matmul(dst, xh_b, y_q, start=False, stop=False)
                return nc.tensor.matmul(dst, xl_b, y_q64, start=False, stop=not more)

            with pe.Fori(0, IMAGES // 2) as i:
                for par in range(2):
                    pe.wait_ge(fq_ready, 2 * i + (par + 1 + AHEAD))
                    pe.wait_ge(conv_taken, 2 * i + (par - 1 + AHEAD))
                    for h in range(HALVES):
                        t = slice(P * h, P * (h + 1))
                        dst = bank[par][:, C * h:C * (h + 1)]
                        products(dst, f2[:, par, 0, 0, t], f2[:, par, 0, 1, t], f2[:, par, 1, 0, t], f2[0:CB, par, 1, 1, t],
                                 cfH[:, 0:C], cfL[:, :], cfH[:, C:2 * C], cfH[0:CB, C:2 * C], more=True)
                        mm = nc.tensor.matmul(dst, ones2[:], bias2[:], start=False, stop=True)
                    mm.then_inc(conv_ready, 1)
                    pe.wait_ge(gram_taken, 2 * i + (par - 1 + AHEAD))
                    for h in range(HALVES):
                        q, p = slice(P * h, P * (h + 1)), slice((PIX - NEAR) * h, (PIX - NEAR) * h + NEAR)
                        dst = bank[2 + 2 * par + h][:, 0:2 * NEAR]
                        nc.tensor.matmul(dst, f2[:, par, 0, 0, q], f2[:, par, 0, :, p], start=True, stop=False)
                        nc.tensor.matmul(dst, f2[:, par, 0, 1, q], f2[:, par, 0, :, p], start=False, stop=False)
                        mm = nc.tensor.matmul(dst, fQ[:, par, q], f2[:, par, 1, :, p], start=False, stop=True)
                    mm.then_inc(gram_ready, 1)

            pe.wait_ge(rn_ready, 1)
            pe.wait_ge(small2_in, 16)
            nc.tensor.transpose(bank[7][0:TILES, 0:P], rn[:], ident).then_inc(rt_ready, 1)
            rnv = rn[:].rearrange("p (b h) -> p h b", h=HALVES)
            wide = bank[5][:, 0:WINDOWS].rearrange("q (k b) -> q k b", b=IMAGES)
            step = P // PAIR
            for d, h0, h1 in [(d, 0, 2) for d in range(step)] + [(d, 1, 2) for d in (-2, -1)] + [(d, 0, 1) for d in (step, step + 1)]:
                off = SHIFT0 + PAIR * d - PAD_PIX
                k0 = d + step * h0
                mm = nc.tensor.matmul(wide[:, k0:k0 + step * (h1 - h0 - 1) + 1:step], c1("shift")[:, off:off + P], rnv[:, h0:h1],
                                      start=(d == 0), stop=(d == step + 1))
            mm.then_inc(rwin_ready, 1)
            pe.wait_ge(attn_in, 16)
            wq, wk = (c1(n).rearrange("p (t n) -> p t n", t=2) for n in ("wq", "wk"))
            for m in range(2):
                for t, k in ((0, P), (1, CB)):
                    mm = nc.tensor.matmul(bank[6][:, 2 * CA * m:2 * CA * (m + 1)], wq[0:k, t, CA * m:CA * (m + 1)], wk[0:k, t, :], start=(t == 0), stop=(t == 1))
            mm.then_inc(m_ready, 1)
            pe.wait_ge(stage_free, CHUNKS)
            for c in range(CHUNKS):
                pe.wait_ge(gsl_ready, c + 1)
                if c == 1:
                    pe.wait_ge(gs_ready, 1)
                    pe.wait_ge(attn_split, 1)
                if c >= 2:
                    pe.wait_ge(co_ready, c - 1)
                    pe.wait_ge(co_high, c - 1)
                for a in range(CHUNK):
                    dst = bank[4 * (c % 2) + a // 2][0:WINDOWS, C * (a % 2):C * (a % 2 + 1)]
                    w = slice(WINDOWS * a, WINDOWS * (a + 1))
                    n = slice(C * (CHUNK * c + a), C * (CHUNK * c + a + 1))
                    nc.tensor.matmul(dst, gsH[:, c % 2, w], bandH[:, n], start=True, stop=False)
                    nc.tensor.matmul(dst, gsH[:, c % 2, w], bandL[:, n], start=False, stop=False)
                    mm = nc.tensor.matmul(dst, gsL[:, c % 2, w], bandH[:, n], start=False, stop=True)
                mm.then_inc(class_ready, 1)

            pe.wait_ge(co_ready, CHUNKS)
            pe.wait_ge(co_high, CHUNKS)
            pe.wait_ge(corr_added, 1)
            for s in (xt_ready, u_ready, v_ready, s_ready, pt_ready, o_ready, t2t_ready, g_ready, pf_ready):
                pe.sem_inc(s, AHEAD)

            def step(t, par):
                old = 1 - par
                if on(t, 1):
                    pe.wait_ge(ul_ready, t + AHEAD)
                    pe.wait_ge(max_ready, t - 1 + AHEAD)
                    for h in range(HALVES):
                        q, k = slice(P * h, P * (h + 1)), slice(0, P * (h + 1))
                        dst = bank[3][:, P * h:P * h + P * (h + 1)]
                        xh_a, xl_a, xh_b, xl_b = XH[:, old, 0, k], XL[:, old, 0, k], XH[:, old, 1, k], XL[0:CB, old, 1, k]
                        nc.tensor.matmul(dst, UH[:, old, 0, q], xh_a, start=True, stop=False)
                        nc.tensor.matmul(dst, UH[:, old, 0, q], xl_a, start=False, stop=False)
                        nc.tensor.matmul(dst, uAl[:, old, q], xh_a, start=False, stop=False)
                        nc.tensor.matmul(dst, UH[:, old, 1, q], xh_b, start=False, stop=False)
                        mm = nc.tensor.matmul(dst, UH[0:CB, old, 1, q], xl_b, start=False, stop=True)
                    mm.then_inc(s_ready, 1)
                if on(t, 0):
                    pe.wait_ge(xl_ready, t + 1 + AHEAD)
                    pe.wait_ge(ul_ready, t + AHEAD)
                    for m in range(2):
                        dst = bank[1][:, PIX * m:PIX * (m + 1)]
                        c = slice(CA * m, CA * (m + 1))
                        q = slice(2 * CA + CA * m, 2 * CA + CA * (m + 1))
                        nc.tensor.matmul(dst, mH[:, c], XH[:, par, 0], start=True, stop=False)
                        nc.tensor.matmul(dst, mH[:, c], XL[:, par, 0], start=False, stop=False)
                        nc.tensor.matmul(dst, mL[:, c], XH[:, par, 0], start=False, stop=False)
                        nc.tensor.matmul(dst, mH[:, q], XH[:, par, 1], start=False, stop=False)
                        mm = nc.tensor.matmul(dst, mH[0:CB, q], XL[0:CB, par, 1], start=False, stop=True)
                    mm.then_inc(u_ready, 1)
                if on(t, 1):
                    pe.wait_ge(exp_ready, t + AHEAD)
                    pe.wait_ge(pt_copied, t - 1 + AHEAD)
                    for k in range(3):
                        mm = nc.tensor.transpose(bank[4][:, P * k:P * (k + 1)], Pr[:, P * k:P * (k + 1)], ident)
                    mm.then_inc(pt_ready, 1)
                if on(t, 0):
                    pe.wait_ge(v_copied, t + AHEAD)
                    for h in range(HALVES):
                        q = slice(P * h, P * (h + 1))
                        mm = products(bank[2][:, C * h:C * (h + 1)], XH[:, par, 0, q], XL[:, par, 0, q], XH[:, par, 1, q], XL[0:CB, par, 1, q],
                                      vwH[:, 0:C], vwL[:], vwH[:, C:2 * C], vwH[0:CB, C:2 * C])
                    mm.then_inc(v_ready, 1)
                if on(t, 3):
                    pe.wait_ge(x2_copied, t - 2 + AHEAD)
                    pe.wait_ge(pos_ready, t - 3 + AHEAD)
                    wg = c2("wg")
                    for h in range(HALVES):
                        dst = bank[7][:, EXPERTS * h:EXPERTS * (h + 1)]
                        nc.tensor.matmul(dst, x2T[:, 0, P * h:P * (h + 1)], wg[:, 0:EXPERTS], start=True, stop=False)
                        mm = nc.tensor.matmul(dst, x2T[CB:P, 1, P * h:P * (h + 1)], wg[CB:P, EXPERTS:2 * EXPERTS], start=False, stop=True)
                    mm.then_inc(g_ready, 1)
                if on(t, 1):
                    pe.wait_ge(pt_copied, t + AHEAD)
                    pe.wait_ge(v_copied, t + AHEAD)
                    pe.wait_ge(o_taken, t - 1 + AHEAD)
                    nc.tensor.matmul(bank[5][:, 0:C], PT[:, 0:P], V[:, old, 0], start=True, stop=True)
                    nc.tensor.matmul(bank[5][:, C:2 * C], PT[:, P:2 * P], V[:, old, 0], start=True, stop=False)
                    nc.tensor.matmul(bank[5][:, C:2 * C], PT[:, 2 * P:3 * P], V[:, old, 1], start=False, stop=True).then_inc(o_ready, 1)
                if on(t, 2):
                    pe.wait_ge(xn2_ready, t - 1 + AHEAD)
                    pe.wait_ge(x2_copied, t - 2 + AHEAD)
                    for part in range(2):
                        for h in range(HALVES):
                            at = PIX * part + P * h
                            mm = nc.tensor.transpose(bank[6][:, at:at + P], xn2[:, h, CB * part:CB * part + P], ident)
                    mm.then_inc(t2t_ready, 1)
                if on(t, -1):
                    pe.wait_ge(xn_ready, t + 2 + AHEAD)
                    pe.wait_ge(xl_ready, t + 1 + AHEAD)
                    for part in range(2):
                        for h in range(HALVES):
                            at = PIX * part + P * h
                            mm = nc.tensor.transpose(bank[0][:, at:at + P], xn[:, h, CA * part:CA * (part + 1)], ident)
                    mm.then_inc(xt_ready, 1)
                if on(t, 3):
                    pe.wait_ge(oh_ready, t - 2 + AHEAD)
                    before, all_ = tri_sb[:, 0:P], tri_sb[:, P:2 * P]
                    e = 2 * EXPERTS
                    nc.tensor.matmul(bank[7][:, e:e + EXPERTS], before, oh[:, 0], start=True, stop=True)
                    e += EXPERTS
                    nc.tensor.matmul(bank[7][:, e:e + EXPERTS], before, oh[:, 1], start=True, stop=False)
                    nc.tensor.matmul(bank[7][:, e:e + EXPERTS], all_, oh[:, 0], start=False, stop=True)
                    e += EXPERTS
                    nc.tensor.matmul(bank[7][:, e:e + EXPERTS], all_, oh[:, 0], start=True, stop=False)
                    nc.tensor.matmul(bank[7][:, e:e + EXPERTS], all_, oh[:, 1], start=False, stop=True).then_inc(pf_ready, 1)

            for t in range(-1, 3):
                step(t, t % 2)
            with pe.Fori(1, IMAGES // 2 - 1) as i:
                for u in range(2):
                    step(2 * i + (u + 1), 1 - u)
            for t in range(IMAGES - 1, IMAGES + 3):
                step(t, t % 2)
            for s in (fxt_ready, h1_ready, h_ready, gt_ready, y_ready):
                pe.sem_inc(s, AHEAD)

            def ffn_step(j, par, back, mid, nxt, w_back=None):
                def expert(j):
                    pe.wait_ge(table_ready, 1)
                    e = pe.value_load(slot_expert[0:1, bass.ds(j, 1)], min_val=0, max_val=EXPERTS - 1)

                    def cols(p0, p1, c0, c1):
                        return wall[p0:p1, bass.ds(e, 1), c0:c1].rearrange("p a c -> p (a c)")
                    return cols

                if back and w_back is None:
                    w_back = expert(j - 1)
                w_mid = expert(j) if mid else None
                if back:
                    pe.wait_ge(gh_ready, j + AHEAD)
                    for k in range(FT):
                        mm = nc.tensor.transpose(bank[5][:, P * k:P * (k + 1)], gh[:, 1 - par, P * k:P * (k + 1)], ident)
                    mm.then_inc(gt_ready, 1)
                if mid:
                    w = w_mid
                    pe.wait_ge(fl2_ready, j + 1 + AHEAD)
                    for m in range(2):
                        dst = bank[1 + 2 * par + m][:, 0:FE]
                        a, q = FE * m, 2 * W12 + FE * m
                        mm = products(dst, FH[:, par, 0], FL[:, par, 0], FH[:, par, 1], FL[0:CB, par, 1],
                                      w(0, P, a, a + FE), w(0, P, W12 + a, W12 + a + FE), w(0, P, q, q + FE), w(0, CB, q, q + FE))
                        mm.then_inc((h1_ready, h_ready)[m], 1)
                if nxt:
                    pe.wait_ge(fx_ready, j + 2 + AHEAD)
                    pe.wait_ge(fl2_ready, j + 1 + AHEAD)
                    for part in range(2):
                        mm = nc.tensor.transpose(bank[0][:, P * part:P * (part + 1)], xf[:, CA * part:CA * (part + 1)], ident)
                    mm.then_inc(fxt_ready, 1)
                if back:
                    w = w_back
                    pe.wait_ge(hl_ready, j + AHEAD)
                    pe.wait_ge(y_taken, j - 2 + AHEAD)
                    dst = bank[7 - par]
                    for k in range(FT):
                        c0 = 3 * W12 + 2 * C * k
                        nc.tensor.matmul(dst[:, 0:2 * C], HH[:, 1 - par, k], w(0, P, c0, c0 + 2 * C), start=(k == 0), stop=False)
                        mm = nc.tensor.matmul(dst[:, 0:C], HL[:, 1 - par, k], w(0, P, c0, c0 + C), start=False, stop=(k == FT - 1))
                    mm.then_inc(y_ready, 1)
                return w_mid

            ffn_step(-1, 1, False, False, True)
            pe.wait_ge(wall_lo, EXPERTS)
            pe.wait_ge(wall_q, EXPERTS)
            ffn_step(0, 0, False, True, True)
            ffn_step(1, 1, True, True, True)
            with pe.Fori(0, SLOTS // 4) as i:
                w = None
                for u in range(4):
                    w = ffn_step(4 * i + (2 + u), u % 2, True, True, True, w)
            ffn_step(SLOTS - 1, 0, True, True, False)
            ffn_step(SLOTS, 1, True, False, False)


def lay_out(x, conv_w, conv_b, wq, wk, wv, Wg, bg, W1, W2, W3):
    import numpy as np

    f = np.float32

    def a_bb(m):
        return np.stack([m[:CA], np.concatenate([m[CA:], m[CA:]])], 1)

    def cols_a_bb(m):
        return np.concatenate([m[:, :CA], m[:, CA:], m[:, CA:]], 1)

    xt = x.reshape(IMAGES, C, PIX)
    x_cm = np.stack([xt[:, :CA], np.concatenate([xt[:, CA:], xt[:, CA:]], 1)], 2).reshape(IMAGES, P, 2 * PIX)
    x_tm = xt.transpose(0, 2, 1).reshape(TILES, P, C).transpose(1, 0, 2)

    group = np.arange(C) // (C // GROUPS)
    gm = (group[:, None] == group[None, :]).astype(f) / (2 * C // GROUPS)
    shift = (np.arange(480)[None, :] == np.arange(P)[:, None] + SHIFT0).astype(f)
    offs = [(i, i) for i in range(KERNEL)] + [(i, REACH) for i in range(KERNEL)]
    offs += [(i, KERNEL - 1 - i) for i in range(KERNEL)] + [(REACH, i) for i in range(KERNEL)]
    centers = [n for n, o in enumerate(offs) if o == (REACH, REACH)]
    rows4 = np.stack([conv_b] + [conv_w[:, C + n] for n in centers[1:]])
    s1 = [a_bb(cols_a_bb(gm)), a_bb(conv_w[:, :C].T), np.broadcast_to(rows4, (P, 4, C)),
          a_bb(cols_a_bb(wq.T)), a_bb(cols_a_bb(wk.T)), a_bb(wv), shift]
    small1 = np.concatenate([a.reshape(P, -1) for a in s1], 1)
    assert small1.shape[1] == S1N

    band = np.zeros((P, PAIR, C), f)
    for n, (r, cx) in enumerate(offs):
        if n in centers[1:]:
            continue
        for p in range(PAIR):
            q = p % SIDE + cx - REACH
            if 0 <= q < SIDE:
                band[(p // SIDE + r) * SIDE + q, p] = conv_w[:, C + n]
    band = band.reshape(P, PAIR * C)

    k = np.arange(P)
    causal = np.where(k[None, :] <= k[:, None], 0.0, NEG).astype(f)
    mask = np.concatenate([causal, np.zeros((P, P), f), causal], 1)
    desc = np.broadcast_to(np.arange(EXPERTS, 0, -1).astype(f), (P, 2, EXPERTS))
    base = np.broadcast_to((np.arange(EXPERTS) * REGION + PAD).astype(f), (P, EXPERTS))
    slot = np.broadcast_to(np.arange(SLOTS + 1).astype(f), (P, SLOTS + 1))
    s2 = [np.eye(P, dtype=f), mask, a_bb(Wg.T), np.broadcast_to(bg, (P, 2, EXPERTS)), desc, base, slot,
          (k[:, None] < k[None, :]).astype(f), np.ones((P, P), f)]
    small2 = np.concatenate([a.reshape(P, -1) for a in s2], 1)
    assert small2.shape[1] == S2N

    w12 = np.zeros((EXPERTS, C, 2, FE), f)
    w12[:, :, 0, :F] = W1.transpose(0, 2, 1)
    w12[:, :, 1, :F] = W2.transpose(0, 2, 1)
    w12 = w12.reshape(EXPERTS, C, W12)
    w3 = np.zeros((EXPERTS, FT * P, C), f)
    w3[:, :F] = W3.transpose(0, 2, 1)
    w3 = w3.reshape(EXPERTS, FT, P, C).transpose(0, 2, 1, 3).reshape(EXPERTS, P, W3C)
    w_all = np.concatenate([w12[:, :CA], np.concatenate([w12[:, CA:], w12[:, CA:]], 1), w3], 2)
    return [("x_cm", x_cm), ("x_tm", x_tm), ("small1", small1), ("small2", small2), ("band", band), ("w_all", w_all)]


def kernel(x, L0_conv_conv_w, L0_conv_conv_b, L1_attn_wq, L1_attn_wk, L1_attn_wv, L1_ffn_Wg, L1_ffn_bg, L1_ffn_W1, L1_ffn_W2, L1_ffn_W3):
    import numpy as np
    import concourse.bacc as bacc
    from concourse.bass_utils import run_bass_kernel_spmd as run

    ins = lay_out(*(np.asarray(a) for a in (x, L0_conv_conv_w, L0_conv_conv_b, L1_attn_wq, L1_attn_wk, L1_attn_wv,
                                            L1_ffn_Wg, L1_ffn_bg, L1_ffn_W1, L1_ffn_W2, L1_ffn_W3)))
    nc = bacc.Bacc("TRN2", target_bir_lowering=False, num_devices=1)
    arrays, args = {}, []
    for name, a in ins:
        arrays["in_" + name] = np.ascontiguousarray(a)
        args.append(nc.dram_tensor("in_" + name, a.shape, mybir.dt.from_np(a.dtype), kind="ExternalInput").ap())
    out = nc.dram_tensor("out_rows", (TILES * P, C), F32, kind="ExternalOutput").ap()
    build(nc, *args, out)
    res = run(nc, [arrays], core_ids=[0])
    t = res.results[0]["out_rows"]
    return np.ascontiguousarray(t.reshape(IMAGES, PIX, C).transpose(0, 2, 1).reshape(IMAGES, C, SIDE, SIDE))
```
